# Optimizing a Trainium2 kernel written in Bass

```python
import numpy as np
import jax
import jax.numpy as jnp

def _softmax(x, axis=-1):
    return jax.nn.softmax(x, axis=axis)

def _gelu(x):
    return jax.nn.gelu(x, approximate=True)

def _silu(x):
    return jax.nn.silu(x)

def _sigmoid(x):
    return jax.nn.sigmoid(x)

def _layernorm(x, axis=-1, eps=1e-05):
    m = jnp.mean(x, axis=axis, keepdims=True)
    v = jnp.var(x, axis=axis, keepdims=True)
    return (x - m) / jnp.sqrt(v + eps)

def _scatter_add(tgt, idx, src, axis=0):
    return tgt.at[idx].add(src)

def _segment_sum(src, seg, n):
    return jax.ops.segment_sum(src, seg, n)
kernel_name = 'mk_gnn_resnorm_d4_gnn_r32_1ccc1c'

def setup_inputs(seed: int=0):
    np.random.seed(seed)
    _w = jnp.asarray

    def _rec_inputs():
        import jax
        import jax.numpy as jnp
        _gk = jax.random.key(seed)
        x = -0.0005121 + 1.001 * jax.random.normal(jax.random.fold_in(_gk, 1), (3125, 64), jnp.float32)
        src = jax.random.randint(jax.random.fold_in(_gk, 2), (100000,), 0, 3125, jnp.int32)
        dst = jax.random.randint(jax.random.fold_in(_gk, 3), (100000,), 0, 3125, jnp.int32)
        _o = jnp.argsort(dst, stable=True)
        src = src[_o]
        dst = dst[_o]
        edge_attr_2 = -0.000414295 + 0.999828 * jax.random.normal(jax.random.fold_in(_gk, 12), (100000, 2), jnp.float32)
        edge_attr_64 = -8.16379e-05 + 0.999858 * jax.random.normal(jax.random.fold_in(_gk, 13), (100000, 64), jnp.float32)
        return (x, src, dst, edge_attr_2, edge_attr_64)
    x, src, dst, edge_attr_2, edge_attr_64 = _rec_inputs()

    def _L0_gnn_setup():
        import jax, jax.numpy as jnp
        import numpy as np
        N = 50000
        EG = 50000
        IN = 64
        OUT = 64
        H = 4
        D = OUT // H
        key = jax.random.key(seed)
        ks = jax.random.split(key, 12)
        s = 1.0 / np.sqrt(IN)
        return {'x': jax.random.normal(ks[0], (N, IN), jnp.float32), 'edge_attr': jax.random.normal(ks[1], (EG, IN), jnp.float32), 'edge_index': jax.random.randint(ks[2], (2, EG), 0, N, jnp.int32), 'Wq': jax.random.uniform(ks[3], (OUT, IN), jnp.float32, -s, s), 'bq': jax.random.uniform(ks[4], (OUT,), jnp.float32, -s, s), 'Wk': jax.random.uniform(ks[5], (OUT, IN), jnp.float32, -s, s), 'bk': jax.random.uniform(ks[6], (OUT,), jnp.float32, -s, s), 'We': jax.random.uniform(ks[7], (OUT, IN), jnp.float32, -s, s), 'be': jax.random.uniform(ks[8], (OUT,), jnp.float32, -s, s), 'Wv': jax.random.uniform(ks[9], (OUT, IN), jnp.float32, -s, s), 'bv': jax.random.uniform(ks[10], (OUT,), jnp.float32, -s, s)}
    _L0_gnn_all = _L0_gnn_setup()
    _L0_gnn_in = {k: v for k, v in _L0_gnn_all.items() if k in ('Wq', 'bq', 'Wk', 'bk', 'We', 'be', 'Wv', 'bv')}
    del _L0_gnn_all

    def _L1_gnn_setup():
        import jax, jax.numpy as jnp
        import numpy as np
        NUM_NODES = 3125
        EMBED_DIM = 64
        NUM_LAYERS = 3
        NUM_EDGES = 100000

        def _lightgcn_embedding(emb, edge_index):
            n = emb.shape[0]
            src, dst = (edge_index[0], edge_index[1])
            deg = jax.ops.segment_sum(jnp.ones(src.shape[0], dtype=emb.dtype), dst, num_segments=n)
            deg_inv_sqrt = jnp.where(deg > 0, jax.lax.rsqrt(jnp.maximum(deg, 1.0)), 0.0)
            w = deg_inv_sqrt[src] * deg_inv_sqrt[dst]
            x = emb
            out = emb
            for _ in range(NUM_LAYERS):
                x = jax.ops.segment_sum(w[:, None] * x[src], dst, num_segments=n)
                out = out + x
            return out / (NUM_LAYERS + 1)
        key = jax.random.key(seed)
        k_emb, k_edge = jax.random.split(key)
        emb = jax.random.normal(k_emb, (NUM_NODES, EMBED_DIM), dtype=jnp.float32) * 0.1
        edge_index = jax.random.randint(k_edge, (2, NUM_EDGES), 0, NUM_NODES, dtype=jnp.int64)
        return {'emb': emb, 'edge_index': edge_index}
    _L1_gnn_all = _L1_gnn_setup()
    _L1_gnn_in = {k: v for k, v in _L1_gnn_all.items() if k in ()}
    del _L1_gnn_all

    def _L2_gnn_setup():
        import jax, jax.numpy as jnp
        import numpy as np
        N_NODES = 3125
        N_EDGES = 100000
        DIM = 64
        key = jax.random.key(seed)
        k1, k2, k3, k4 = jax.random.split(key, 4)
        features = jax.random.normal(k1, (N_NODES, DIM), dtype=jnp.float32)
        attn_w = jax.random.normal(k2, (2 * DIM,), dtype=jnp.float32) / np.sqrt(2 * DIM)
        src = jax.random.randint(k3, (N_EDGES,), 0, N_NODES, dtype=jnp.int32)
        dst = jax.random.randint(k4, (N_EDGES,), 0, N_NODES, dtype=jnp.int32)
        return {'features': features, 'attn_w': attn_w, 'src': src, 'dst': dst}
    _L2_gnn_all = _L2_gnn_setup()
    _L2_gnn_in = {k: v for k, v in _L2_gnn_all.items() if k in ('attn_w',)}
    del _L2_gnn_all

    def _L3_gnn_setup():
        import jax, jax.numpy as jnp
        import numpy as np
        K = 3
        SLOPE = 0.01
        N_NODES = 50000
        N_EDGES = 25000
        D_IN = 64
        D_OUT = 64
        E_DIM = 2

        def _moments(z_e, Wm_list):
            moms = [z_e]
            mu = z_e.mean(axis=0, keepdims=True)
            for k in range(2, K + 1):
                mk = jnp.mean((z_e - mu) ** k, axis=0)
                mk = jnp.sign(mk) * jnp.abs(mk) ** (1.0 / k)
                moms.append(mk @ Wm_list[k - 2].T)
            return moms
        key = jax.random.key(seed)
        ks = jax.random.split(key, 10)
        s = 0.1
        return {'h': jax.random.normal(ks[0], (N_NODES, D_IN), dtype=jnp.float32), 'e': jax.random.normal(ks[1], (N_EDGES, E_DIM), dtype=jnp.float32), 'src': jax.random.randint(ks[2], (N_EDGES,), 0, N_NODES), 'dst': jax.random.randint(ks[3], (N_EDGES,), 0, N_NODES), 'W_fc': jax.random.normal(ks[4], (D_OUT, D_IN), dtype=jnp.float32) * s, 'W_attn': jax.random.normal(ks[5], (1, 2 * D_OUT * K + E_DIM), dtype=jnp.float32) * s, 'W_edge': jax.random.normal(ks[6], (E_DIM, E_DIM), dtype=jnp.float32) * s, 'W_e2n': jax.random.normal(ks[7], (D_OUT, E_DIM), dtype=jnp.float32) * s, 'W_m1': jax.random.normal(ks[8], (D_OUT, D_OUT), dtype=jnp.float32) * s, 'W_m2': jax.random.normal(ks[9], (D_OUT, D_OUT), dtype=jnp.float32) * s}
    _L3_gnn_all = _L3_gnn_setup()
    _L3_gnn_in = {k: v for k, v in _L3_gnn_all.items() if k in ('W_fc', 'W_attn', 'W_edge', 'W_e2n', 'W_m1', 'W_m2')}
    del _L3_gnn_all
    return {'x': x, 'src': src, 'dst': dst, 'edge_attr_2': edge_attr_2, 'edge_attr_64': edge_attr_64, 'L0_gnn_Wq': _L0_gnn_in['Wq'], 'L0_gnn_bq': _L0_gnn_in['bq'], 'L0_gnn_Wk': _L0_gnn_in['Wk'], 'L0_gnn_bk': _L0_gnn_in['bk'], 'L0_gnn_We': _L0_gnn_in['We'], 'L0_gnn_be': _L0_gnn_in['be'], 'L0_gnn_Wv': _L0_gnn_in['Wv'], 'L0_gnn_bv': _L0_gnn_in['bv'], 'L2_gnn_attn_w': _L2_gnn_in['attn_w'], 'L3_gnn_W_fc': _L3_gnn_in['W_fc'], 'L3_gnn_W_attn': _L3_gnn_in['W_attn'], 'L3_gnn_W_edge': _L3_gnn_in['W_edge'], 'L3_gnn_W_e2n': _L3_gnn_in['W_e2n'], 'L3_gnn_W_m1': _L3_gnn_in['W_m1'], 'L3_gnn_W_m2': _L3_gnn_in['W_m2']}

def reference(x, src, dst, edge_attr_2, edge_attr_64, L0_gnn_Wq, L0_gnn_bq, L0_gnn_Wk, L0_gnn_bk, L0_gnn_We, L0_gnn_be, L0_gnn_Wv, L0_gnn_bv, L2_gnn_attn_w, L3_gnn_W_fc, L3_gnn_W_attn, L3_gnn_W_edge, L3_gnn_W_e2n, L3_gnn_W_m1, L3_gnn_W_m2):
    import jax
    import jax.numpy as jnp

    def _L0_gnn_ref(x, edge_attr, edge_index, Wq, bq, Wk, bk, We, be, Wv, bv):
        import jax, jax.numpy as jnp
        import numpy as np
        N = 50000
        EG = 50000
        IN = 64
        OUT = 64
        H = 4
        D = OUT // H
        n = x.shape[0]
        Qh = (x @ Wq.T + bq).reshape(n, H, D)
        Kh = (x @ Wk.T + bk).reshape(n, H, D)
        Vh = (x @ Wv.T + bv).reshape(n, H, D)
        Ee = (edge_attr @ We.T + be).reshape(-1, H, D)
        src = edge_index[0]
        dst = edge_index[1]
        score = (Kh[src] * Qh[dst] * (1.0 / np.sqrt(D)) * Ee).sum(-1)
        score = jnp.exp(jnp.clip(score, -5.0, 5.0))
        msg = Vh[src] * score[..., None]
        wV = jax.ops.segment_sum(msg, dst, num_segments=n)
        return wV.reshape(n, H * D)

    def _L1_gnn_ref(emb, edge_index):
        import jax, jax.numpy as jnp
        import numpy as np
        NUM_NODES = 3125
        EMBED_DIM = 64
        NUM_LAYERS = 3
        NUM_EDGES = 100000

        def _lightgcn_embedding(emb, edge_index):
            n = emb.shape[0]
            src, dst = (edge_index[0], edge_index[1])
            deg = jax.ops.segment_sum(jnp.ones(src.shape[0], dtype=emb.dtype), dst, num_segments=n)
            deg_inv_sqrt = jnp.where(deg > 0, jax.lax.rsqrt(jnp.maximum(deg, 1.0)), 0.0)
            w = deg_inv_sqrt[src] * deg_inv_sqrt[dst]
            x = emb
            out = emb
            for _ in range(NUM_LAYERS):
                x = jax.ops.segment_sum(w[:, None] * x[src], dst, num_segments=n)
                out = out + x
            return out / (NUM_LAYERS + 1)
        return _lightgcn_embedding(emb, edge_index)

    def _L2_gnn_ref(features, attn_w, src, dst):
        import jax, jax.numpy as jnp
        import numpy as np
        N_NODES = 3125
        N_EDGES = 100000
        DIM = 64
        n = features.shape[0]
        d = features.shape[1]
        a_src, a_dst = (attn_w[:d], attn_w[d:])
        s_src = features @ a_src
        s_dst = features @ a_dst
        e = jax.nn.leaky_relu(s_src[src] + s_dst[dst], negative_slope=0.01)
        emax = jax.ops.segment_max(e, dst, num_segments=n)
        ee = jnp.exp(e - emax[dst])
        denom = jax.ops.segment_sum(ee, dst, num_segments=n)
        alpha = ee / denom[dst]
        h = jax.ops.segment_sum(alpha[:, None] * features[src], dst, num_segments=n)
        return jax.nn.elu(h)

    def _L3_gnn_ref(h, e, src, dst, W_fc, W_attn, W_edge, W_e2n, W_m1, W_m2):
        import jax, jax.numpy as jnp
        import numpy as np
        K = 3
        SLOPE = 0.01
        N_NODES = 50000
        N_EDGES = 25000
        D_IN = 64
        D_OUT = 64
        E_DIM = 2

        def _moments(z_e, Wm_list):
            moms = [z_e]
            mu = z_e.mean(axis=0, keepdims=True)
            for k in range(2, K + 1):
                mk = jnp.mean((z_e - mu) ** k, axis=0)
                mk = jnp.sign(mk) * jnp.abs(mk) ** (1.0 / k)
                moms.append(mk @ Wm_list[k - 2].T)
            return moms
        N = h.shape[0]
        D = W_fc.shape[0]
        z = h @ W_fc.T
        z_src = z[src]
        z_dst = z[dst]
        ex = e @ W_edge.T
        wm = [W_m1, W_m2]
        src_m = _moments(z_src, wm)
        dst_m = _moments(z_dst, wm)
        wa = W_attn[0]
        blk = [wa[i * D:(i + 1) * D] for i in range(2 * K)]
        w_e = wa[2 * K * D:]
        a = z_src @ blk[0] + z_dst @ blk[K] + ex @ w_e
        for k in range(1, K):
            a = a + src_m[k] @ blk[k] + dst_m[k] @ blk[K + k]
        att = jnp.where(a > 0, a, SLOPE * a)
        m = jax.ops.segment_max(att, dst, num_segments=N)
        expv = jnp.exp(att - m[dst])
        denom = jax.ops.segment_sum(expv, dst, num_segments=N)
        w = expv / denom[dst]
        ez = ex @ W_e2n.T
        msg = w[:, None] * (z_src + ez)
        return jax.ops.segment_sum(msg, dst, num_segments=N)
    edge_index = jnp.stack([src, dst])
    x = _layernorm(x + _L0_gnn_ref(x, edge_attr_64, edge_index, L0_gnn_Wq, L0_gnn_bq, L0_gnn_Wk, L0_gnn_bk, L0_gnn_We, L0_gnn_be, L0_gnn_Wv, L0_gnn_bv), axis=-1)
    x = _layernorm(x + _L1_gnn_ref(x, edge_index), axis=-1)
    x = _layernorm(x + _L2_gnn_ref(x, L2_gnn_attn_w, src, dst), axis=-1)
    x = _layernorm(x + _L3_gnn_ref(x, edge_attr_2, src, dst, L3_gnn_W_fc, L3_gnn_W_attn, L3_gnn_W_edge, L3_gnn_W_e2n, L3_gnn_W_m1, L3_gnn_W_m2), axis=-1)
    return x

_drawn_inputs = setup_inputs


def setup_inputs(seed=0):
    import zlib

    import numpy as np

    out = dict(_drawn_inputs(seed))
    spreads = {}
    factors = {'edge_attr_2': 8.0,
     'L0_gnn_bq': 5.915,
     'L0_gnn_bk': 5.269,
     'L0_gnn_be': 5.094,
     'L3_gnn_W_edge': 8.0,
     'L3_gnn_W_e2n': 8.0,
     'L3_gnn_W_m1': 8.0,
     'L3_gnn_W_m2': 55.533,
     'L3_gnn_W_attn': 5.152}
    for name, (base, spread) in spreads.items():
        noise = np.random.default_rng([zlib.crc32(name.encode()), seed]).standard_normal(out[name].shape)
        drawn = base * np.exp(spread * noise) if base else spread * noise
        out[name] = jnp.asarray(drawn.astype(out[name].dtype))
    for name, factor in factors.items():
        out[name] = (out[name] * factor).astype(out[name].dtype)
    return out
```

```python
import numpy as np
import concourse.bass as bass
from concourse import mybir
from contextlib import ExitStack

fp32, i32 = mybir.dt.float32, mybir.dt.int32
ALU, ACT, AX = mybir.AluOpType, mybir.ActivationFunctionType, mybir.AxisListType

P = 128
N, D, E = 3125, 64, 100000
H, DH = 4, 16
NT = -(-N // P)
NP = NT * P
NL = N - (NT - 1) * P
C = 8
ST = P * C
G = -(-E // ST)
PL = (E - (G - 1) * ST) // C
W = 64
NS = 2
IT = G // NS
NONE = 1.0e6
FAR = -1.0e30
LOW = -1.0e20
EPS = 1e-5
RT = 7
MT = 4
assert G % NS == 0 and (E - (G - 1) * ST) % C == 0


def build(nc, x, src, dst, edge_attr_2, edge_attr_64, Wq, bq, Wk, bk, We, be, Wv, bv,
          attn_w, W_fc, W_attn, W_edge, W_e2n, W_m1, W_m2, out):
    ctx = ExitStack()
    with ctx:
        def sb(name, shape, dt=fp32):
            return ctx.enter_context(nc.sbuf_tensor(name, shape, dt))

        def sem(name):
            return ctx.enter_context(nc.semaphore(name))

        def dram(name, shape):
            return nc.dram_tensor(name, shape, fp32, kind="Internal").ap()

        def bc(ap, axis, n):
            ap = ap.unsqueeze(axis)
            shape = list(ap.shape)
            shape[axis] = n
            return ap.to_broadcast(shape)

        kv_tab = dram("kv_tab", [NP, 2 * D])
        q_tab = dram("q_tab", [NP + W, D])
        hop_tab = [dram(f"hop_tab{i}", [NP, D]) for i in range(3)]
        att_tab = [dram(f"att_tab{i}", [NP, D + 2]) for i in range(2)]

        ident = sb("ident", [P, P])
        ones = sb("ones", [P, P])
        iota_i = sb("iota_i", [P, P], i32)
        iota = sb("iota", [P, P])
        src_i = sb("src_i", [P, G, C], i32)
        dst_i = sb("dst_i", [P, G, C], i32)
        src_lo = sb("src_lo", [P, G, C])
        src_hi = sb("src_hi", [P, G, C])
        scr_i = sb("scr_i", [P, G, C], i32)
        dst_rel0 = sb("dst_rel0", [P, G, C])
        dst_rel = sb("dst_rel", [P, G, C])
        lowest = sb("lowest", [P, G])
        lowest_col = sb("lowest_col", [G, 1])
        lowest_diag = sb("lowest_diag", [G, G])
        base0 = sb("base0", [1, G])
        base = sb("base", [1, G])
        base_i = sb("base_i", [1, G], i32)
        span = sb("span", [P, 2])
        span1 = sb("span1", [P, 1])
        sweeps_f = sb("sweeps_f", [1, 4])
        sweeps_i = sb("sweeps_i", [1, 2], i32)
        ea2 = sb("ea2", [P, G, C, 2])
        xrow = sb("xrow", [P, NT, D])
        xT = sb("xT", [D + 1, NP])
        rows = sb("rows", [P, NT, D + 4])
        acc = sb("acc", [P, NP + W])
        tmp = sb("tmp", [P, NT, D])
        stat = sb("stat", [P, 4, NT])
        dis = sb("dis", [P, NT])
        in_deg = sb("in_deg", [P, NT])
        out_deg = sb("out_deg", [P, NT])
        total = sb("total", [P, NT, D])
        tab = sb("tab", [P, NT, 2 * D])
        qt = sb("qt", [P, NT, D])
        wrow = sb("wrow", [D, 5, D])
        webd_row = sb("webd_row", [P, P])
        webd = sb("webd", [P, P])
        wcat = sb("wcat", [D + 1, 3 * D])
        be_row = sb("be_row", [1, C, D])
        kv = sb("kv", [P, NS, C, 2 * D])
        idx = sb("idx", [P, NS, C], i32)
        ea = sb("ea", [P, NS, C * D])
        qwin = sb("qwin", [W, NS, D])
        eaT = sb("eaT", [P, C * D])
        hot = sb("hot", [P, C, W])
        hotT = sb("hotT", [W, C * P])
        prod = sb("prod", [P, C * D])
        score = sb("score", [P, C * H])
        expo = sb("expo", [P, C * H])
        msg = sb("msg", [P, C, D + 1])
        lo_hot = sb("lo_hot", [P, C, P], mybir.dt.bfloat16)
        hi_hot = sb("hi_hot", [P, C, NT], mybir.dt.bfloat16)
        zeros_b = sb("zeros_b", [P, P], mybir.dt.bfloat16)
        ad_row = sb("ad_row", [P, NP + W])
        top = sb("top", [P, NP + W])
        edge_c = sb("edge_c", [P, G, C])
        edge_t = sb("edge_t", [P, G, C])
        g_edge = sb("g_edge", [P, NS, C, D + 4])
        u_edge = sb("u_edge", [P, C])
        logit = sb("logit", [P, C, W])
        logit2 = sb("logit2", [P, C, W])
        prob = sb("prob", [P, C, W])
        far = sb("far", [P, C, W])
        pmax = sb("pmax", [P, W])
        nmax = sb("nmax", [W, 1])
        ndiag = sb("ndiag", [W, W])
        newtop = sb("newtop", [P, W])
        drop = sb("drop", [P, W])
        decay = sb("decay", [P, W])
        attc = sb("attc", [D, 2])
        attrep = sb("attrep", [D, P])
        blk = sb("blk", [D, 6])
        w_e = sb("w_e", [2, 1])
        w_e_rep = sb("w_e_rep", [2, P])
        wedge = sb("wedge", [2, 2])
        we2n = sb("we2n", [D, 2])
        wm = sb("wm", [D, 2, D])
        wfcT = sb("wfcT", [D, D + 1])
        small = sb("small", [P, 32])
        m_row = sb("m_row", [1, 8, D])
        wmv = sb("wmv", [1, 4, D])
        wedge_rep = sb("wedge_rep", [2, 2, P])
        edge_w = sb("edge_w", [P, 2])
        e2n_rep = sb("e2n_rep", [P, 2, D])
        konst = sb("konst", [1, 1])
        mean_z = sb("mean_z", [P, D])
        e2nT = sb("e2nT", [2, D])

        bank = [ctx.enter_context(nc.psum_tensor(f"bank{i}", [P, 512], fp32)) for i in range(8)]

        s_zero, s_graph, s_x, s_w = sem("zeroed"), sem("graph_loaded"), sem("x_loaded"), sem("w_loaded")
        s_const, s_tail = sem("const"), sem("tail_loaded")
        s_wt, s_wts, s_base, s_basec, s_bdiag, s_brep = (
            sem("w_turned"), sem("w_copied"), sem("low_turned"), sem("low_ready"), sem("diag_ready"), sem("base_spread"))
        s_sp, s_spt = sem("span_ready"), sem("span_turned")

        with nc.Block() as block:
            @block.gpsimd
            def _(pool):
                nc.gpsimd.memset(ident[:, :], 0.0).then_inc(s_const, 1)
                nc.gpsimd.iota(iota_i[:, :], pattern=[[1, P]], base=0, channel_multiplier=0).then_inc(s_const, 1)
                pool.wait_ge(s_const, 2)
                nc.gpsimd.affine_select(out=ident[:, :], in_=ident[:, :], compare_op=ALU.not_equal, fill=1.0,
                                        base=0, pattern=[[-1, P]], channel_multiplier=1).then_inc(s_const, 1)

            @block.sync
            def _(sp):
                full = (G - 1) * ST
                sp.dma_start(wrow[:, 0, :], Wk).then_inc(s_w, 16)
                sp.dma_start(wrow[:, 1, :], Wv).then_inc(s_w, 16)
                sp.dma_start(wrow[:, 2, :], Wq).then_inc(s_w, 16)
                sp.dma_start(wrow[:, 3, :], W_fc).then_inc(s_w, 16)
                for i, b in enumerate((bk, bv, bq)):
                    sp.dma_start(wcat[D:D + 1, i * D:(i + 1) * D], b.rearrange("(a n) -> a n", a=1)).then_inc(s_w, 16)
                for c in range(C):
                    sp.dma_start(be_row[:, c, :], be.rearrange("(a n) -> a n", a=1)).then_inc(s_w, 16)
                sp.dma_start(attc[:, :], attn_w.rearrange("(k p) -> p k", p=D), allow_slow_non_contiguous=True).then_inc(s_w, 16)
                sp.dma_start(blk[:, :], W_attn[0, 0:6 * D].rearrange("(k p) -> p k", p=D), allow_slow_non_contiguous=True).then_inc(s_w, 16)
                sp.dma_start(w_e[:, :], W_attn[0, 6 * D:6 * D + 2].rearrange("(p a) -> p a", a=1), allow_slow_non_contiguous=True).then_inc(s_w, 16)
                sp.dma_start(wedge[:, :], W_edge).then_inc(s_w, 16)
                sp.dma_start(we2n[:, :], W_e2n).then_inc(s_w, 16)
                sp.dma_start(wm[:, 0, :], W_m1).then_inc(s_w, 16)
                sp.dma_start(wm[:, 1, :], W_m2).then_inc(s_w, 16)
                sp.dma_start(xrow[:, 0:NT - 1, :], x[0:(NT - 1) * P, :].rearrange("(t p) f -> p t f", p=P)).then_inc(s_x, 16)
                sp.dma_start(dst_i[:, 0:G - 1, :], dst[0:full].rearrange("(g p c) -> p g c", p=P, c=C)).then_inc(s_graph, 16)
                sp.dma_start(src_i[:, 0:G - 1, :], src[0:full].rearrange("(g p c) -> p g c", p=P, c=C)).then_inc(s_graph, 16)
                sp.dma_start(ea2[:, 0:G - 1, :, :], edge_attr_2[0:full, :].rearrange("(g p c) k -> p g c k", p=P, c=C)).then_inc(s_graph, 16)
                sp.wait_ge(s_zero, 1)
                sp.dma_start(webd_row[0:D, 0:D], We).then_inc(s_tail, 16)
                sp.dma_start(webd_row[D:P, D:P], We).then_inc(s_tail, 16)
                sp.dma_start(xrow[0:NL, NT - 1, :], x[(NT - 1) * P:N, :]).then_inc(s_tail, 16)
                sp.dma_start(dst_i[0:PL, G - 1, :], dst[full:E].rearrange("(p c) -> p c", c=C)).then_inc(s_tail, 16)
                sp.dma_start(src_i[0:PL, G - 1, :], src[full:E].rearrange("(p c) -> p c", c=C)).then_inc(s_tail, 16)
                sp.dma_start(ea2[0:PL, G - 1, :, :], edge_attr_2[full:E, :].rearrange("(p c) k -> p c k", c=C)).then_inc(s_tail, 16)

            @block.vector
            def _(dve):
                nc.vector.memset(dst_i[:, G - 1, :], int(NONE))
                nc.vector.memset(src_i[:, G - 1, :], int(NONE))
                nc.vector.memset(ea2[:, G - 1, :, :], 0.0)
                nc.vector.memset(webd_row[:, :], 0.0)
                nc.vector.memset(xrow[:, NT - 1, :], 0.0)
                nc.vector.memset(ones[:, :], 1.0)
                nc.vector.memset(zeros_b[:, :], 0.0)
                nc.vector.memset(msg[:, :, D:D + 1], 1.0)
                nc.vector.memset(xT[D:D + 1, :], 1.0)
                nc.vector.memset(span[:, :], 0.0)
                dve.drain().then_inc(s_zero, 1)
                dve.wait_ge(s_const, 3)
                nc.vector.tensor_copy(iota[:, :], iota_i[:, :])
                dve.wait_ge(s_graph, 48)
                dve.wait_ge(s_tail, 96)
                nc.vector.tensor_scalar(scr_i[:, :, :], src_i[:, :, :], P - 1, None, ALU.bitwise_and)
                dve.drain()
                nc.vector.tensor_copy(src_lo[:, :, :], scr_i[:, :, :])
                dve.drain()
                nc.vector.tensor_scalar(scr_i[:, :, :], src_i[:, :, :], 7, None, ALU.arith_shift_right)
                dve.drain()
                nc.vector.tensor_copy(src_hi[:, :, :], scr_i[:, :, :])
                nc.vector.tensor_copy(dst_rel0[:, :, :], dst_i[:, :, :])
                dve.drain()
                nc.vector.tensor_reduce(lowest[:, :], dst_rel0[:, :, :], AX.X, ALU.min)
                dve.drain().then_inc(s_base, 1)
                dve.wait_ge(s_basec, 1)
                nc.vector.tensor_reduce(lowest_col[:, :], bank[0][0:G, 0:P], AX.X, ALU.min)
                dve.drain()
                nc.vector.tensor_scalar(lowest_diag[:, :], ident[0:G, 0:G], lowest_col[:, 0:1], None, ALU.mult)
                dve.drain().then_inc(s_bdiag, 1)
                dve.wait_ge(s_brep, 1)
                nc.vector.tensor_copy(base0[:, :], bank[1][0:1, 0:G])
                nc.vector.tensor_tensor(dst_rel0[:, :, :], dst_rel0[:, :, :], bc(bank[1][:, 0:G], 2, C), ALU.subtract)
                dve.drain()
                nc.vector.tensor_reduce(span[:, 0:1], dst_rel0[:, 0:G - 1, :], AX.XY, ALU.max)
                nc.vector.tensor_reduce(span[0:PL, 1:2], dst_rel0[0:PL, G - 1, :], AX.X, ALU.max)
                dve.drain()
                nc.vector.tensor_reduce(span1[:, :], span[:, :], AX.X, ALU.max)
                dve.drain().then_inc(s_sp, 1)
                dve.wait_ge(s_spt, 1)
                nc.vector.tensor_reduce(sweeps_f[:, 0:1], bank[2][0:1, 0:P], AX.X, ALU.max)
                dve.drain()
                nc.vector.tensor_copy(sweeps_i[:, 1:2], sweeps_f[:, 0:1])
                dve.drain()
                nc.vector.tensor_scalar(sweeps_i[:, 0:1], sweeps_i[:, 1:2], 6, None, ALU.arith_shift_right)
                dve.drain()
                nc.vector.tensor_copy(sweeps_f[:, 1:2], sweeps_i[:, 0:1])
                dve.drain()
                nc.vector.tensor_scalar(sweeps_f[:, 2:3], sweeps_f[:, 1:2], 1.0, None, ALU.add)
                dve.drain()
                nc.vector.tensor_copy(sweeps_i[:, 0:1], sweeps_f[:, 2:3])
                nc.vector.reciprocal(sweeps_f[:, 3:4], sweeps_f[:, 2:3])

            @block.tensor
            def _(pe):
                pe.wait_ge(s_const, 3)
                pe.wait_ge(s_w, 16 * 22)
                pe.wait_ge(s_tail, 96)
                for i in range(4):
                    nc.tensor.transpose(bank[3][0:D, i * D:(i + 1) * D], wrow[:, i, :], ident[0:D, 0:D])
                nc.tensor.transpose(bank[4][:, 0:P], webd_row[:, :], ident[:, :]).then_inc(s_wt, 1)
                pe.wait_ge(s_base, 1)
                nc.tensor.transpose(bank[0][0:G, 0:P], lowest[:, :], ident[:, :]).then_inc(s_basec, 1)
                pe.wait_ge(s_bdiag, 1)
                nc.tensor.matmul(bank[1][:, 0:G], ones[0:G, :], lowest_diag[:, :], start=True, stop=True).then_inc(s_brep, 1)
                pe.wait_ge(s_sp, 1)
                nc.tensor.transpose(bank[2][0:1, 0:P], span1[:, :], ident[:, :]).then_inc(s_spt, 1)

            @block.scalar
            def _(act):
                act.wait_ge(s_wt, 1)
                nc.scalar.activation(wcat[0:D, :], bank[3][0:D, 0:3 * D], ACT.Copy)
                nc.scalar.activation(wfcT[:, 0:D], bank[3][0:D, 3 * D:4 * D], ACT.Copy)
                nc.scalar.activation(webd[:, :], bank[4][:, 0:P], ACT.Copy)

        def project(tag, cols, K, rhs, evacuate, row_rep=None):
            turned, copied, done, taken = (sem(f"{tag}_turned"), sem(f"{tag}_copied"), sem(f"{tag}_done"), sem(f"{tag}_taken"))
            arow, arow_out = sem(f"{tag}_arow"), sem(f"{tag}_arow_out")
            groups = [range(t, min(t + MT, NT)) for t in range(0, NT, MT)]
            per = max(1, min(2, 512 // cols))
            mms = [range(t, min(t + per, NT)) for t in range(0, NT, per)]
            chunks = [(c, min(c + 512, NP)) for c in range(0, NP, 512)]
            with nc.Block() as block:
                @block.tensor
                def _(pe):
                    for k, ts in enumerate(groups):
                        if k >= 2:
                            pe.wait_ge(copied, k - 1)
                        for j, t in enumerate(ts):
                            last = nc.tensor.transpose(bank[k % 2][0:D, j * P:(j + 1) * P], xrow[:, t, :], ident[:, :])
                        last.then_inc(turned, 1)
                    pe.wait_ge(copied, len(groups))
                    for k, ts in enumerate(mms):
                        if k >= 2:
                            pe.wait_ge(taken, k - 1)
                        for j, t in enumerate(ts):
                            last = nc.tensor.matmul(bank[2 + k % 2][:, j * cols:(j + 1) * cols], xT[0:K, t * P:(t + 1) * P],
                                                    rhs, start=True, stop=True)
                        last.then_inc(done, 1)
                    if row_rep is not None:
                        for k, (a, b) in enumerate(chunks):
                            if k >= 2:
                                pe.wait_ge(arow_out, k - 1)
                            nc.tensor.matmul(bank[4 + k % 2][:, 0:b - a], row_rep, xT[0:D, a:b], start=True, stop=True).then_inc(arow, 1)

                @block.scalar
                def _(act):
                    for k, ts in enumerate(groups):
                        act.wait_ge(turned, k + 1)
                        nc.scalar.activation(xT[0:D, ts[0] * P:(ts[-1] + 1) * P], bank[k % 2][0:D, 0:len(ts) * P], ACT.Copy).then_inc(copied, 1)
                    if row_rep is not None:
                        for k, (a, b) in enumerate(chunks):
                            act.wait_ge(arow, k + 1)
                            nc.scalar.activation(ad_row[:, a:b], bank[4 + k % 2][:, 0:b - a], ACT.Copy).then_inc(arow_out, 1)

                @block.vector
                def _(dve):
                    for k, ts in enumerate(mms):
                        dve.wait_ge(done, k + 1)
                        ps = bank[2 + k % 2][:, 0:len(ts) * cols].rearrange("p (t n) -> p t n", n=cols)
                        evacuate(ts[0], ts[-1] + 1, ps).then_inc(taken, 1)
                    if row_rep is not None:
                        nc.vector.memset(ad_row[:, NP:NP + W], 0.0)

        def store_table(tag, pairs):
            stored = sem(f"{tag}_stored")
            with nc.Block() as block:
                @block.sync
                def _(sp):
                    for t, view in pairs:
                        sp.dma_start(t, view).then_inc(stored, 16)
                    sp.wait_ge(stored, 16 * len(pairs))

        def take_l0(a, b, ps):
            nc.vector.tensor_scalar(tab[:, a:b, 0:D], ps[:, :, 0:D], DH ** -0.5, None, ALU.mult)
            nc.vector.tensor_copy(tab[:, a:b, D:2 * D], ps[:, :, D:2 * D])
            return nc.vector.tensor_copy(qt[:, a:b, :], ps[:, :, 2 * D:3 * D])

        project("l0", 3 * D, D + 1, wcat[:, :], take_l0)
        with nc.Block() as block:
            @block.vector
            def _(dve):
                nc.vector.memset(tmp[0:W, 0, :], 0.0)
        by_tile = "(t p) f -> p t f"
        store_table("l0", [(kv_tab.rearrange(by_tile, p=P), tab[:, :, :]),
                           (q_tab[0:NP, :].rearrange(by_tile, p=P), qt[:, :, :]),
                           (q_tab[NP:NP + W, :], tmp[0:W, 0, :])])

        def start_sweep(dve, ready):
            nc.vector.tensor_scalar(dst_rel[:, :, :], dst_rel[:, :, :], float(-W), None, ALU.add)
            nc.vector.tensor_scalar(base[:, :], base[:, :], float(W), float(NP), ALU.add, ALU.min)
            dve.drain()
            nc.vector.tensor_copy(base_i[:, :], base[:, :])
            dve.drain().then_inc(ready, 1)

        def reset_windows(dve):
            nc.vector.tensor_scalar(dst_rel[:, :, :], dst_rel0[:, :, :], float(W), None, ALU.add)
            nc.vector.tensor_scalar(base[:, :], base0[:, :], float(-W), None, ALU.add)
            nc.vector.memset(acc[:, :], 0.0)
            dve.drain()

        def sweeps(eng):
            return eng.value_load(sweeps_i[0:1, 0:1], min_val=1, max_val=NP // W)

        def spans(eng, g):
            return eng.value_load(base_i[0:1, bass.ds(g, 1)], min_val=0, max_val=NP)

        passed = sem("passed")

        def pass_on(eng):
            eng.sem_inc(passed, 1)

        ea_main = edge_attr_64[0:(G - 1) * ST, :].rearrange("(g p c) f -> g p (c f)", p=P, c=C)
        ea_last = edge_attr_64[(G - 1) * ST:E, :].rearrange("(p c) f -> p (c f)", c=C)

        src_main = src[0:(G - 1) * ST].rearrange("(g p c) -> g p c", p=P, c=C)
        src_last = src[(G - 1) * ST:E].rearrange("(p c) -> p c", c=C)

        def load_idx(sp, g, s, last, into):
            if last:
                sp.dma_start(idx[0:PL, s, :], src_last).then_inc(into, 16)
            else:
                sp.dma_start(idx[:, s, :], src_main[bass.ds(g, 1), :, :].rearrange("g p c -> (g p) c")).then_inc(into, 16)

        begun = sem("a_begun")
        slot_free, idx_in = sem("a_slot_free"), [sem(f"a_idx{s}") for s in range(NS)]
        ea_in, kv_in = [sem(f"a_ea{s}") for s in range(NS)], [sem(f"a_kv{s}") for s in range(NS)]
        hot_ok, ea_t, ea_ts, hot_t, hot_ts = sem("a_hot"), sem("a_eaT"), sem("a_eaTs"), sem("a_hotT"), sem("a_hotTs")
        ee_ok, qd_ok, sc_ok, ex_ok, msg_ok, sum_ok = (sem("a_ee"), sem("a_qd"), sem("a_score"), sem("a_exp"), sem("a_msg"), sem("a_sum"))
        lohi_ok, lohi_used, deg0 = sem("a_lohi"), sem("a_lohi_used"), sem("a_deg0")
        with nc.Block() as block:
            @block.sync
            def _(sp):
                nj = sweeps(sp)
                with sp.Fori(0, nj) as j:
                    sp.wait_ge(begun, j + 1)
                    pass_on(sp)

                    def load(g, n, s, last):
                        sp.wait_ge(slot_free, n)
                        pass_on(sp)
                        load_idx(sp, g, s, last, idx_in[s])
                        b = spans(sp, g)
                        sp.dma_start(qwin[:, s, :], q_tab[bass.ds(b, W), :]).then_inc(ea_in[s], 16)
                        if last:
                            sp.dma_start(ea[0:PL, s, :], ea_last).then_inc(ea_in[s], 16)
                        else:
                            sp.dma_start(ea[:, s, :], ea_main[bass.ds(g, 1), :, :].rearrange("g p n -> (g p) n")).then_inc(ea_in[s], 16)

                    with sp.Fori(0, IT - 1) as it:
                        for s in range(NS):
                            load(it * NS + s, j * G + it * NS + s + 1, s, False)
                    for s in range(NS):
                        g = G - NS + s
                        load(g, j * G + g + 1, s, g == G - 1)

            @block.gpsimd
            def _(pool):
                nj = sweeps(pool)
                with pool.Fori(0, nj) as j:
                    with pool.Fori(0, IT) as it:
                        for s in range(NS):
                            pool.wait_ge(idx_in[s], (j * IT + it + 1) * 16)
                            pass_on(pool)
                            for c in range(C):
                                nc.gpsimd.indirect_dma_start(
                                    kv[:, s, c, :], None, kv_tab, bass.IndirectOffsetOnAxis(ap=idx[:, s, c:c + 1], axis=0)
                                ).then_inc(kv_in[s], 16)

            @block.vector
            def _(dve):
                nj = sweeps(dve)
                reset_windows(dve)
                dve.sem_inc(slot_free, NS)
                with dve.Fori(0, nj) as j:
                    start_sweep(dve, begun)
                    with dve.Fori(0, IT) as it:
                        for s in range(NS):
                            g = it * NS + s
                            n = j * G + g + 1
                            m = j * IT + it + 1
                            nc.vector.tensor_tensor(hot[:, :, :], bc(dst_rel[:, bass.ds(g, 1), :].rearrange("p g c -> p (g c)"), 2, W),
                                                    bc(iota[:, 0:W], 1, C), ALU.is_equal).then_inc(hot_ok, 1)
                            nc.vector.tensor_tensor(lo_hot[:, :, :], bc(src_lo[:, bass.ds(g, 1), :].rearrange("p g c -> p (g c)"), 2, P),
                                                    bc(iota[:, :], 1, C), ALU.is_equal)
                            nc.vector.tensor_tensor(hi_hot[:, :, :], bc(src_hi[:, bass.ds(g, 1), :].rearrange("p g c -> p (g c)"), 2, NT),
                                                    bc(iota[:, 0:NT], 1, C), ALU.is_equal).then_inc(lohi_ok, 1)
                            dve.wait_ge(kv_in[s], m * (16 * C))
                            dve.wait_ge(ee_ok, n)
                            kvs = kv[:, s, :, :]
                            nc.vector.tensor_tensor(prod[:, :].rearrange("p (c f) -> p c f", c=C),
                                                    bank[3][:, :].rearrange("p (c f) -> p c f", c=C), kvs[:, :, 0:D], ALU.mult)
                            dve.drain()
                            dve.wait_ge(qd_ok, n)
                            nc.vector.tensor_tensor(prod[:, :], prod[:, :], bank[4][:, :], ALU.mult)
                            dve.drain()
                            nc.vector.tensor_reduce(score[:, :], prod[:, :].rearrange("p (a d) -> p a d", d=DH), AX.X, ALU.add)
                            dve.drain()
                            nc.vector.tensor_scalar(score[:, :], score[:, :], -5.0, 5.0, ALU.max, ALU.min).then_inc(sc_ok, 1)
                            dve.wait_ge(ex_ok, n)
                            nc.vector.tensor_tensor(msg[:, :, 0:D].rearrange("p c (h d) -> p c h d", h=H),
                                                    kvs[:, :, D:2 * D].rearrange("p c (h d) -> p c h d", h=H),
                                                    bc(expo[:, :].rearrange("p (c h) -> p c h", h=H), 3, DH), ALU.mult).then_inc(msg_ok, 1)
                            b = spans(dve, g)
                            dve.wait_ge(sum_ok, n)
                            nc.vector.tensor_tensor(acc[0:D + 1, bass.ds(b, W)], acc[0:D + 1, bass.ds(b, W)], bank[5][0:D + 1, 0:W], ALU.add).then_inc(slot_free, 1)
                            dve.drain()
                            dve.wait_ge(lohi_used, n)
                            pass_on(dve)

            @block.scalar
            def _(act):
                nj = sweeps(act)
                with act.Fori(0, nj) as j:
                    with act.Fori(0, IT) as it:
                        for s in range(NS):
                            n = j * G + it * NS + s + 1
                            act.wait_ge(ea_t, n)
                            nc.scalar.activation(eaT[:, :], bank[0][:, :], ACT.Copy).then_inc(ea_ts, 1)
                            act.wait_ge(hot_t, n)
                            nc.scalar.activation(hotT[:, 0:512], bank[1][0:W, :], ACT.Copy)
                            nc.scalar.activation(hotT[:, 512:1024], bank[2][0:W, :], ACT.Copy).then_inc(hot_ts, 1)
                            act.wait_ge(sc_ok, n)
                            nc.scalar.activation(expo[:, :], score[:, :], ACT.Exp).then_inc(ex_ok, 1)

            @block.tensor
            def _(pe):
                nj = sweeps(pe)
                nc.tensor.matmul(bank[6][:, 0:NT], zeros_b[:, :], zeros_b[:, 0:NT], start=True, stop=False, skip_group_check=True)
                with pe.Fori(0, nj) as j:
                    with pe.Fori(0, IT) as it:
                        for s in range(NS):
                            n = j * G + it * NS + s + 1
                            m = j * IT + it + 1
                            pe.wait_ge(ea_in[s], m * 32)
                            for q in range(4):
                                last = nc.tensor.transpose(bank[0][:, q * P:(q + 1) * P], ea[:, s, q * P:(q + 1) * P], ident[:, :])
                            last.then_inc(ea_t, 1)
                            pe.wait_ge(hot_ok, n)
                            pass_on(pe)
                            for c in range(C):
                                last = nc.tensor.transpose(bank[1 + c // 4][0:W, c % 4 * P:(c % 4 + 1) * P], hot[:, c, :], ident[:, :])
                            last.then_inc(hot_t, 1)
                            pe.wait_ge(lohi_ok, n)
                            for c in range(C):
                                last = nc.tensor.matmul(bank[6][:, 0:NT], lo_hot[:, c, :], hi_hot[:, c, :], start=False, stop=False, skip_group_check=True)
                            last.then_inc(lohi_used, 1)
                            pe.wait_ge(ea_ts, n)
                            for q in range(4):
                                nc.tensor.matmul(bank[3][:, q * P:(q + 1) * P], eaT[:, q * P:(q + 1) * P], webd[:, :],
                                                 start=q == 0, stop=False, skip_group_check=True)
                            last = nc.tensor.matmul(bank[3][:, :], ones[0:1, :], be_row[:, :, :].rearrange("a c f -> a (c f)"),
                                                    start=False, stop=True, skip_group_check=True)
                            last.then_inc(ee_ok, 1)
                            pe.wait_ge(hot_ts, n)
                            for c in range(C):
                                last = nc.tensor.matmul(bank[4][:, c * D:(c + 1) * D], hotT[:, c * P:(c + 1) * P], qwin[:, s, :], start=True, stop=True)
                            last.then_inc(qd_ok, 1)
                            pe.wait_ge(msg_ok, n)
                            for c in range(C):
                                last = nc.tensor.matmul(bank[5][0:D + 1, 0:W], msg[:, c, :], hot[:, c, :], start=c == 0, stop=c == C - 1)
                            last.then_inc(sum_ok, 1)
                nc.tensor.matmul(bank[6][:, 0:NT], zeros_b[:, :], zeros_b[:, 0:NT], start=False, stop=True, skip_group_check=True)

        def read_back(tag, M):
            turned = sem(f"{tag}_rows")
            groups = [range(t, min(t + RT, NT)) for t in range(0, NT, RT)]
            with nc.Block() as block:
                @block.tensor
                def _(pe):
                    for k, ts in enumerate(groups):
                        for i, t in enumerate(ts):
                            last = nc.tensor.transpose(bank[k][:, i * M:(i + 1) * M], acc[0:M, t * P:(t + 1) * P], ident[0:M, 0:M])
                        last.then_inc(turned, 1)

                @block.vector
                def _(dve):
                    for k, ts in enumerate(groups):
                        dve.wait_ge(turned, k + 1)
                        nc.vector.tensor_copy(rows[:, ts[0]:ts[-1] + 1, 0:M], bank[k][:, 0:len(ts) * M].rearrange("p (t m) -> p t m", m=M))

        def layernorm(tag, before, after, replicate=None):
            var_ok, std_ok, aux_ok = sem(f"{tag}_var"), sem(f"{tag}_std"), sem(f"{tag}_aux")
            aux_in = sem(f"{tag}_aux_in")
            with nc.Block() as block:
                @block.vector
                def _(dve):
                    before(dve, aux_in, aux_ok)
                    dve.drain()
                    nc.vector.tensor_reduce(stat[:, 0, :], xrow[:, :, :], AX.X, ALU.add)
                    dve.drain()
                    nc.vector.tensor_scalar(stat[:, 1, :], stat[:, 0, :], 1.0 / D, None, ALU.mult)
                    dve.drain()
                    nc.vector.tensor_tensor(tmp[:, :, :], xrow[:, :, :], bc(stat[:, 1, :], 2, D), ALU.subtract)
                    dve.drain()
                    nc.vector.tensor_tensor(xrow[:, :, :], tmp[:, :, :], tmp[:, :, :], ALU.mult)
                    dve.drain()
                    nc.vector.tensor_reduce(stat[:, 2, :], xrow[:, :, :], AX.X, ALU.add)
                    dve.drain()
                    nc.vector.tensor_scalar(stat[:, 3, :], stat[:, 2, :], 1.0 / D, EPS, ALU.mult, ALU.add)
                    dve.drain().then_inc(var_ok, 1)
                    dve.wait_ge(std_ok, 1)
                    nc.vector.reciprocal(stat[:, 1, :], stat[:, 0, :])
                    dve.drain()
                    nc.vector.tensor_tensor(xrow[:, :, :], tmp[:, :, :], bc(stat[:, 1, :], 2, D), ALU.mult)
                    dve.drain()
                    after(dve)

                @block.scalar
                def _(act):
                    if replicate is not None:
                        replicate[1](act, aux_in, aux_ok)
                    act.wait_ge(var_ok, 1)
                    nc.scalar.activation(stat[:, 0, :], stat[:, 3, :], ACT.Sqrt).then_inc(std_ok, 1)

                @block.tensor
                def _(pe):
                    if replicate is not None:
                        replicate[0](pe, aux_in, aux_ok)

        read_back("l0", D + 1)

        def l0_before(dve, aux_in, aux_ok):
            nc.vector.tensor_tensor(xrow[:, :, :], xrow[:, :, :], rows[:, :, 0:D], ALU.add)
            nc.vector.tensor_copy(in_deg[:, :], rows[:, :, D])
            nc.vector.tensor_copy(out_deg[:, :], bank[6][:, 0:NT])
            dve.drain()
            nc.vector.tensor_scalar(dis[:, :], in_deg[:, :], 1.0, None, ALU.max)
            dve.wait_ge(aux_ok, 1)
            nc.vector.tensor_scalar(out_deg[:, :], out_deg[:, :], bank[7][:, 0:1], None, ALU.mult)
            dve.drain().then_inc(aux_in, 1)
            dve.wait_ge(aux_ok, 2)
            nc.vector.reciprocal(dis[:, :], small[:, 0:NT])
            nc.vector.tensor_scalar(stat[:, 0, :], in_deg[:, :], 1.0, None, ALU.min)
            dve.drain()
            nc.vector.tensor_tensor(dis[:, :], dis[:, :], stat[:, 0, :], ALU.mult)

        def l0_after(dve):
            nc.vector.tensor_copy(total[:, :, :], xrow[:, :, :])
            nc.vector.tensor_tensor(qt[:, :, :], xrow[:, :, :], bc(dis[:, :], 2, D), ALU.mult)

        def spread_sweeps(pe, aux_in, aux_ok):
            nc.tensor.matmul(bank[7][:, 0:1], ones[0:1, :], sweeps_f[:, 3:4], start=True, stop=True).then_inc(aux_ok, 1)

        def root_degree(act, aux_in, aux_ok):
            act.wait_ge(aux_in, 1)
            nc.scalar.activation(small[:, 0:NT], dis[:, :], ACT.Sqrt).then_inc(aux_ok, 1)

        layernorm("l0", l0_before, l0_after, (spread_sweeps, root_degree))
        store_table("hop0", [(hop_tab[0].rearrange(by_tile, p=P), qt[:, :, :])])

        def sweep_pool(pool, table, width, into, begun, idx_in, rows_in):
            nj = sweeps(pool)
            with pool.Fori(0, nj) as j:
                with pool.Fori(0, IT) as it:
                    for s in range(NS):
                        pool.wait_ge(idx_in[s], (j * IT + it + 1) * 16)
                        pass_on(pool)
                        for c in range(C):
                            nc.gpsimd.indirect_dma_start(
                                into[:, s, c, 0:width], None, table, bass.IndirectOffsetOnAxis(ap=idx[:, s, c:c + 1], axis=0)
                            ).then_inc(rows_in[s], 16)

        def sweep_loads(sp, begun, slot_free, idx_in):
            nj = sweeps(sp)
            with sp.Fori(0, nj) as j:
                sp.wait_ge(begun, j + 1)
                pass_on(sp)
                with sp.Fori(0, IT - 1) as it:
                    for s in range(NS):
                        sp.wait_ge(slot_free, j * G + it * NS + s + 1)
                        load_idx(sp, it * NS + s, s, False, idx_in[s])
                for s in range(NS):
                    g = G - NS + s
                    sp.wait_ge(slot_free, j * G + g + 1)
                    load_idx(sp, g, s, g == G - 1, idx_in[s])

        def hop(k):
            begun, slot_free, hot_ok, sum_ok = sem(f"h{k}_begun"), sem(f"h{k}_free"), sem(f"h{k}_hot"), sem(f"h{k}_sum")
            idx_in, rows_in = [sem(f"h{k}_idx{s}") for s in range(NS)], [sem(f"h{k}_rows{s}") for s in range(NS)]
            with nc.Block() as block:
                @block.sync
                def _(sp):
                    sweep_loads(sp, begun, slot_free, idx_in)

                @block.gpsimd
                def _(pool):
                    sweep_pool(pool, hop_tab[k], D, g_edge, begun, idx_in, rows_in)

                @block.vector
                def _(dve):
                    nj = sweeps(dve)
                    reset_windows(dve)
                    dve.sem_inc(slot_free, NS)
                    with dve.Fori(0, nj) as j:
                        start_sweep(dve, begun)
                        with dve.Fori(0, IT) as it:
                            for s in range(NS):
                                g = it * NS + s
                                n = j * G + g + 1
                                nc.vector.tensor_tensor(hot[:, :, :], bc(dst_rel[:, bass.ds(g, 1), :].rearrange("p g c -> p (g c)"), 2, W),
                                                        bc(iota[:, 0:W], 1, C), ALU.is_equal).then_inc(hot_ok, 1)
                                b = spans(dve, g)
                                dve.wait_ge(sum_ok, n)
                                nc.vector.tensor_tensor(acc[0:D, bass.ds(b, W)], acc[0:D, bass.ds(b, W)], bank[5][0:D, 0:W], ALU.add).then_inc(slot_free, 1)
                                dve.drain()

                @block.tensor
                def _(pe):
                    nj = sweeps(pe)
                    with pe.Fori(0, nj) as j:
                        with pe.Fori(0, IT) as it:
                            for s in range(NS):
                                pe.wait_ge(hot_ok, j * G + it * NS + s + 1)
                                pe.wait_ge(rows_in[s], (j * IT + it + 1) * (16 * C))
                                for c in range(C):
                                    last = nc.tensor.matmul(bank[5][0:D, 0:W], g_edge[:, s, c, 0:D], hot[:, c, :], start=c == 0, stop=c == C - 1)
                                last.then_inc(sum_ok, 1)

        for k in range(3):
            hop(k)
            read_back(f"hop{k}", D)
            if k < 2:
                with nc.Block() as block:
                    @block.vector
                    def _(dve):
                        nc.vector.tensor_tensor(tmp[:, :, :], rows[:, :, 0:D], bc(dis[:, :], 2, D), ALU.mult)
                        dve.drain()
                        nc.vector.tensor_tensor(total[:, :, :], total[:, :, :], tmp[:, :, :], ALU.add)
                        nc.vector.tensor_tensor(qt[:, :, :], tmp[:, :, :], bc(dis[:, :], 2, D), ALU.mult)
                store_table(f"hop{k + 1}", [(hop_tab[k + 1].rearrange(by_tile, p=P), qt[:, :, :])])

        def l1_before(dve, aux_in, aux_ok):
            nc.vector.tensor_tensor(tmp[:, :, :], rows[:, :, 0:D], bc(dis[:, :], 2, D), ALU.mult)
            dve.drain()
            nc.vector.tensor_tensor(total[:, :, :], total[:, :, :], tmp[:, :, :], ALU.add)
            dve.drain()
            nc.vector.tensor_scalar(total[:, :, :], total[:, :, :], 0.25, None, ALU.mult)
            dve.drain()
            nc.vector.tensor_tensor(xrow[:, :, :], xrow[:, :, :], total[:, :, :], ALU.add)

        def l1_after(dve):
            nc.vector.tensor_copy(tab[:, :, 0:D], xrow[:, :, :])
            nc.vector.memset(tab[:, :, D + 1:D + 2], 1.0)
            nc.vector.memset(edge_c[:, :, :], 0.0)
            nc.vector.tensor_copy(attrep[:, :], attc[:, 1:2].to_broadcast([D, P]))

        layernorm("l1", l1_before, l1_after)

        def attention(tag, table, M, edge_features):
            begun, slot_free = sem(f"{tag}_begun"), sem(f"{tag}_free")
            idx_in, rows_in = [sem(f"{tag}_idx{s}") for s in range(NS)], [sem(f"{tag}_rows{s}") for s in range(NS)]
            pm_ok, pm_t, nd_ok, top_rep, drop_ok, decay_ok, arg_ok, prob_ok, sum_ok = (
                sem(f"{tag}_{n}") for n in ("pmax", "pmaxT", "diag", "toprep", "drop", "decay", "arg", "prob", "sum"))
            with nc.Block() as block:
                @block.sync
                def _(sp):
                    sweep_loads(sp, begun, slot_free, idx_in)

                @block.gpsimd
                def _(pool):
                    sweep_pool(pool, table, D + 2, g_edge, begun, idx_in, rows_in)

                @block.vector
                def _(dve):
                    nj = sweeps(dve)
                    reset_windows(dve)
                    nc.vector.memset(top[:, :], LOW)
                    dve.sem_inc(slot_free, NS)
                    with dve.Fori(0, nj) as j:
                        start_sweep(dve, begun)
                        with dve.Fori(0, IT) as it:
                            for s in range(NS):
                                g = it * NS + s
                                n = j * G + g + 1
                                ge = g_edge[:, s, :, :]
                                b = spans(dve, g)
                                nc.vector.tensor_tensor(far[:, :, :], bc(dst_rel[:, bass.ds(g, 1), :].rearrange("p g c -> p (g c)"), 2, W),
                                                        bc(iota[:, 0:W], 1, C), ALU.not_equal)
                                if edge_features:
                                    nc.vector.tensor_copy(ge[:, :, D + 2:D + 4], ea2[:, bass.ds(g, 1), :, :].rearrange("p g c k -> p (g c) k"))
                                dve.wait_ge(rows_in[s], (j * IT + it + 1) * (16 * C))
                                nc.vector.tensor_tensor(u_edge[:, :], ge[:, :, D], edge_c[:, bass.ds(g, 1), :].rearrange("p g c -> p (g c)"), ALU.add)
                                dve.drain()
                                nc.vector.tensor_tensor(logit[:, :, :], bc(u_edge[:, :], 2, W), bc(ad_row[:, bass.ds(b, W)], 1, C), ALU.add)
                                dve.drain()
                                nc.vector.scalar_tensor_tensor(logit2[:, :, :], logit[:, :, :], 0.01, logit[:, :, :], ALU.mult, ALU.max)
                                dve.drain()
                                nc.vector.scalar_tensor_tensor(logit[:, :, :], far[:, :, :], FAR, logit2[:, :, :], ALU.mult, ALU.add)
                                dve.drain()
                                nc.vector.tensor_reduce(pmax[:, :], logit[:, :, :].rearrange("p c n -> p n c"), AX.X, ALU.max).then_inc(pm_ok, 1)
                                dve.wait_ge(pm_t, n)
                                nc.vector.tensor_reduce(nmax[:, :], bank[0][0:W, 0:P], AX.X, ALU.max)
                                dve.drain()
                                nc.vector.tensor_scalar(ndiag[:, :], ident[0:W, 0:W], nmax[:, 0:1], None, ALU.mult).then_inc(nd_ok, 1)
                                dve.wait_ge(top_rep, n)
                                nc.vector.tensor_tensor(newtop[:, :], top[:, bass.ds(b, W)], bank[1][:, 0:W], ALU.max)
                                dve.drain()
                                nc.vector.tensor_tensor(drop[:, :], top[:, bass.ds(b, W)], newtop[:, :], ALU.subtract).then_inc(drop_ok, 1)
                                nc.vector.tensor_tensor(logit2[:, :, :], logit[:, :, :], bc(newtop[:, :], 1, C), ALU.subtract).then_inc(arg_ok, 1)
                                dve.drain()
                                nc.vector.tensor_copy(top[:, bass.ds(b, W)], newtop[:, :])
                                dve.wait_ge(decay_ok, n)
                                nc.vector.tensor_tensor(acc[0:M, bass.ds(b, W)], acc[0:M, bass.ds(b, W)], decay[0:M, :], ALU.mult)
                                dve.drain()
                                dve.wait_ge(sum_ok, n)
                                nc.vector.tensor_tensor(acc[0:M, bass.ds(b, W)], acc[0:M, bass.ds(b, W)], bank[2][0:M, 0:W], ALU.add).then_inc(slot_free, 1)
                                dve.drain()

                @block.scalar
                def _(act):
                    nj = sweeps(act)
                    with act.Fori(0, nj) as j:
                        with act.Fori(0, IT) as it:
                            for s in range(NS):
                                n = j * G + it * NS + s + 1
                                act.wait_ge(drop_ok, n)
                                nc.scalar.activation(decay[:, :], drop[:, :], ACT.Exp).then_inc(decay_ok, 1)
                                act.wait_ge(arg_ok, n)
                                nc.scalar.activation(prob[:, :, :], logit2[:, :, :], ACT.Exp).then_inc(prob_ok, 1)

                @block.tensor
                def _(pe):
                    nj = sweeps(pe)
                    with pe.Fori(0, nj) as j:
                        with pe.Fori(0, IT) as it:
                            for s in range(NS):
                                n = j * G + it * NS + s + 1
                                pe.wait_ge(pm_ok, n)
                                pass_on(pe)
                                nc.tensor.transpose(bank[0][0:W, 0:P], pmax[:, :], ident[:, :]).then_inc(pm_t, 1)
                                pe.wait_ge(nd_ok, n)
                                nc.tensor.matmul(bank[1][:, 0:W], ones[0:W, :], ndiag[:, :], start=True, stop=True).then_inc(top_rep, 1)
                                pe.wait_ge(prob_ok, n)
                                for c in range(C):
                                    last = nc.tensor.matmul(bank[2][0:M, 0:W], g_edge[:, s, c, 0:M], prob[:, c, :], start=c == 0, stop=c == C - 1)
                                last.then_inc(sum_ok, 1)

        project("l2", 1, D, attc[:, 0:1], lambda a, b, ps: nc.vector.tensor_copy(tab[:, a:b, D:D + 1], ps), attrep[:, :])
        store_table("l2", [(att_tab[0].rearrange(by_tile, p=P), tab[:, :, 0:D + 2])])
        attention("l2", att_tab[0], D + 2, False)
        read_back("l2", D + 2)

        def normalise(dve, width):
            nc.vector.tensor_scalar(stat[:, 0, :], rows[:, :, D + 1], 1e-30, None, ALU.max)
            dve.drain()
            nc.vector.reciprocal(stat[:, 1, :], stat[:, 0, :])
            dve.drain()
            nc.vector.tensor_tensor(tmp[:, :, :], rows[:, :, 0:D], bc(stat[:, 1, :], 2, D), ALU.mult)
            dve.drain()

        def l2_before(dve, aux_in, aux_ok):
            normalise(dve, D)
            nc.vector.tensor_scalar(total[:, :, :], tmp[:, :, :], 0.0, None, ALU.min)
            dve.drain().then_inc(aux_in, 1)
            dve.wait_ge(aux_ok, 1)
            nc.vector.tensor_scalar(qt[:, :, :], total[:, :, :], -1.0, None, ALU.add)
            dve.drain()
            nc.vector.scalar_tensor_tensor(total[:, :, :], tmp[:, :, :], 0.0, qt[:, :, :], ALU.max, ALU.add)
            dve.drain()
            nc.vector.tensor_tensor(xrow[:, :, :], xrow[:, :, :], total[:, :, :], ALU.add)

        def l2_exp(act, aux_in, aux_ok):
            act.wait_ge(aux_in, 1)
            nc.scalar.activation(total[:, :, :], total[:, :, :], ACT.Exp).then_inc(aux_ok, 1)

        layernorm("l2", l2_before, lambda dve: nc.vector.memset(tab[:, :, D + 1:D + 2], 1.0), (lambda pe, a, b: None, l2_exp))

        f_a, f_b, f_c, f_d = sem("fold_in"), sem("fold_out"), sem("fold_reps"), sem("fold_e2n")
        with nc.Block() as block:
            @block.vector
            def _(dve):
                nc.vector.tensor_copy(attrep[:, :], blk[:, 3:4].to_broadcast([D, P]))
                nc.vector.tensor_copy(w_e_rep[:, :], w_e[:, 0:1].to_broadcast([2, P]))
                nc.vector.tensor_copy(wedge_rep[:, 0, :], wedge[:, 0:1].to_broadcast([2, P]))
                nc.vector.tensor_copy(wedge_rep[:, 1, :], wedge[:, 1:2].to_broadcast([2, P]))
                dve.drain().then_inc(f_a, 1)
                dve.wait_ge(f_b, 1)
                nc.vector.tensor_copy(wfcT[:, D:D + 1], bank[0][0:D, 0:1])
                nc.vector.tensor_copy(attrep[:, :], bank[1][0:D, 0:P])
                nc.vector.tensor_copy(wmv[:, :, :], bank[2][0:1, 0:4 * D].rearrange("p (k f) -> p k f", k=4))
                nc.vector.tensor_copy(e2nT[:, :], bank[3][0:2, 0:D])
                nc.vector.tensor_copy(edge_w[:, :], bank[4][:, 0:2])
                dve.drain().then_inc(f_c, 1)
                dve.wait_ge(f_d, 1)
                nc.vector.tensor_copy(e2n_rep[:, :, :], bank[5][:, 0:2 * D].rearrange("p (k f) -> p k f", k=2))

            @block.tensor
            def _(pe):
                pe.wait_ge(f_a, 1)
                nc.tensor.matmul(bank[0][0:D, 0:1], wrow[:, 3, :], blk[:, 0:1], start=True, stop=True)
                nc.tensor.matmul(bank[1][0:D, 0:P], wrow[:, 3, :], attrep[:, :], start=True, stop=True)
                for i, (b, w) in enumerate(((1, 0), (2, 1), (4, 0), (5, 1))):
                    nc.tensor.matmul(bank[2][0:1, i * D:(i + 1) * D], blk[:, b:b + 1], wm[:, w, :], start=True, stop=True)
                nc.tensor.transpose(bank[3][0:2, 0:D], we2n[:, :], ident[0:D, 0:D])
                nc.tensor.matmul(bank[4][:, 0:2], w_e_rep[:, :], wedge[:, :], start=True, stop=True).then_inc(f_b, 1)
                pe.wait_ge(f_c, 1)
                nc.tensor.matmul(bank[5][:, 0:D], wedge_rep[:, 0, :], e2nT[:, :], start=True, stop=True)
                nc.tensor.matmul(bank[5][:, D:2 * D], wedge_rep[:, 1, :], e2nT[:, :], start=True, stop=True).then_inc(f_d, 1)

        project("l3", D + 1, D, wfcT[:, :], lambda a, b, ps: nc.vector.tensor_copy(tab[:, a:b, 0:D + 1], ps), attrep[:, :])
        store_table("l3", [(att_tab[1].rearrange(by_tile, p=P), tab[:, :, 0:D + 2])])

        mu_ok, zc_ok, mom_ok, root_in, root_ok, const_in, const_ok, zdone = (
            sem(f"m_{n}") for n in ("mean", "centred", "moment", "root_in", "root", "const_in", "const", "zdone"))
        with nc.Block() as block:
            @block.tensor
            def _(pe):
                for i, deg in enumerate((out_deg, in_deg)):
                    for t in range(NT):
                        last = nc.tensor.matmul(bank[i][:, 0:D], deg[:, t:t + 1].to_broadcast([P, P]), tab[:, t, 0:D], start=t == 0, stop=t == NT - 1)
                last.then_inc(mu_ok, 1)
                for i, deg in enumerate((out_deg, in_deg)):
                    pe.wait_ge(zc_ok, i + 1)
                    for t in range(NT):
                        nc.tensor.matmul(bank[2 + 2 * i][0:1, 0:D], deg[:, t:t + 1], total[:, t, :], start=t == 0, stop=t == NT - 1)
                        last = nc.tensor.matmul(bank[3 + 2 * i][0:1, 0:D], deg[:, t:t + 1], qt[:, t, :], start=t == 0, stop=t == NT - 1)
                    last.then_inc(mom_ok, 1)
                pe.wait_ge(const_in, 1)
                nc.tensor.matmul(bank[6][:, 0:1], ones[0:1, :], konst[:, :], start=True, stop=True).then_inc(const_ok, 1)

            @block.vector
            def _(dve):
                dve.wait_ge(mu_ok, 1)
                for i in range(2):
                    nc.vector.tensor_scalar(mean_z[:, :], bank[i][:, 0:D], 1.0 / E, None, ALU.mult)
                    dve.drain()
                    nc.vector.tensor_tensor(tmp[:, :, :], tab[:, :, 0:D], bc(mean_z[:, :], 1, NT), ALU.subtract)
                    dve.drain()
                    if i:
                        dve.wait_ge(mom_ok, 1)
                    nc.vector.tensor_tensor(total[:, :, :], tmp[:, :, :], tmp[:, :, :], ALU.mult)
                    dve.drain()
                    nc.vector.tensor_tensor(qt[:, :, :], total[:, :, :], tmp[:, :, :], ALU.mult).then_inc(zc_ok, 1)
                dve.wait_ge(mom_ok, 2)
                for i in range(2):
                    nc.vector.tensor_scalar(m_row[:, 2 * i, :], bank[2 + 2 * i][0:1, 0:D], 1.0 / E, None, ALU.mult)
                    nc.vector.tensor_scalar(m_row[:, 2 * i + 1, :], bank[3 + 2 * i][0:1, 0:D], 1.0 / E, None, ALU.mult)
                dve.drain()
                cubes = m_row[:, 0:4, :].rearrange("a (i k) f -> a i k f", k=2)[:, :, 1, :]
                signs = m_row[:, 4:8, :].rearrange("a (i k) f -> a i k f", k=2)[:, :, 1, :]
                sizes = m_row[:, 4:8, :].rearrange("a (i k) f -> a i k f", k=2)[:, :, 0, :]
                nc.vector.scalar_tensor_tensor(sizes, cubes, -1.0, cubes, ALU.mult, ALU.max)
                nc.vector.tensor_scalar(signs, cubes, 0.0, None, ALU.is_gt)
                dve.drain()
                nc.vector.tensor_scalar(cubes, cubes, 0.0, None, ALU.is_lt)
                dve.drain()
                nc.vector.tensor_tensor(signs, signs, cubes, ALU.subtract)
                nc.vector.tensor_scalar(sizes, sizes, 1e-19, None, ALU.max)
                dve.drain().then_inc(root_in, 1)
                dve.wait_ge(root_ok, 1)
                nc.vector.tensor_tensor(cubes, sizes, signs, ALU.mult)
                dve.drain()
                nc.vector.tensor_tensor(m_row[:, 4:8, :], m_row[:, 0:4, :], wmv[:, :, :], ALU.mult)
                dve.drain()
                nc.vector.tensor_reduce(konst[:, :], m_row[:, 4:8, :].rearrange("a k f -> a (k f)"), AX.X, ALU.add)
                dve.drain().then_inc(const_in, 1)
                dve.wait_ge(const_ok, 1)
                nc.vector.tensor_scalar(edge_t[:, :, :], ea2[:, :, :, 0], edge_w[:, 0:1], bank[6][:, 0:1], ALU.mult, ALU.add)
                dve.drain()
                nc.vector.scalar_tensor_tensor(edge_c[:, :, :], ea2[:, :, :, 1], edge_w[:, 1:2], edge_t[:, :, :], ALU.mult, ALU.add)

            @block.scalar
            def _(act):
                act.wait_ge(root_in, 1)
                squares = m_row[:, 0:4, :].rearrange("a (i k) f -> a i k f", k=2)[:, :, 0, :]
                sizes = m_row[:, 4:8, :].rearrange("a (i k) f -> a i k f", k=2)[:, :, 0, :]
                nc.scalar.activation(squares, squares, ACT.Sqrt)
                nc.scalar.activation(sizes, sizes, ACT.Ln)
                act.drain()
                nc.scalar.activation(sizes, sizes, ACT.Exp, scale=1.0 / 3.0)
                act.drain().then_inc(root_ok, 1)

        attention("l3", att_tab[1], D + 4, True)
        read_back("l3", D + 4)

        def l3_before(dve, aux_in, aux_ok):
            for k in range(2):
                nc.vector.tensor_tensor(total[:, :, :], bc(rows[:, :, D + 2 + k], 2, D), bc(e2n_rep[:, k, :], 1, NT), ALU.mult)
                dve.drain()
                nc.vector.tensor_tensor(rows[:, :, 0:D], rows[:, :, 0:D], total[:, :, :], ALU.add)
                dve.drain()
            normalise(dve, D)
            nc.vector.tensor_tensor(xrow[:, :, :], xrow[:, :, :], tmp[:, :, :], ALU.add)

        layernorm("l3", l3_before, lambda dve: None)
        stored = sem("out_stored")
        with nc.Block() as block:
            @block.sync
            def _(sp):
                sp.dma_start(out[0:(NT - 1) * P, :].rearrange(by_tile, p=P), xrow[:, 0:NT - 1, :]).then_inc(stored, 16)
                sp.dma_start(out[(NT - 1) * P:N, :], xrow[0:NL, NT - 1, :]).then_inc(stored, 16)
                sp.wait_ge(stored, 32)


_INS = ["x", "src", "dst", "edge_attr_2", "edge_attr_64", "L0_gnn_Wq", "L0_gnn_bq", "L0_gnn_Wk", "L0_gnn_bk",
        "L0_gnn_We", "L0_gnn_be", "L0_gnn_Wv", "L0_gnn_bv", "L2_gnn_attn_w", "L3_gnn_W_fc", "L3_gnn_W_attn",
        "L3_gnn_W_edge", "L3_gnn_W_e2n", "L3_gnn_W_m1", "L3_gnn_W_m2"]


def kernel(**inputs):
    import concourse.bacc as bacc
    from concourse.bass_utils import run_bass_kernel_spmd

    nc = bacc.Bacc("TRN2", target_bir_lowering=False, num_devices=1)
    arrays, args = {}, []
    for name in _INS:
        a = np.ascontiguousarray(inputs[name])
        arrays[f"in_{name}"] = a
        args.append(nc.dram_tensor(f"in_{name}", a.shape, mybir.dt.from_np(a.dtype), kind="ExternalInput").ap())
    out = nc.dram_tensor("out_0", (N, D), fp32, kind="ExternalOutput").ap()
    build(nc, *args, out)
    return run_bass_kernel_spmd(nc, [arrays], core_ids=[0]).results[0]["out_0"]
```

```python
import numpy as np
import concourse.bass as bass
from concourse import mybir
from contextlib import ExitStack

fp32, i32, u8 = mybir.dt.float32, mybir.dt.int32, mybir.dt.uint8
bf16, fp16, fp8 = mybir.dt.bfloat16, mybir.dt.float16, mybir.dt.float8e4
ALU, ACT, AX = mybir.AluOpType, mybir.ActivationFunctionType, mybir.AxisListType

P = 128
N, D, E = 3125, 64, 100000
H, DH = 4, 16
NT = -(-N // P)
NP = NT * P
NL = N - (NT - 1) * P
C = 8
ST = P * C
G = -(-E // ST)
PL = (E - (G - 1) * ST) // C
W = 64
TB = -(-(G * C) // P)
TE = E // P
GT = 2
GG = C // GT
WC = 14
KC = NT * WC
DIV = -(-(1 << 16) // WC)
NS = 2
IT = G // NS
NONE = 1.0e6
FAR = -1.0e30
LOW = -1.0e20
EPS = 1e-5
RT = 7
MT = 4
assert G % NS == 0 and (E - (G - 1) * ST) % C == 0


def build(nc, x, src, dst, edge_attr_2, edge_attr_64, Wq, bq, Wk, bk, We, be, Wv, bv,
          attn_w, W_fc, W_attn, W_edge, W_e2n, W_m1, W_m2, out):
    ctx = ExitStack()
    with ctx:
        def sb(name, shape, dt=fp32):
            return ctx.enter_context(nc.sbuf_tensor(name, shape, dt))

        def sem(name):
            return ctx.enter_context(nc.semaphore(name))

        def dram(name, shape):
            return nc.dram_tensor(name, shape, fp32, kind="Internal").ap()

        def bc(ap, axis, n):
            ap = ap.unsqueeze(axis)
            shape = list(ap.shape)
            shape[axis] = n
            return ap.to_broadcast(shape)

        kv_tab = dram("kv_tab", [NP, 2 * D])
        q_tab = dram("q_tab", [NP + W, D])
        hop_tab = [dram(f"hop_tab{i}", [NP, D]) for i in range(3)]
        att_tab = [dram(f"att_tab{i}", [NP, D + 2]) for i in range(2)]

        ident = sb("ident", [P, P])
        ones = sb("ones", [P, P])
        iota = sb("iota", [P, P])
        iota_neg = sb("iota_neg", [P, P])
        dst_rel0 = sb("dst_rel0", [P, G, C])
        dst_rel = sb("dst_rel", [P, G, C])
        edge_scratch = sb("edge_scratch", [P, G, C])
        base0 = sb("base0", [1, G, 8])
        base = sb("base", [1, G, 8])
        base_i = sb("base_i", [1, G, 8], i32)
        sweeps_f = sb("sweeps_f", [1, 4])
        sweeps_i = sb("sweeps_i", [1, 8], i32)
        flag_i = sb("flag_i", [1, 4], i32)
        xrow = sb("xrow", [P, NT, D])
        acc = sb("acc", [P, NP + W])
        xT = acc
        shared = sb("shared", [P, NT * (4 * D + 4)])

        def carve(*fields):
            at, views = 0, []
            for shape in fields:
                size = int(np.prod(shape))
                names = "abcd"[:len(shape)]
                view = shared[:, at:at + size]
                if len(shape) > 1:
                    view = view.rearrange(f"p ({' '.join(names)}) -> p {' '.join(names)}", **dict(zip(names, shape)))
                views.append(view)
                at += size
            assert at <= NT * (4 * D + 4)
            return views

        rows, tmp, total, qt = carve((NT, D + 4), (NT, D), (NT, D), (NT, D))
        kv, ea, hotT, eaT, prod, msg, qwin = carve((NS, C, 2 * D), (NS, C * D), (C * P,), (C * D,), (C * D,), (C, D + 1), (NS, D))
        hotT, qwin = hotT[0:W, :], qwin[0:W, :, :]
        stat = sb("stat", [P, 4, NT])
        dis = sb("dis", [P, NT])
        in_deg = sb("in_deg", [P, NT])
        out_deg = sb("out_deg", [P, NT])
        wrow = sb("wrow", [D, 5, D])
        webd = sb("webd", [P, P])
        wcat = sb("wcat", [D + 1, 3 * D])
        idx = sb("idx", [P, NS, C], i32)
        g_edge = sb("g_edge", [P, NS, C, D + 4])
        hot = sb("hot", [P, C, W])
        be_row = sb("be_row", [1, C, D])
        attc = sb("attc", [D, 2])
        attrep = sb("attrep", [D, P])
        blk = sb("blk", [D, 6])
        w_e = sb("w_e", [2, 1])
        wedge = sb("wedge", [2, 2])
        we2n = sb("we2n", [D, 2])
        wm = sb("wm", [D, 2, D])
        wfcT = sb("wfcT", [D, D + 1])
        small = sb("small", [P, 32])

        bits_u8 = sb("bits_u8", [P, NP], u8)
        zeros_b = sb("zeros_b", [P, P], fp16)
        bank = [ctx.enter_context(nc.psum_tensor(f"bank{i}", [P, 512], fp32)) for i in range(8)]

        early = ExitStack()
        ctx.enter_context(early)
        holder = [early]

        def sb(name, shape, dt=fp32):
            return holder[0].enter_context(nc.sbuf_tensor(name, shape, dt))

        score = sb("score", [P, C * H])
        expo = sb("expo", [P, C * H])
        count = sb("count", [P, NT, NP + 16], u8)
        tab = count[:, :, :].rearrange("p h n -> p (h n)")[:, 0:NT * 2 * D * 4].bitcast(fp32).rearrange("p (t f) -> p t f", t=NT)
        counting = ExitStack()
        ctx.enter_context(counting)
        holder[0] = counting
        tile_lo = sb("tile_lo", [P, G, C])
        tile_hi = sb("tile_hi", [P, G, C])
        tile_rel0 = sb("tile_rel0", [P, G * GG, GT])
        tile_key = sb("tile_key", [P, G, C])
        tile_rel = sb("tile_rel", [P, G * GG, GT])
        tile_hiw = sb("tile_hiw", [P, G, C])
        key_hot = sb("key_hot", [P, C, KC], fp16)
        lo_dist = sb("lo_dist", [P, C, P], fp16)
        lo_hot = sb("lo_hot", [P, C, P], fp16)
        iota_key = sb("iota_key", [P, KC], fp16)
        starting = ExitStack()
        ctx.enter_context(starting)
        holder[0] = starting
        dst_i = sb("dst_i", [P, G, C], i32)
        lowest = sb("lowest", [P, 4 * P])
        lowest_col = sb("lowest_col", [P, 4])
        lowest_diag = sb("lowest_diag", [P, 4, P])
        group_base = sb("group_base", [P, 4 * P])
        super_base = sb("super_base", [P, G])
        span = sb("span", [P, 4])
        iota_i = sb("iota_i", [P, KC], i32)
        webd_row = sb("webd_row", [P, P])

        s_zero, s_graph, s_x, s_w = sem("zeroed"), sem("graph_loaded"), sem("x_loaded"), sem("w_loaded")
        s_const, s_tail = sem("const"), sem("tail_loaded")
        s_rows, s_tiles, s_wt = sem("edge_rows_ready"), sem("edge_rows_turned"), sem("w_turned")
        s_base, s_basec, s_bdiag, s_brep = sem("low_ready"), sem("low_turned"), sem("diag_ready"), sem("base_spread")
        s_sp, s_spt = sem("span_ready"), sem("span_turned")
        src_r = acc[:, 0:TB * P].bitcast(i32).rearrange("p (k e) -> p k e", k=TB)
        dst_r = acc[:, TB * P:2 * TB * P].bitcast(i32).rearrange("p (k e) -> p k e", k=TB)
        lo_r = acc[:, 2 * TB * P:3 * TB * P].bitcast(i32).rearrange("p (k e) -> p k e", k=TB)
        tab_flat = tab[:, :, :].rearrange("p t f -> p (t f)")
        lo_f, hi_f, dst_f = (tab_flat[:, i * TB * P:(i + 1) * TB * P].rearrange("p (k e) -> p k e", k=TB) for i in range(3))

        with nc.Block() as block:
            @block.gpsimd
            def _(pool):
                nc.gpsimd.memset(ident[:, :], 0.0).then_inc(s_const, 1)
                nc.gpsimd.iota(iota_i[:, :], pattern=[[1, KC]], base=0, channel_multiplier=0).then_inc(s_const, 1)
                pool.wait_ge(s_const, 2)
                nc.gpsimd.affine_select(out=ident[:, :], in_=ident[:, :], compare_op=ALU.not_equal, fill=1.0,
                                        base=0, pattern=[[-1, P]], channel_multiplier=1).then_inc(s_const, 1)

            @block.sync
            def _(sp):
                full = (G - 1) * ST
                head = (TB - 1) * P * P
                sp.dma_start(dst_r[:, 0:TB - 1, :], dst[0:head].rearrange("(k r e) -> r k e", r=P, e=P)).then_inc(s_graph, 16)
                sp.dma_start(src_r[:, 0:TB - 1, :], src[0:head].rearrange("(k r e) -> r k e", r=P, e=P)).then_inc(s_graph, 16)
                sp.dma_start(dst_i[:, 0:G - 1, :], dst[0:full].rearrange("(g p c) -> p g c", p=P, c=C)).then_inc(s_graph, 16)
                sp.wait_ge(s_zero, 1)
                whole = TE - (TB - 1) * P
                for into, of in ((dst_r, dst), (src_r, src)):
                    sp.dma_start(into[0:whole, TB - 1, :], of[head:TE * P].rearrange("(r e) -> r e", e=P)).then_inc(s_tail, 16)
                    sp.dma_start(into[whole:whole + 1, TB - 1, 0:E - TE * P], of[TE * P:E].rearrange("(a e) -> a e", a=1)).then_inc(s_tail, 16)
                sp.dma_start(webd_row[0:D, 0:D], We).then_inc(s_tail, 16)
                sp.dma_start(webd_row[D:P, D:P], We).then_inc(s_tail, 16)
                sp.dma_start(xrow[0:NL, NT - 1, :], x[(NT - 1) * P:N, :]).then_inc(s_tail, 16)
                sp.dma_start(dst_i[0:PL, G - 1, :], dst[full:E].rearrange("(p c) -> p c", c=C)).then_inc(s_tail, 16)

            @block.scalar
            def _(act):
                act.dma_start(xrow[:, 0:NT - 1, :], x[0:(NT - 1) * P, :].rearrange("(t p) f -> p t f", p=P)).then_inc(s_x, 16)
                act.dma_start(wrow[:, 0, :], Wk).then_inc(s_w, 16)
                act.dma_start(wrow[:, 1, :], Wv).then_inc(s_w, 16)
                act.dma_start(wrow[:, 2, :], Wq).then_inc(s_w, 16)
                act.dma_start(wrow[:, 3, :], W_fc).then_inc(s_w, 16)
                for i, b in enumerate((bk, bv, bq)):
                    act.dma_start(wcat[D:D + 1, i * D:(i + 1) * D], b.rearrange("(a n) -> a n", a=1)).then_inc(s_w, 16)
                act.dma_start(be_row[:, :, :], be.rearrange("(a n) -> a n", a=1).unsqueeze(1).to_broadcast([1, C, D])).then_inc(s_w, 16)
                act.dma_start(attc[:, :], attn_w.rearrange("(k p) -> p k", p=D), allow_slow_non_contiguous=True).then_inc(s_w, 16)
                act.dma_start(blk[:, :], W_attn[0, 0:6 * D].rearrange("(k p) -> p k", p=D), allow_slow_non_contiguous=True).then_inc(s_w, 16)
                act.dma_start(w_e[:, :], W_attn[0, 6 * D:6 * D + 2].rearrange("(p a) -> p a", a=1), allow_slow_non_contiguous=True).then_inc(s_w, 16)
                act.dma_start(wedge[:, :], W_edge).then_inc(s_w, 16)
                act.dma_start(we2n[:, :], W_e2n).then_inc(s_w, 16)
                act.dma_start(wm[:, 0, :], W_m1).then_inc(s_w, 16)
                act.dma_start(wm[:, 1, :], W_m2).then_inc(s_w, 16)
                act.wait_ge(s_wt, 1)
                nc.scalar.activation(wcat[0:D, :], bank[3][0:D, 0:3 * D], ACT.Copy)
                nc.scalar.activation(wfcT[:, 0:D], bank[3][0:D, 3 * D:4 * D], ACT.Copy)
                nc.scalar.activation(webd[:, :], bank[4][:, 0:P], ACT.Copy)
                act.wait_ge(s_x, 16)

            @block.vector
            def _(dve):
                nc.vector.memset(dst_i[:, G - 1, :], int(NONE))
                nc.vector.memset(dst_r[:, TB - 1, :], int(NONE))
                nc.vector.memset(src_r[:, TB - 1, :], int(NONE))
                nc.vector.memset(webd_row[:, :], 0.0)
                nc.vector.memset(xrow[:, NT - 1, :], 0.0)
                dve.drain().then_inc(s_zero, 1)
                nc.vector.memset(ones[:, :], 1.0)
                nc.vector.memset(zeros_b[:, :], 0.0)
                nc.vector.memset(span[:, :], 0.0)
                nc.vector.memset(base0[:, :, :], 0.0)
                nc.vector.memset(lowest[:, :], NONE)
                dve.wait_ge(s_const, 3)
                nc.vector.tensor_copy(iota[:, :], iota_i[:, 0:P])
                nc.vector.tensor_scalar(iota_neg[:, :], iota_i[:, 0:P], -1.0, None, ALU.mult)
                nc.vector.tensor_copy(iota_key[:, :], iota_i[:, :])
                dve.wait_ge(s_graph, 48)
                dve.wait_ge(s_tail, 16 * 8)
                nc.vector.tensor_scalar(lo_r, src_r, P - 1, None, ALU.bitwise_and)
                nc.vector.tensor_copy(dst_f, dst_r)
                nc.vector.tensor_copy(dst_rel0[:, :, :], dst_i[:, :, :])
                dve.drain()
                nc.vector.tensor_copy(lo_f, lo_r)
                dve.drain()
                nc.vector.tensor_scalar(lo_r, src_r, 7, None, ALU.arith_shift_right)
                dve.drain()
                nc.vector.tensor_copy(hi_f, lo_r)
                dve.drain().then_inc(s_rows, 1)
                dve.wait_ge(s_tiles, 1)
                rest = G * C - 4 * P
                for into, (b0, b1) in ((tile_lo, (0, 1)), (tile_hi, (2, 5)), (tile_rel0, (6, 7))):
                    flat = into[:, :, :].rearrange("p a b -> p (a b)")
                    nc.vector.tensor_copy(flat[:, 0:4 * P], bank[b0][:, :])
                    nc.vector.tensor_copy(flat[:, 4 * P:G * C], bank[b1][:, 0:rest])
                dve.drain()
                nc.vector.tensor_reduce(lowest[:, 0:G * GG], tile_rel0[:, :, :], AX.X, ALU.min)
                dve.drain().then_inc(s_base, 1)
                dve.wait_ge(s_basec, 1)
                nc.vector.tensor_reduce(lowest_col[:, :], bank[0][:, :].rearrange("p (k e) -> p k e", k=4), AX.X, ALU.min)
                dve.drain()
                for k in range(4):
                    nc.vector.tensor_scalar(lowest_diag[:, k, :], ident[:, :], lowest_col[:, k:k + 1], None, ALU.mult)
                dve.drain().then_inc(s_bdiag, 1)
                dve.wait_ge(s_brep, 1)
                nc.vector.tensor_copy(group_base[:, :], bank[1][:, :])
                dve.drain()
                groups = group_base[:, 0:G * GG]
                nc.vector.tensor_reduce(super_base[:, :], groups.rearrange("p (g q) -> p g q", q=GG), AX.X, ALU.min)
                nc.vector.tensor_tensor(tile_rel0[:, :, :], tile_rel0[:, :, :], bc(groups, 2, GT), ALU.subtract)
                nc.vector.tensor_copy(base0[:, :, 1:1 + GG], group_base[0:1, 0:G * GG].rearrange("p (g q) -> p g q", q=GG))
                dve.drain()
                nc.vector.tensor_copy(base0[:, :, 0], super_base[0:1, :])
                nc.vector.tensor_tensor(dst_rel0[:, :, :], dst_rel0[:, :, :], bc(super_base[:, :], 2, C), ALU.subtract)
                nc.vector.scalar_tensor_tensor(tile_rel[:, :, :], tile_rel0[:, :, :], NONE / 10, tile_rel0[:, :, :], ALU.is_lt, ALU.mult)
                dve.drain()
                nc.vector.tensor_reduce(span[:, 2:3], dst_rel0[:, 0:G - 1, :], AX.XY, ALU.max)
                nc.vector.tensor_reduce(span[0:PL, 3:4], dst_rel0[0:PL, G - 1, :], AX.X, ALU.max)
                nc.vector.tensor_reduce(span[:, 1:2], tile_rel[:, :, :], AX.XY, ALU.max)
                dve.drain()
                nc.vector.tensor_reduce(span[:, 0:1], span[:, 2:4], AX.X, ALU.max)
                dve.drain().then_inc(s_sp, 1)
                dve.wait_ge(s_spt, 1)
                nc.vector.tensor_reduce(sweeps_f[:, 0:2], bank[2][0:1, 0:2 * P].rearrange("a (k e) -> a k e", k=2), AX.X, ALU.max)
                dve.drain()
                nc.vector.tensor_scalar(sweeps_f[:, 1:2], sweeps_f[:, 1:2], float(DIV), None, ALU.mult)
                dve.drain()
                nc.vector.tensor_copy(sweeps_i[:, 2:4], sweeps_f[:, 0:2])
                dve.drain()
                nc.vector.tensor_scalar(sweeps_i[:, 4:5], sweeps_i[:, 2:3], W.bit_length() - 1, None, ALU.arith_shift_right)
                nc.vector.tensor_scalar(sweeps_i[:, 5:6], sweeps_i[:, 3:4], 16, None, ALU.arith_shift_right)
                dve.drain()
                nc.vector.tensor_copy(sweeps_f[:, 0:2], sweeps_i[:, 4:6])
                dve.drain()
                nc.vector.tensor_tensor(sweeps_f[:, 2:3], sweeps_f[:, 0:1], sweeps_f[:, 1:2], ALU.max)
                dve.drain()
                nc.vector.tensor_scalar(sweeps_i[:, 0:1], sweeps_f[:, 0:1], 1.0, None, ALU.add)
                nc.vector.tensor_scalar(sweeps_i[:, 1:2], sweeps_f[:, 2:3], 1.0, None, ALU.add)
                nc.vector.tensor_scalar(tile_hiw[:, :, :], tile_hi[:, :, :], float(WC), 1.0, ALU.mult, ALU.add)
                nc.vector.memset(xT[D:D + 1, 0:NP], 1.0)

            @block.tensor
            def _(pe):
                pe.wait_ge(s_const, 3)
                pe.wait_ge(s_rows, 1)
                for rows_of, (b0, b1) in ((lo_f, (0, 1)), (hi_f, (2, 5)), (dst_f, (6, 7))):
                    for k in range(TB):
                        last = nc.tensor.transpose(bank[b0 if k < 4 else b1][:, k % 4 * P:(k % 4 + 1) * P], rows_of[:, k, :], ident[:, :])
                last.then_inc(s_tiles, 1)
                pe.wait_ge(s_w, 16 * 15)
                pe.wait_ge(s_tail, 16 * 8)
                for i in range(4):
                    nc.tensor.transpose(bank[3][0:D, i * D:(i + 1) * D], wrow[:, i, :], ident[0:D, 0:D])
                nc.tensor.transpose(bank[4][:, 0:P], webd_row[:, :], ident[:, :]).then_inc(s_wt, 1)
                pe.wait_ge(s_base, 1)
                for k in range(4):
                    last = nc.tensor.transpose(bank[0][:, k * P:(k + 1) * P], lowest[:, k * P:(k + 1) * P], ident[:, :])
                last.then_inc(s_basec, 1)
                pe.wait_ge(s_bdiag, 1)
                for k in range(4):
                    last = nc.tensor.matmul(bank[1][:, k * P:(k + 1) * P], ones[:, :], lowest_diag[:, k, :], start=True, stop=True)
                last.then_inc(s_brep, 1)
                pe.wait_ge(s_sp, 1)
                nc.tensor.transpose(bank[2][0:1, 0:P], span[:, 0:1], ident[:, :])
                nc.tensor.transpose(bank[2][0:1, P:2 * P], span[:, 1:2], ident[:, :]).then_inc(s_spt, 1)

        starting.close()
        holder[0] = counting

        def project(tag, cols, K, rhs, evacuate, row_rep=None):
            turned, copied, done, taken = (sem(f"{tag}_turned"), sem(f"{tag}_copied"), sem(f"{tag}_done"), sem(f"{tag}_taken"))
            arow, arow_out = sem(f"{tag}_arow"), sem(f"{tag}_arow_out")
            groups = [range(t, min(t + MT, NT)) for t in range(0, NT, MT)]
            per = max(1, min(2, 512 // cols))
            mms = [range(t, min(t + per, NT)) for t in range(0, NT, per)]
            chunks = [(c, min(c + 512, NP)) for c in range(0, NP, 512)]
            with nc.Block() as block:
                @block.tensor
                def _(pe):
                    for k, ts in enumerate(groups):
                        if k >= 2:
                            pe.wait_ge(copied, k - 1)
                        for j, t in enumerate(ts):
                            last = nc.tensor.transpose(bank[k % 2][0:D, j * P:(j + 1) * P], xrow[:, t, :], ident[:, :])
                        last.then_inc(turned, 1)
                    pe.wait_ge(copied, len(groups))
                    for k, ts in enumerate(mms):
                        if k >= 2:
                            pe.wait_ge(taken, k - 1)
                        for j, t in enumerate(ts):
                            last = nc.tensor.matmul(bank[2 + k % 2][:, j * cols:(j + 1) * cols], xT[0:K, t * P:(t + 1) * P],
                                                    rhs, start=True, stop=True)
                        last.then_inc(done, 1)
                    if row_rep is not None:
                        for k, (a, b) in enumerate(chunks):
                            if k >= 2:
                                pe.wait_ge(arow_out, k - 1)
                            nc.tensor.matmul(bank[4 + k % 2][:, 0:b - a], row_rep, xT[0:D, a:b], start=True, stop=True).then_inc(arow, 1)

                @block.scalar
                def _(act):
                    for k, ts in enumerate(groups):
                        act.wait_ge(turned, k + 1)
                        nc.scalar.activation(xT[0:D, ts[0] * P:(ts[-1] + 1) * P], bank[k % 2][0:D, 0:len(ts) * P], ACT.Copy).then_inc(copied, 1)
                    if row_rep is not None:
                        for k, (a, b) in enumerate(chunks):
                            act.wait_ge(arow, k + 1)
                            nc.scalar.activation(ad_row[:, a:b], bank[4 + k % 2][:, 0:b - a], ACT.Copy).then_inc(arow_out, 1)

                @block.vector
                def _(dve):
                    for k, ts in enumerate(mms):
                        dve.wait_ge(done, k + 1)
                        ps = bank[2 + k % 2][:, 0:len(ts) * cols].rearrange("p (t n) -> p t n", n=cols)
                        evacuate(ts[0], ts[-1] + 1, ps).then_inc(taken, 1)
                    if row_rep is not None:
                        nc.vector.memset(ad_row[:, NP:NP + W], 0.0)

        def store_table(tag, pairs):
            stored = sem(f"{tag}_stored")
            with nc.Block() as block:
                @block.sync
                def _(sp):
                    for t, view in pairs:
                        sp.dma_start(t, view).then_inc(stored, 16)
                    sp.wait_ge(stored, 16 * len(pairs))

        def take_l0(a, b, ps):
            nc.vector.tensor_scalar(tab[:, a:b, 0:D], ps[:, :, 0:D], DH ** -0.5, None, ALU.mult)
            nc.vector.tensor_copy(tab[:, a:b, D:2 * D], ps[:, :, D:2 * D])
            return nc.vector.tensor_copy(qt[:, a:b, :], ps[:, :, 2 * D:3 * D])

        project("l0", 3 * D, D + 1, wcat[:, :], take_l0)
        with nc.Block() as block:
            @block.vector
            def _(dve):
                nc.vector.memset(tmp[0:W, 0, :], 0.0)
        by_tile = "(t p) f -> p t f"
        store_table("l0", [(kv_tab.rearrange(by_tile, p=P), tab[:, :, :]),
                           (q_tab[0:NP, :].rearrange(by_tile, p=P), qt[:, :, :]),
                           (q_tab[NP:NP + W, :], tmp[0:W, 0, :])])

        def start_sweep(dve, ready, counting=False):
            nc.vector.tensor_scalar(dst_rel[:, :, :], dst_rel[:, :, :], float(-W), None, ALU.add)
            nc.vector.tensor_scalar(base[:, :, 0:1], base[:, :, 0:1], float(W), float(NP), ALU.add, ALU.min)
            if counting:
                nc.vector.tensor_scalar(base[:, :, 1:1 + GG], base[:, :, 1:1 + GG], float(WC), float(NP), ALU.add, ALU.min)
                nc.vector.tensor_scalar(tile_rel[:, :, :], tile_rel[:, :, :], float(-WC), None, ALU.add)
                dve.drain()
                rel = tile_rel[:, :, :].rearrange("p a b -> p (a b)")
                key, far_key = (t[:, :, :].rearrange("p a b -> p (a b)") for t in (tile_key, edge_scratch))
                nc.vector.tensor_tensor(key, rel, tile_hiw[:, :, :].rearrange("p a b -> p (a b)"), ALU.add)
                nc.vector.tensor_scalar(far_key, rel, 0.0, None, ALU.is_ge)
                dve.drain()
                nc.vector.tensor_tensor(key, key, far_key, ALU.mult)
                dve.drain()
                nc.vector.scalar_tensor_tensor(far_key, rel, float(WC), key, ALU.is_lt, ALU.mult)
                dve.drain()
                nc.vector.tensor_scalar(key, far_key, -1.0, None, ALU.add)
            dve.drain()
            nc.vector.tensor_copy(base_i[:, :, :], base[:, :, :])
            dve.drain().then_inc(ready, 1)

        def reset_windows(dve, counting=False):
            nc.vector.tensor_scalar(dst_rel[:, :, :], dst_rel0[:, :, :], float(W), None, ALU.add)
            nc.vector.tensor_scalar(base[:, :, :], base0[:, :, :], float(-W), None, ALU.add)
            if counting:
                nc.vector.tensor_scalar(tile_rel[:, :, :], tile_rel0[:, :, :], float(WC), None, ALU.add)
                dve.drain()
                nc.vector.tensor_scalar(base[:, :, 1:1 + GG], base0[:, :, 1:1 + GG], float(-WC), None, ALU.add)
                nc.vector.memset(base[:, :, 1 + GG:8], 0.0)
            else:
                dve.drain()
                nc.vector.memset(base[:, :, 1:8], 0.0)
            nc.vector.memset(acc[:, :], 0.0)
            dve.drain()

        def sweeps(eng, which=0):
            return eng.value_load(sweeps_i[0:1, which:which + 1], min_val=1, max_val=NP // WC + 1)

        def spans(eng, g):
            return eng.value_load(base_i[0:1, bass.ds(g, 1), 0:1].rearrange("a g k -> a (g k)"), min_val=0, max_val=NP)

        passed = sem("passed")

        def pass_on(eng):
            eng.sem_inc(passed, 1)

        ea_main = edge_attr_64[0:(G - 1) * ST, :].rearrange("(g p c) f -> g p (c f)", p=P, c=C)
        ea_last = edge_attr_64[(G - 1) * ST:E, :].rearrange("(p c) f -> p (c f)", c=C)

        src_main = src[0:(G - 1) * ST].rearrange("(g p c) -> g p c", p=P, c=C)
        src_last = src[(G - 1) * ST:E].rearrange("(p c) -> p c", c=C)

        def load_idx(sp, g, s, last, into):
            if last:
                sp.dma_start(idx[0:PL, s, :], src_last).then_inc(into, 16)
            else:
                sp.dma_start(idx[:, s, :], src_main[bass.ds(g, 1), :, :].rearrange("g p c -> (g p) c")).then_inc(into, 16)

        begun = sem("a_begun")
        slot_free, idx_in = sem("a_slot_free"), [sem(f"a_idx{s}") for s in range(NS)]
        ea_in, kv_in = [sem(f"a_ea{s}") for s in range(NS)], [sem(f"a_kv{s}") for s in range(NS)]
        hot_ok, ea_t, ea_ts, hot_t, hot_ts = sem("a_hot"), sem("a_eaT"), sem("a_eaTs"), sem("a_hotT"), sem("a_hotTs")
        ee_ok, qd_ok, sc_ok, ex_ok, msg_ok, sum_ok = (sem("a_ee"), sem("a_qd"), sem("a_score"), sem("a_exp"), sem("a_msg"), sem("a_sum"))
        key_ok, lo_ok, count_ok, bank_free = sem("a_key"), sem("a_lo"), sem("a_count"), sem("a_count_added")
        with nc.Block() as block:
            @block.sync
            def _(sp):
                nj = sweeps(sp, 1)
                with sp.Fori(0, nj) as j:
                    sp.wait_ge(begun, j + 1)
                    pass_on(sp)

                    def load(g, n, s, last):
                        sp.wait_ge(slot_free, n)
                        pass_on(sp)
                        load_idx(sp, g, s, last, idx_in[s])
                        b = spans(sp, g)
                        sp.dma_start(qwin[:, s, :], q_tab[bass.ds(b, W), :]).then_inc(ea_in[s], 16)
                        if last:
                            sp.dma_start(ea[0:PL, s, :], ea_last).then_inc(ea_in[s], 16)
                        else:
                            sp.dma_start(ea[:, s, :], ea_main[bass.ds(g, 1), :, :].rearrange("g p n -> (g p) n")).then_inc(ea_in[s], 16)

                    with sp.Fori(0, IT - 1) as it:
                        for s in range(NS):
                            load(it * NS + s, j * G + it * NS + s + 1, s, False)
                    for s in range(NS):
                        g = G - NS + s
                        load(g, j * G + g + 1, s, g == G - 1)

            @block.gpsimd
            def _(pool):
                nj = sweeps(pool, 1)
                with pool.Fori(0, nj) as j:
                    with pool.Fori(0, IT) as it:
                        for s in range(NS):
                            pool.wait_ge(idx_in[s], (j * IT + it + 1) * 16)
                            pass_on(pool)
                            for c in range(C):
                                nc.gpsimd.indirect_dma_start(
                                    kv[:, s, c, :], None, kv_tab, bass.IndirectOffsetOnAxis(ap=idx[:, s, c:c + 1], axis=0)
                                ).then_inc(kv_in[s], 16)

            @block.vector
            def _(dve):
                nj = sweeps(dve, 1)
                nc.vector.memset(count[:, :, :].rearrange("p h n -> p (h n)").bitcast(i32), 0)
                nc.vector.memset(msg[:, :, D:D + 1], 1.0)
                reset_windows(dve, True)
                dve.sem_inc(slot_free, NS)
                dve.sem_inc(bank_free, 2)
                with dve.Fori(0, nj) as j:
                    start_sweep(dve, begun, True)
                    with dve.Fori(0, IT) as it:
                        for s in range(NS):
                            g = it * NS + s
                            n = j * G + g + 1
                            m = j * IT + it + 1
                            nc.vector.tensor_tensor(hot[:, :, :], bc(dst_rel[:, bass.ds(g, 1), :].rearrange("p g c -> p (g c)"), 2, W),
                                                    bc(iota[:, 0:W], 1, C), ALU.is_equal).then_inc(hot_ok, 1)
                            keys = tile_key[:, bass.ds(g, 1), :].rearrange("p g c -> p (g c)")
                            for c in range(C):
                                last = nc.vector.tensor_scalar(key_hot[:, c, :], iota_key[:, :], keys[:, c:c + 1], None, ALU.is_equal)
                            last.then_inc(key_ok, 1)
                            b, *group_at = nc.values_load_multi_w_load_instructions(
                                base_i[0:1, bass.ds(g, 1), 0:1 + GG].rearrange("a g k -> a (g k)"), engines=[mybir.EngineType.DVE],
                                min_val=0, max_val=NP)[1]

                            def add_counts(q):
                                at = count[:, :, bass.ds(group_at[q], WC)]
                                dve.wait_ge(count_ok, j * (G * GG) + g * GG + q + 1)
                                nc.vector.tensor_tensor(at, at, bank[6 + q % 2][:, 0:KC].rearrange("p (h w) -> p h w", w=WC),
                                                        ALU.add).then_inc(bank_free, 1)
                                dve.drain()

                            kvs = kv[:, s, :, :]
                            dve.wait_ge(kv_in[s], m * (16 * C))
                            dve.wait_ge(ee_ok, n)
                            nc.vector.tensor_tensor(prod[:, :].rearrange("p (c f) -> p c f", c=C),
                                                    bank[3][:, :].rearrange("p (c f) -> p c f", c=C), kvs[:, :, 0:D], ALU.mult)
                            dve.drain()
                            dve.wait_ge(qd_ok, n)
                            nc.vector.tensor_tensor(prod[:, :], prod[:, :], bank[4][:, :], ALU.mult)
                            dve.drain()
                            nc.vector.tensor_reduce(score[:, :], prod[:, :].rearrange("p (a d) -> p a d", d=DH), AX.X, ALU.add)
                            dve.drain()
                            nc.vector.tensor_scalar(score[:, :], score[:, :], -5.0, 5.0, ALU.max, ALU.min).then_inc(sc_ok, 1)
                            add_counts(0)
                            add_counts(1)
                            dve.wait_ge(ex_ok, n)
                            nc.vector.tensor_tensor(msg[:, :, 0:D].rearrange("p c (h d) -> p c h d", h=H),
                                                    kvs[:, :, D:2 * D].rearrange("p c (h d) -> p c h d", h=H),
                                                    bc(expo[:, :].rearrange("p (c h) -> p c h", h=H), 3, DH), ALU.mult).then_inc(msg_ok, 1)
                            add_counts(2)
                            add_counts(3)
                            dve.wait_ge(sum_ok, n)
                            nc.vector.tensor_tensor(acc[0:D + 1, bass.ds(b, W)], acc[0:D + 1, bass.ds(b, W)], bank[5][0:D + 1, 0:W], ALU.add).then_inc(slot_free, 1)
                            dve.drain()

            @block.scalar
            def _(act):
                nj = sweeps(act, 1)
                with act.Fori(0, nj) as j:
                    with act.Fori(0, IT) as it:
                        for s in range(NS):
                            g = it * NS + s
                            n = j * G + g + 1
                            act.wait_ge(ea_t, n)
                            nc.scalar.activation(eaT[:, :], bank[0][:, :], ACT.Copy).then_inc(ea_ts, 1)
                            act.wait_ge(hot_t, n)
                            nc.scalar.activation(hotT[:, 0:512], bank[1][0:W, :], ACT.Copy)
                            nc.scalar.activation(hotT[:, 512:1024], bank[2][0:W, :], ACT.Copy).then_inc(hot_ts, 1)
                            los = tile_lo[:, bass.ds(g, 1), :].rearrange("p g c -> p (g c)")
                            for c in range(C):
                                nc.scalar.activation(lo_dist[:, c, :], iota_neg[:, :], ACT.Abs, bias=los[:, c:c + 1])
                            act.drain()
                            nc.scalar.activation(lo_hot[:, :, :], lo_dist[:, :, :], ACT.Relu, bias=1.0, scale=-1.0).then_inc(lo_ok, 1)
                            act.wait_ge(sc_ok, n)
                            nc.scalar.activation(expo[:, :], score[:, :], ACT.Exp).then_inc(ex_ok, 1)

            @block.tensor
            def _(pe):
                nj = sweeps(pe, 1)
                with pe.Fori(0, nj) as j:
                    with pe.Fori(0, IT) as it:
                        for s in range(NS):
                            g = it * NS + s
                            n = j * G + g + 1
                            m = j * IT + it + 1
                            pe.wait_ge(ea_in[s], m * 32)
                            for q in range(4):
                                last = nc.tensor.transpose(bank[0][:, q * P:(q + 1) * P], ea[:, s, q * P:(q + 1) * P], ident[:, :])
                            last.then_inc(ea_t, 1)
                            pe.wait_ge(hot_ok, n)
                            pass_on(pe)
                            for c in range(C):
                                last = nc.tensor.transpose(bank[1 + c // 4][0:W, c % 4 * P:(c % 4 + 1) * P], hot[:, c, :], ident[:, :])
                            last.then_inc(hot_t, 1)
                            pe.wait_ge(ea_ts, n)
                            for q in range(4):
                                nc.tensor.matmul(bank[3][:, q * P:(q + 1) * P], eaT[:, q * P:(q + 1) * P], webd[:, :],
                                                 start=q == 0, stop=False, skip_group_check=True)
                            last = nc.tensor.matmul(bank[3][:, :], ones[0:1, :], be_row[:, :, :].rearrange("a c f -> a (c f)"),
                                                    start=False, stop=True, skip_group_check=True)
                            last.then_inc(ee_ok, 1)
                            pe.wait_ge(hot_ts, n)
                            for c in range(C):
                                last = nc.tensor.matmul(bank[4][:, c * D:(c + 1) * D], hotT[:, c * P:(c + 1) * P], qwin[:, s, :], start=True, stop=True)
                            last.then_inc(qd_ok, 1)
                            pe.wait_ge(key_ok, n)
                            pe.wait_ge(lo_ok, n)
                            for q in range(GG):
                                pe.wait_ge(bank_free, j * (G * GG) + g * GG + q + 1)
                                pass_on(pe)
                                for i in range(GT):
                                    c = GT * q + i
                                    last = nc.tensor.matmul(bank[6 + q % 2][:, 0:KC], lo_hot[:, c, :], key_hot[:, c, :], start=i == 0, stop=i == GT - 1)
                                last.then_inc(count_ok, 1)
                            pe.wait_ge(msg_ok, n)
                            for c in range(C):
                                last = nc.tensor.matmul(bank[5][0:D + 1, 0:W], msg[:, c, :], hot[:, c, :], start=c == 0, stop=c == C - 1)
                            last.then_inc(sum_ok, 1)

        rows_turned = sem("rows_turned")
        read = []

        def read_back(M):
            turned, before = rows_turned, 4 * len(read)
            read.append(M)
            groups = [range(t, min(t + RT, NT)) for t in range(0, NT, RT)]
            with nc.Block() as block:
                @block.tensor
                def _(pe):
                    for k, ts in enumerate(groups):
                        for i, t in enumerate(ts):
                            last = nc.tensor.transpose(bank[k][:, i * M:(i + 1) * M], acc[0:M, t * P:(t + 1) * P], ident[0:M, 0:M])
                        last.then_inc(turned, 1)

                @block.vector
                def _(dve):
                    for k, ts in enumerate(groups):
                        dve.wait_ge(turned, before + k + 1)
                        nc.vector.tensor_copy(rows[:, ts[0]:ts[-1] + 1, 0:M], bank[k][:, 0:len(ts) * M].rearrange("p (t m) -> p t m", m=M))

        var_ok, std_ok = sem("variance_ready"), sem("deviation_ready")
        norms = []

        def layernorm(tag, before, after, replicate=None):
            norms.append(tag)
            nth = len(norms)
            aux_in, aux_ok = (sem(f"{tag}_aux_in"), sem(f"{tag}_aux")) if replicate is not None else (None, None)
            with nc.Block() as block:
                @block.vector
                def _(dve):
                    before(dve, aux_in, aux_ok)
                    dve.drain()
                    nc.vector.tensor_reduce(stat[:, 0, :], xrow[:, :, :], AX.X, ALU.add)
                    dve.drain()
                    nc.vector.tensor_scalar(stat[:, 1, :], stat[:, 0, :], 1.0 / D, None, ALU.mult)
                    dve.drain()
                    nc.vector.tensor_tensor(tmp[:, :, :], xrow[:, :, :], bc(stat[:, 1, :], 2, D), ALU.subtract)
                    dve.drain()
                    nc.vector.tensor_tensor(xrow[:, :, :], tmp[:, :, :], tmp[:, :, :], ALU.mult)
                    dve.drain()
                    nc.vector.tensor_reduce(stat[:, 2, :], xrow[:, :, :], AX.X, ALU.add)
                    dve.drain()
                    nc.vector.tensor_scalar(stat[:, 3, :], stat[:, 2, :], 1.0 / D, EPS, ALU.mult, ALU.add)
                    dve.drain().then_inc(var_ok, 1)
                    dve.wait_ge(std_ok, nth)
                    nc.vector.reciprocal(stat[:, 1, :], stat[:, 0, :])
                    dve.drain()
                    nc.vector.tensor_tensor(xrow[:, :, :], tmp[:, :, :], bc(stat[:, 1, :], 2, D), ALU.mult)
                    dve.drain()
                    after(dve)

                @block.scalar
                def _(act):
                    if replicate is not None:
                        replicate[1](act, aux_in, aux_ok)
                    act.wait_ge(var_ok, nth)
                    nc.scalar.activation(stat[:, 0, :], stat[:, 3, :], ACT.Sqrt).then_inc(std_ok, 1)

                @block.tensor
                def _(pe):
                    if replicate is not None:
                        replicate[0](pe, aux_in, aux_ok)

        ored, worst, worst_t = sem("counts_ored"), sem("worst_ready"), sem("worst_turned")
        half = NT // 2
        count8 = count[:, :, :].bitcast(fp8)
        bits = bits_u8[:, :].bitcast(i32)
        with nc.Block() as block:
            @block.vector
            def _(dve):
                nc.vector.memset(bits_u8[:, :], 0)
                for h in range(NT):
                    dve.drain()
                    nc.vector.tensor_tensor(bits, bits, count[:, h, 0:NP].bitcast(i32), ALU.bitwise_or).then_inc(ored, 1)
                dve.drain()
                nc.vector.tensor_reduce(small[:, 0:1], bits_u8[:, :], AX.X, ALU.max)
                dve.drain().then_inc(worst, 1)
                for h in range(half, NT):
                    nc.vector.tensor_scalar(count8[:, h, 0:NP], count[:, h, 0:NP], 1.0, None, ALU.mult, ALU.add,
                                            accum_out=out_deg[:, h:h + 1], saturate=False)
                dve.wait_ge(worst_t, 1)
                nc.vector.tensor_reduce(sweeps_f[:, 0:1], bank[0][0:1, 0:P], AX.X, ALU.max)
                dve.drain()
                nc.vector.tensor_scalar(flag_i[:, 0:1], sweeps_f[:, 0:1], 16.0, None, ALU.is_ge)

            @block.tensor
            def _(pe):
                pe.wait_ge(worst, 1)
                nc.tensor.transpose(bank[0][0:1, 0:P], small[:, 0:1], ident[:, :]).then_inc(worst_t, 1)

            @block.scalar
            def _(act):
                for h in range(half):
                    act.wait_ge(ored, h + 1)
                    nc.scalar.activation(count8[:, h, 0:NP], count[:, h, 0:NP], ACT.Copy, accum_out=out_deg[:, h:h + 1], saturate=False)

        def many(eng):
            return eng.value_load(flag_i[0:1, 0:1], min_val=0, max_val=1)

        gl_ok, gl_used, gl_done = sem("g_hots"), sem("g_hots_used"), sem("g_done")
        hi_hot = key_hot[:, :, 0:NT]
        with nc.Block() as block:
            @block.vector
            def _(dve):
                with dve.If(many(dve) > 0):
                    with dve.Fori(0, G) as g:
                        nc.vector.tensor_tensor(lo_hot[:, :, :], bc(tile_lo[:, bass.ds(g, 1), :].rearrange("p g c -> p (g c)"), 2, P),
                                                bc(iota[:, :], 1, C), ALU.is_equal)
                        nc.vector.tensor_tensor(hi_hot, bc(tile_hi[:, bass.ds(g, 1), :].rearrange("p g c -> p (g c)"), 2, NT),
                                                bc(iota[:, 0:NT], 1, C), ALU.is_equal)
                        dve.drain().then_inc(gl_ok, 1)
                        dve.wait_ge(gl_used, g + 1)
                        pass_on(dve)
                    dve.wait_ge(gl_done, 1)
                    nc.vector.tensor_copy(out_deg[:, :], bank[6][:, 0:NT])

            @block.tensor
            def _(pe):
                with pe.If(many(pe) > 0):
                    nc.tensor.matmul(bank[6][:, 0:NT], zeros_b[:, :], zeros_b[:, 0:NT], start=True, stop=False, skip_group_check=True)
                    with pe.Fori(0, G) as g:
                        pe.wait_ge(gl_ok, g + 1)
                        pass_on(pe)
                        for c in range(C):
                            last = nc.tensor.matmul(bank[6][:, 0:NT], lo_hot[:, c, :], hi_hot[:, c, :], start=False, stop=False, skip_group_check=True)
                        last.then_inc(gl_used, 1)
                    nc.tensor.matmul(bank[6][:, 0:NT], zeros_b[:, :], zeros_b[:, 0:NT], start=False, stop=True, skip_group_check=True).then_inc(gl_done, 1)

        counting.close()
        hopping = ExitStack()
        ctx.enter_context(hopping)
        holder[0] = hopping
        parts = sb("parts", [P, NT, 3, D], bf16)
        parts_new = sb("parts_new", [P, NT, 3, D], bf16)

        read_back(D + 1)

        def l0_before(dve, aux_in, aux_ok):
            nc.vector.tensor_tensor(xrow[:, :, :], xrow[:, :, :], rows[:, :, 0:D], ALU.add)
            nc.vector.tensor_copy(in_deg[:, :], rows[:, :, D])
            dve.drain()
            nc.vector.tensor_scalar(dis[:, :], in_deg[:, :], 1.0, None, ALU.max)
            dve.drain().then_inc(aux_in, 1)
            dve.wait_ge(aux_ok, 1)
            nc.vector.reciprocal(dis[:, :], small[:, 0:NT])
            nc.vector.tensor_scalar(stat[:, 0, :], in_deg[:, :], 1.0, None, ALU.min)
            dve.drain()
            nc.vector.tensor_tensor(dis[:, :], dis[:, :], stat[:, 0, :], ALU.mult)

        def l0_after(dve):
            nc.vector.tensor_tensor(qt[:, :, :], xrow[:, :, :], bc(dis[:, :], 2, D), ALU.mult)
            split(dve, parts, qt[:, :, :], tmp[:, :, :], rows[:, :, 0:D])
            nc.vector.tensor_copy(total[:, :, :], xrow[:, :, :])

        def root_degree(act, aux_in, aux_ok):
            act.wait_ge(aux_in, 1)
            nc.scalar.activation(small[:, 0:NT], dis[:, :], ACT.Sqrt).then_inc(aux_ok, 1)

        def split(dve, into, of, rest, rest2):
            dve.drain()
            nc.vector.tensor_copy(into[:, :, 0, :], of)
            dve.drain()
            nc.vector.tensor_tensor(rest, of, into[:, :, 0, :], ALU.subtract)
            dve.drain()
            nc.vector.tensor_copy(into[:, :, 1, :], rest)
            dve.drain()
            nc.vector.tensor_tensor(rest2, rest, into[:, :, 1, :], ALU.subtract)
            dve.drain()
            nc.vector.tensor_copy(into[:, :, 2, :], rest2)
            dve.drain()

        layernorm("l0", l0_before, l0_after, (lambda pe, a, b: None, root_degree))

        HG = [range(t, min(t + 2, NT)) for t in range(0, NT, 2)]
        x_ok, agg_ok, agg_used = sem("hop_rows"), sem("hop_sum"), sem("hop_sum_used")
        with nc.Block() as block:
            @block.tensor
            def _(pe):
                with pe.If(many(pe) < 1):
                    with pe.Fori(0, 3) as k:
                        pe.wait_ge(x_ok, k + 1)
                        pass_on(pe)
                        for q, ts in enumerate(HG):
                            if q >= 4:
                                pe.wait_ge(agg_used, k * len(HG) + q - 3)
                                pass_on(pe)
                            for i, t in enumerate(ts):
                                for h in range(NT):
                                    last = nc.tensor.matmul(bank[q % 4][:, i * 3 * D:(i + 1) * 3 * D], count8[:, h, t * P:(t + 1) * P],
                                                            parts[:, h, :, :].rearrange("p k f -> p (k f)"), start=h == 0, stop=h == NT - 1)
                            last.then_inc(agg_ok, 1)

            @block.vector
            def _(dve):
                with dve.If(many(dve) < 1):
                    dve.sem_inc(x_ok, 1)
                    with dve.Fori(0, 3) as k:
                        for q, ts in enumerate(HG):
                            w = slice(ts[0], ts[-1] + 1)
                            dve.wait_ge(agg_ok, k * len(HG) + q + 1)
                            nc.vector.tensor_reduce(tmp[:, w, :], bank[q % 4][:, 0:len(ts) * 3 * D].rearrange("p (t k f) -> p t f k", k=3, f=D),
                                                    AX.X, ALU.add).then_inc(agg_used, 1)
                            dve.drain()
                            nc.vector.tensor_tensor(rows[:, w, 0:D], tmp[:, w, :], bc(dis[:, w], 2, D), ALU.mult)
                            dve.drain()
                            nc.vector.tensor_tensor(total[:, w, :], total[:, w, :], rows[:, w, 0:D], ALU.add)
                            nc.vector.tensor_tensor(qt[:, w, :], rows[:, w, 0:D], bc(dis[:, w], 2, D), ALU.mult)
                            split(dve, parts_new[:, w, :, :], qt[:, w, :], tmp[:, w, :], rows[:, w, 0:D])
                        nc.vector.tensor_copy(parts[:, :, :, :], parts_new[:, :, :, :])
                        dve.drain().then_inc(x_ok, 1)

        def sweep_pool(pool, table, width, into, idx_in, rows_in, k=0):
            nj = sweeps(pool)
            with pool.Fori(k * nj, (k + 1) * nj) as j:
                with pool.Fori(0, IT) as it:
                    for s in range(NS):
                        pool.wait_ge(idx_in[s], (j * IT + it + 1) * 16)
                        pass_on(pool)
                        for c in range(C):
                            nc.gpsimd.indirect_dma_start(
                                into[:, s, c, 0:width], None, table, bass.IndirectOffsetOnAxis(ap=idx[:, s, c:c + 1], axis=0)
                            ).then_inc(rows_in[s], 16)

        def sweep_loads(sp, begun, slot_free, idx_in, k=0):
            nj = sweeps(sp)
            with sp.Fori(k * nj, (k + 1) * nj) as j:
                sp.wait_ge(begun, j + 1)
                pass_on(sp)
                with sp.Fori(0, IT - 1) as it:
                    for s in range(NS):
                        sp.wait_ge(slot_free, j * G + it * NS + s + 1)
                        load_idx(sp, it * NS + s, s, False, idx_in[s])
                for s in range(NS):
                    g = G - NS + s
                    sp.wait_ge(slot_free, j * G + g + 1)
                    load_idx(sp, g, s, g == G - 1, idx_in[s])

        begun, slot_free, hot_ok, sum_ok = sem("h_begun"), sem("h_free"), sem("h_hot"), sem("h_sum")
        idx_in, rows_in = [sem(f"h_idx{s}") for s in range(NS)], [sem(f"h_rows{s}") for s in range(NS)]
        turned, stored = sem("h_turned"), sem("h_stored")

        def hop(k):
            with nc.Block() as block:
                @block.sync
                def _(sp):
                    with sp.If(many(sp) > 0):
                        sp.dma_start(hop_tab[k].rearrange(by_tile, p=P), qt[:, :, :]).then_inc(stored, 16)
                        sp.wait_ge(stored, 16 * (k + 1))
                        sweep_loads(sp, begun, slot_free, idx_in, k)

                @block.gpsimd
                def _(pool):
                    with pool.If(many(pool) > 0):
                        pool.wait_ge(stored, 16 * (k + 1))
                        sweep_pool(pool, hop_tab[k], D, g_edge, idx_in, rows_in, k)

                @block.vector
                def _(dve):
                    with dve.If(many(dve) > 0):
                        nj = sweeps(dve)
                        reset_windows(dve)
                        if k == 0:
                            dve.sem_inc(slot_free, NS)
                        with dve.Fori(k * nj, (k + 1) * nj) as j:
                            start_sweep(dve, begun)
                            with dve.Fori(0, IT) as it:
                                for s in range(NS):
                                    g = it * NS + s
                                    n = j * G + g + 1
                                    nc.vector.tensor_tensor(hot[:, :, :], bc(dst_rel[:, bass.ds(g, 1), :].rearrange("p g c -> p (g c)"), 2, W),
                                                            bc(iota[:, 0:W], 1, C), ALU.is_equal).then_inc(hot_ok, 1)
                                    b = spans(dve, g)
                                    dve.wait_ge(sum_ok, n)
                                    nc.vector.tensor_tensor(acc[0:D, bass.ds(b, W)], acc[0:D, bass.ds(b, W)], bank[5][0:D, 0:W], ALU.add).then_inc(slot_free, 1)
                                    dve.drain()
                        for q in range(-(-NT // RT)):
                            ts = range(q * RT, min((q + 1) * RT, NT))
                            dve.wait_ge(turned, k * 4 + q + 1)
                            nc.vector.tensor_tensor(tmp[:, ts[0]:ts[-1] + 1, :], bank[q][:, 0:len(ts) * D].rearrange("p (t m) -> p t m", m=D),
                                                    bc(dis[:, ts[0]:ts[-1] + 1], 2, D), ALU.mult)
                        dve.drain()
                        nc.vector.tensor_tensor(total[:, :, :], total[:, :, :], tmp[:, :, :], ALU.add)
                        nc.vector.tensor_tensor(qt[:, :, :], tmp[:, :, :], bc(dis[:, :], 2, D), ALU.mult)

                @block.tensor
                def _(pe):
                    with pe.If(many(pe) > 0):
                        nj = sweeps(pe)
                        with pe.Fori(k * nj, (k + 1) * nj) as j:
                            with pe.Fori(0, IT) as it:
                                for s in range(NS):
                                    pe.wait_ge(hot_ok, j * G + it * NS + s + 1)
                                    pe.wait_ge(rows_in[s], (j * IT + it + 1) * (16 * C))
                                    for c in range(C):
                                        last = nc.tensor.matmul(bank[5][0:D, 0:W], g_edge[:, s, c, 0:D], hot[:, c, :], start=c == 0, stop=c == C - 1)
                                    last.then_inc(sum_ok, 1)
                        pe.wait_ge(slot_free, (k + 1) * nj * G + NS)
                        pass_on(pe)
                        for q in range(-(-NT // RT)):
                            for i, t in enumerate(range(q * RT, min((q + 1) * RT, NT))):
                                last = nc.tensor.transpose(bank[q][:, i * D:(i + 1) * D], acc[0:D, t * P:(t + 1) * P], ident[0:D, 0:D])
                            last.then_inc(turned, 1)

        for k in range(3):
            hop(k)

        def l1_before(dve, aux_in, aux_ok):
            nc.vector.tensor_scalar(total[:, :, :], total[:, :, :], 0.25, None, ALU.mult)
            dve.drain()
            nc.vector.tensor_tensor(xrow[:, :, :], xrow[:, :, :], total[:, :, :], ALU.add)

        def l1_after(dve):
            nc.vector.tensor_copy(tab[:, :, 0:D], xrow[:, :, :])
            nc.vector.memset(tab[:, :, D + 1:D + 2], 1.0)
            nc.vector.memset(edge_c[:, :, :], 0.0)
            nc.vector.tensor_copy(attrep[:, :], attc[:, 1:2].to_broadcast([D, P]))
            nc.vector.memset(ea2[:, G - 1, :, :], 0.0)

        hopping.close()
        early.close()
        holder[0] = ctx
        tab = sb("tab", [P, NT, 2 * D])
        ea2 = sb("ea2", [P, G, C, 2])
        ad_row = sb("ad_row", [P, NP + W])
        top = sb("top", [P, NP + W])
        edge_c = sb("edge_c", [P, G, C])
        edge_t = sb("edge_t", [P, G, C])
        u_edge = sb("u_edge", [P, C])
        logit = sb("logit", [P, C, W])
        logit2 = sb("logit2", [P, C, W])
        prob = sb("prob", [P, C, W])
        far = sb("far", [P, C, W])
        pmax = sb("pmax", [P, W])
        nmax = sb("nmax", [W, 1])
        ndiag = sb("ndiag", [W, W])
        newtop = sb("newtop", [P, W])
        drop = sb("drop", [P, W])
        decay = sb("decay", [P, W])
        w_e_rep = sb("w_e_rep", [2, P])
        m_row = sb("m_row", [1, 8, D])
        wmv = sb("wmv", [1, 4, D])
        wedge_rep = sb("wedge_rep", [2, 2, P])
        edge_w = sb("edge_w", [P, 2])
        e2n_rep = sb("e2n_rep", [P, 2, D])
        konst = sb("konst", [1, 1])
        mean_z = sb("mean_z", [P, D])
        e2nT = sb("e2nT", [2, D])


        layernorm("l1", l1_before, l1_after)

        def attention(tag, table, M, edge_features):
            begun, slot_free = sem(f"{tag}_begun"), sem(f"{tag}_free")
            idx_in, rows_in = [sem(f"{tag}_idx{s}") for s in range(NS)], [sem(f"{tag}_rows{s}") for s in range(NS)]
            pm_ok, pm_t, nd_ok, top_rep, drop_ok, decay_ok, arg_ok, prob_ok, sum_ok = (
                sem(f"{tag}_{n}") for n in ("pmax", "pmaxT", "diag", "toprep", "drop", "decay", "arg", "prob", "sum"))
            with nc.Block() as block:
                @block.sync
                def _(sp):
                    sweep_loads(sp, begun, slot_free, idx_in)

                @block.gpsimd
                def _(pool):
                    sweep_pool(pool, table, D + 2, g_edge, idx_in, rows_in)

                @block.vector
                def _(dve):
                    nj = sweeps(dve)
                    reset_windows(dve)
                    nc.vector.memset(top[:, :], LOW)
                    dve.sem_inc(slot_free, NS)
                    with dve.Fori(0, nj) as j:
                        start_sweep(dve, begun)
                        with dve.Fori(0, IT) as it:
                            for s in range(NS):
                                g = it * NS + s
                                n = j * G + g + 1
                                ge = g_edge[:, s, :, :]
                                b = spans(dve, g)
                                nc.vector.tensor_tensor(far[:, :, :], bc(dst_rel[:, bass.ds(g, 1), :].rearrange("p g c -> p (g c)"), 2, W),
                                                        bc(iota[:, 0:W], 1, C), ALU.not_equal)
                                if edge_features:
                                    nc.vector.tensor_copy(ge[:, :, D + 2:D + 4], ea2[:, bass.ds(g, 1), :, :].rearrange("p g c k -> p (g c) k"))
                                dve.wait_ge(rows_in[s], (j * IT + it + 1) * (16 * C))
                                nc.vector.tensor_tensor(u_edge[:, :], ge[:, :, D], edge_c[:, bass.ds(g, 1), :].rearrange("p g c -> p (g c)"), ALU.add)
                                dve.drain()
                                nc.vector.tensor_tensor(logit[:, :, :], bc(u_edge[:, :], 2, W), bc(ad_row[:, bass.ds(b, W)], 1, C), ALU.add)
                                dve.drain()
                                nc.vector.scalar_tensor_tensor(logit2[:, :, :], logit[:, :, :], 0.01, logit[:, :, :], ALU.mult, ALU.max)
                                dve.drain()
                                nc.vector.scalar_tensor_tensor(logit[:, :, :], far[:, :, :], FAR, logit2[:, :, :], ALU.mult, ALU.add)
                                dve.drain()
                                nc.vector.tensor_reduce(pmax[:, :], logit[:, :, :].rearrange("p c n -> p n c"), AX.X, ALU.max).then_inc(pm_ok, 1)
                                dve.wait_ge(pm_t, n)
                                nc.vector.tensor_reduce(nmax[:, :], bank[0][0:W, 0:P], AX.X, ALU.max)
                                dve.drain()
                                nc.vector.tensor_scalar(ndiag[:, :], ident[0:W, 0:W], nmax[:, 0:1], None, ALU.mult).then_inc(nd_ok, 1)
                                dve.wait_ge(top_rep, n)
                                nc.vector.tensor_tensor(newtop[:, :], top[:, bass.ds(b, W)], bank[1][:, 0:W], ALU.max)
                                dve.drain()
                                nc.vector.tensor_tensor(drop[:, :], top[:, bass.ds(b, W)], newtop[:, :], ALU.subtract).then_inc(drop_ok, 1)
                                nc.vector.tensor_tensor(logit2[:, :, :], logit[:, :, :], bc(newtop[:, :], 1, C), ALU.subtract).then_inc(arg_ok, 1)
                                dve.drain()
                                nc.vector.tensor_copy(top[:, bass.ds(b, W)], newtop[:, :])
                                dve.wait_ge(decay_ok, n)
                                nc.vector.tensor_tensor(acc[0:M, bass.ds(b, W)], acc[0:M, bass.ds(b, W)], decay[0:M, :], ALU.mult)
                                dve.drain()
                                dve.wait_ge(sum_ok, n)
                                nc.vector.tensor_tensor(acc[0:M, bass.ds(b, W)], acc[0:M, bass.ds(b, W)], bank[2][0:M, 0:W], ALU.add).then_inc(slot_free, 1)
                                dve.drain()

                @block.scalar
                def _(act):
                    nj = sweeps(act)
                    with act.Fori(0, nj) as j:
                        with act.Fori(0, IT) as it:
                            for s in range(NS):
                                n = j * G + it * NS + s + 1
                                act.wait_ge(drop_ok, n)
                                nc.scalar.activation(decay[:, :], drop[:, :], ACT.Exp).then_inc(decay_ok, 1)
                                act.wait_ge(arg_ok, n)
                                nc.scalar.activation(prob[:, :, :], logit2[:, :, :], ACT.Exp).then_inc(prob_ok, 1)

                @block.tensor
                def _(pe):
                    nj = sweeps(pe)
                    with pe.Fori(0, nj) as j:
                        with pe.Fori(0, IT) as it:
                            for s in range(NS):
                                n = j * G + it * NS + s + 1
                                pe.wait_ge(pm_ok, n)
                                pass_on(pe)
                                nc.tensor.transpose(bank[0][0:W, 0:P], pmax[:, :], ident[:, :]).then_inc(pm_t, 1)
                                pe.wait_ge(nd_ok, n)
                                nc.tensor.matmul(bank[1][:, 0:W], ones[0:W, :], ndiag[:, :], start=True, stop=True).then_inc(top_rep, 1)
                                pe.wait_ge(prob_ok, n)
                                for c in range(C):
                                    last = nc.tensor.matmul(bank[2][0:M, 0:W], g_edge[:, s, c, 0:M], prob[:, c, :], start=c == 0, stop=c == C - 1)
                                last.then_inc(sum_ok, 1)

        project("l2", 1, D, attc[:, 0:1], lambda a, b, ps: nc.vector.tensor_copy(tab[:, a:b, D:D + 1], ps), attrep[:, :])
        store_table("l2", [(att_tab[0].rearrange(by_tile, p=P), tab[:, :, 0:D + 2])])
        attention("l2", att_tab[0], D + 2, False)
        read_back(D + 2)

        def normalise(dve, width):
            nc.vector.tensor_scalar(stat[:, 0, :], rows[:, :, D + 1], 1e-30, None, ALU.max)
            dve.drain()
            nc.vector.reciprocal(stat[:, 1, :], stat[:, 0, :])
            dve.drain()
            nc.vector.tensor_tensor(tmp[:, :, :], rows[:, :, 0:D], bc(stat[:, 1, :], 2, D), ALU.mult)
            dve.drain()

        def l2_before(dve, aux_in, aux_ok):
            normalise(dve, D)
            nc.vector.tensor_scalar(total[:, :, :], tmp[:, :, :], 0.0, None, ALU.min)
            dve.drain().then_inc(aux_in, 1)
            dve.wait_ge(aux_ok, 1)
            nc.vector.tensor_scalar(qt[:, :, :], total[:, :, :], -1.0, None, ALU.add)
            dve.drain()
            nc.vector.scalar_tensor_tensor(total[:, :, :], tmp[:, :, :], 0.0, qt[:, :, :], ALU.max, ALU.add)
            dve.drain()
            nc.vector.tensor_tensor(xrow[:, :, :], xrow[:, :, :], total[:, :, :], ALU.add)

        def l2_exp(act, aux_in, aux_ok):
            act.wait_ge(aux_in, 1)
            nc.scalar.activation(total[:, :, :], total[:, :, :], ACT.Exp).then_inc(aux_ok, 1)

        layernorm("l2", l2_before, lambda dve: nc.vector.memset(tab[:, :, D + 1:D + 2], 1.0), (lambda pe, a, b: None, l2_exp))

        ea2_in = sem("edge_attr_2_loaded")
        f_a, f_b, f_c, f_d = sem("fold_in"), sem("fold_out"), sem("fold_reps"), sem("fold_e2n")
        with nc.Block() as block:
            @block.sync
            def _(sp):
                full = (G - 1) * ST
                sp.dma_start(ea2[:, 0:G - 1, :, :], edge_attr_2[0:full, :].rearrange("(g p c) k -> p g c k", p=P, c=C)).then_inc(ea2_in, 16)
                sp.dma_start(ea2[0:PL, G - 1, :, :], edge_attr_2[full:E, :].rearrange("(p c) k -> p c k", c=C)).then_inc(ea2_in, 16)
                sp.wait_ge(ea2_in, 32)

            @block.vector
            def _(dve):
                nc.vector.tensor_copy(attrep[:, :], blk[:, 3:4].to_broadcast([D, P]))
                nc.vector.tensor_copy(w_e_rep[:, :], w_e[:, 0:1].to_broadcast([2, P]))
                nc.vector.tensor_copy(wedge_rep[:, 0, :], wedge[:, 0:1].to_broadcast([2, P]))
                nc.vector.tensor_copy(wedge_rep[:, 1, :], wedge[:, 1:2].to_broadcast([2, P]))
                dve.drain().then_inc(f_a, 1)
                dve.wait_ge(f_b, 1)
                nc.vector.tensor_copy(wfcT[:, D:D + 1], bank[0][0:D, 0:1])
                nc.vector.tensor_copy(attrep[:, :], bank[1][0:D, 0:P])
                nc.vector.tensor_copy(wmv[:, :, :], bank[2][0:1, 0:4 * D].rearrange("p (k f) -> p k f", k=4))
                nc.vector.tensor_copy(e2nT[:, :], bank[3][0:2, 0:D])
                nc.vector.tensor_copy(edge_w[:, :], bank[4][:, 0:2])
                dve.drain().then_inc(f_c, 1)
                dve.wait_ge(f_d, 1)
                nc.vector.tensor_copy(e2n_rep[:, :, :], bank[5][:, 0:2 * D].rearrange("p (k f) -> p k f", k=2))

            @block.tensor
            def _(pe):
                pe.wait_ge(f_a, 1)
                nc.tensor.matmul(bank[0][0:D, 0:1], wrow[:, 3, :], blk[:, 0:1], start=True, stop=True)
                nc.tensor.matmul(bank[1][0:D, 0:P], wrow[:, 3, :], attrep[:, :], start=True, stop=True)
                for i, (b, w) in enumerate(((1, 0), (2, 1), (4, 0), (5, 1))):
                    nc.tensor.matmul(bank[2][0:1, i * D:(i + 1) * D], blk[:, b:b + 1], wm[:, w, :], start=True, stop=True)
                nc.tensor.transpose(bank[3][0:2, 0:D], we2n[:, :], ident[0:D, 0:D])
                nc.tensor.matmul(bank[4][:, 0:2], w_e_rep[:, :], wedge[:, :], start=True, stop=True).then_inc(f_b, 1)
                pe.wait_ge(f_c, 1)
                nc.tensor.matmul(bank[5][:, 0:D], wedge_rep[:, 0, :], e2nT[:, :], start=True, stop=True)
                nc.tensor.matmul(bank[5][:, D:2 * D], wedge_rep[:, 1, :], e2nT[:, :], start=True, stop=True).then_inc(f_d, 1)

        project("l3", D + 1, D, wfcT[:, :], lambda a, b, ps: nc.vector.tensor_copy(tab[:, a:b, 0:D + 1], ps), attrep[:, :])
        store_table("l3", [(att_tab[1].rearrange(by_tile, p=P), tab[:, :, 0:D + 2])])

        mu_ok, zc_ok, mom_ok, root_in, root_ok, const_in, const_ok, zdone = (
            sem(f"m_{n}") for n in ("mean", "centred", "moment", "root_in", "root", "const_in", "const", "zdone"))
        with nc.Block() as block:
            @block.tensor
            def _(pe):
                for i, deg in enumerate((out_deg, in_deg)):
                    for t in range(NT):
                        last = nc.tensor.matmul(bank[i][:, 0:D], deg[:, t:t + 1].to_broadcast([P, P]), tab[:, t, 0:D], start=t == 0, stop=t == NT - 1)
                last.then_inc(mu_ok, 1)
                for i, deg in enumerate((out_deg, in_deg)):
                    pe.wait_ge(zc_ok, i + 1)
                    for t in range(NT):
                        nc.tensor.matmul(bank[2 + 2 * i][0:1, 0:D], deg[:, t:t + 1], total[:, t, :], start=t == 0, stop=t == NT - 1)
                        last = nc.tensor.matmul(bank[3 + 2 * i][0:1, 0:D], deg[:, t:t + 1], qt[:, t, :], start=t == 0, stop=t == NT - 1)
                    last.then_inc(mom_ok, 1)
                pe.wait_ge(const_in, 1)
                nc.tensor.matmul(bank[6][:, 0:1], ones[0:1, :], konst[:, :], start=True, stop=True).then_inc(const_ok, 1)

            @block.vector
            def _(dve):
                dve.wait_ge(mu_ok, 1)
                for i in range(2):
                    nc.vector.tensor_scalar(mean_z[:, :], bank[i][:, 0:D], 1.0 / E, None, ALU.mult)
                    dve.drain()
                    nc.vector.tensor_tensor(tmp[:, :, :], tab[:, :, 0:D], bc(mean_z[:, :], 1, NT), ALU.subtract)
                    dve.drain()
                    if i:
                        dve.wait_ge(mom_ok, 1)
                    nc.vector.tensor_tensor(total[:, :, :], tmp[:, :, :], tmp[:, :, :], ALU.mult)
                    dve.drain()
                    nc.vector.tensor_tensor(qt[:, :, :], total[:, :, :], tmp[:, :, :], ALU.mult).then_inc(zc_ok, 1)
                dve.wait_ge(mom_ok, 2)
                for i in range(2):
                    nc.vector.tensor_scalar(m_row[:, 2 * i, :], bank[2 + 2 * i][0:1, 0:D], 1.0 / E, None, ALU.mult)
                    nc.vector.tensor_scalar(m_row[:, 2 * i + 1, :], bank[3 + 2 * i][0:1, 0:D], 1.0 / E, None, ALU.mult)
                dve.drain()
                cubes = m_row[:, 0:4, :].rearrange("a (i k) f -> a i k f", k=2)[:, :, 1, :]
                signs = m_row[:, 4:8, :].rearrange("a (i k) f -> a i k f", k=2)[:, :, 1, :]
                sizes = m_row[:, 4:8, :].rearrange("a (i k) f -> a i k f", k=2)[:, :, 0, :]
                nc.vector.scalar_tensor_tensor(sizes, cubes, -1.0, cubes, ALU.mult, ALU.max)
                nc.vector.tensor_scalar(signs, cubes, 0.0, None, ALU.is_gt)
                dve.drain()
                nc.vector.tensor_scalar(cubes, cubes, 0.0, None, ALU.is_lt)
                dve.drain()
                nc.vector.tensor_tensor(signs, signs, cubes, ALU.subtract)
                nc.vector.tensor_scalar(sizes, sizes, 1e-19, None, ALU.max)
                dve.drain().then_inc(root_in, 1)
                dve.wait_ge(root_ok, 1)
                nc.vector.tensor_tensor(cubes, sizes, signs, ALU.mult)
                dve.drain()
                nc.vector.tensor_tensor(m_row[:, 4:8, :], m_row[:, 0:4, :], wmv[:, :, :], ALU.mult)
                dve.drain()
                nc.vector.tensor_reduce(konst[:, :], m_row[:, 4:8, :].rearrange("a k f -> a (k f)"), AX.X, ALU.add)
                dve.drain().then_inc(const_in, 1)
                dve.wait_ge(const_ok, 1)
                nc.vector.tensor_scalar(edge_t[:, :, :], ea2[:, :, :, 0], edge_w[:, 0:1], bank[6][:, 0:1], ALU.mult, ALU.add)
                dve.drain()
                nc.vector.scalar_tensor_tensor(edge_c[:, :, :], ea2[:, :, :, 1], edge_w[:, 1:2], edge_t[:, :, :], ALU.mult, ALU.add)

            @block.scalar
            def _(act):
                act.wait_ge(root_in, 1)
                squares = m_row[:, 0:4, :].rearrange("a (i k) f -> a i k f", k=2)[:, :, 0, :]
                sizes = m_row[:, 4:8, :].rearrange("a (i k) f -> a i k f", k=2)[:, :, 0, :]
                nc.scalar.activation(squares, squares, ACT.Sqrt)
                nc.scalar.activation(sizes, sizes, ACT.Ln)
                act.drain()
                nc.scalar.activation(sizes, sizes, ACT.Exp, scale=1.0 / 3.0)
                act.drain().then_inc(root_ok, 1)

        attention("l3", att_tab[1], D + 4, True)
        read_back(D + 4)

        def l3_before(dve, aux_in, aux_ok):
            for k in range(2):
                nc.vector.tensor_tensor(total[:, :, :], bc(rows[:, :, D + 2 + k], 2, D), bc(e2n_rep[:, k, :], 1, NT), ALU.mult)
                dve.drain()
                nc.vector.tensor_tensor(rows[:, :, 0:D], rows[:, :, 0:D], total[:, :, :], ALU.add)
                dve.drain()
            normalise(dve, D)
            nc.vector.tensor_tensor(xrow[:, :, :], xrow[:, :, :], tmp[:, :, :], ALU.add)

        layernorm("l3", l3_before, lambda dve: None)
        stored = sem("out_stored")
        with nc.Block() as block:
            @block.sync
            def _(sp):
                sp.dma_start(out[0:(NT - 1) * P, :].rearrange(by_tile, p=P), xrow[:, 0:NT - 1, :]).then_inc(stored, 16)
                sp.dma_start(out[(NT - 1) * P:N, :], xrow[0:NL, NT - 1, :]).then_inc(stored, 16)
                sp.wait_ge(stored, 32)


_INS = ["x", "src", "dst", "edge_attr_2", "edge_attr_64", "L0_gnn_Wq", "L0_gnn_bq", "L0_gnn_Wk", "L0_gnn_bk",
        "L0_gnn_We", "L0_gnn_be", "L0_gnn_Wv", "L0_gnn_bv", "L2_gnn_attn_w", "L3_gnn_W_fc", "L3_gnn_W_attn",
        "L3_gnn_W_edge", "L3_gnn_W_e2n", "L3_gnn_W_m1", "L3_gnn_W_m2"]


def kernel(**inputs):
    import concourse.bacc as bacc
    from concourse.bass_utils import run_bass_kernel_spmd

    nc = bacc.Bacc("TRN2", target_bir_lowering=False, num_devices=1)
    arrays, args = {}, []
    for name in _INS:
        a = np.ascontiguousarray(inputs[name])
        arrays[f"in_{name}"] = a
        args.append(nc.dram_tensor(f"in_{name}", a.shape, mybir.dt.from_np(a.dtype), kind="ExternalInput").ap())
    out = nc.dram_tensor("out_0", (N, D), fp32, kind="ExternalOutput").ap()
    build(nc, *args, out)
    return run_bass_kernel_spmd(nc, [arrays], core_ids=[0]).results[0]["out_0"]
```

```python
import numpy as np
import concourse.bass as bass
from concourse import mybir
from contextlib import ExitStack, nullcontext

fp32, i32, u8 = mybir.dt.float32, mybir.dt.int32, mybir.dt.uint8
bf16, fp16, fp8 = mybir.dt.bfloat16, mybir.dt.float16, mybir.dt.float8e4
ALU, ACT, AX = mybir.AluOpType, mybir.ActivationFunctionType, mybir.AxisListType

P = 128
N, D, E = 3125, 64, 100000
H, DH = 4, 16
NT = -(-N // P)
NP = NT * P
NL = N - (NT - 1) * P
C = 8
ST = P * C
G = -(-E // ST)
PL = (E - (G - 1) * ST) // C
W = 64
TB = -(-(G * C) // P)
TE = E // P
GT = 2
GG = C // GT
WC = 14
KC = NT * WC
DIV = -(-(1 << 16) // WC)
RS = 4
NS = 2
IT = G // NS
BF = 3
NONE = 1.0e6
FAR = -1.0e30
LOW = -1.0e20
EPS = 1e-5
RT = 7
KW = 5 * P
NK = NP // KW
MT = 4
assert G % NS == 0 and (E - (G - 1) * ST) % C == 0


def build(nc, x, src, dst, edge_attr_2, edge_attr_64, Wq, bq, Wk, bk, We, be, Wv, bv,
          attn_w, W_fc, W_attn, W_edge, W_e2n, W_m1, W_m2, out):
    ctx = ExitStack()
    with ctx:
        def sb(name, shape, dt=fp32):
            return ctx.enter_context(nc.sbuf_tensor(name, shape, dt))

        def sem(name):
            return ctx.enter_context(nc.semaphore(name))

        def dram(name, shape):
            return nc.dram_tensor(name, shape, fp32, kind="Internal").ap()

        def bc(ap, axis, n):
            ap = ap.unsqueeze(axis)
            shape = list(ap.shape)
            shape[axis] = n
            return ap.to_broadcast(shape)

        kv_tab = dram("kv_tab", [NP, 2 * D])
        q_tab = dram("q_tab", [NP + W, D])
        hop_tab = [dram(f"hop_tab{i}", [NP, D]) for i in range(3)]
        att_tab = [dram(f"att_tab{i}", [NP, D + 2]) for i in range(2)]

        ident = sb("ident", [P, P])
        ones = sb("ones", [P, P])
        iota = sb("iota", [P, P])
        iota_neg = sb("iota_neg", [P, P])
        dst_rel0 = sb("dst_rel0", [P, G, C])
        dst_rel = sb("dst_rel", [P, G, C])
        edge_scratch = sb("edge_scratch", [P, G, C])
        base0 = sb("base0", [1, G, 8])
        base = sb("base", [1, G, 8])
        base_i = sb("base_i", [1, G, 8], i32)
        sweeps_f = sb("sweeps_f", [1, 4])
        sweeps_i = sb("sweeps_i", [1, 8], i32)
        flag_i = sb("flag_i", [1, 4], i32)
        xrow = sb("xrow", [P, NT, D])
        acc = sb("acc", [P, NP + W])
        xT = acc
        shared = sb("shared", [P, NT * (4 * D + 4)])

        def carve(*fields, shared=shared):
            at, views = 0, []
            for shape in fields:
                size = int(np.prod(shape))
                names = "abcd"[:len(shape)]
                view = shared[:, at:at + size]
                if len(shape) > 1:
                    view = view.rearrange(f"p ({' '.join(names)}) -> p {' '.join(names)}", **dict(zip(names, shape)))
                views.append(view)
                at += size
            assert at <= shared.shape[1]
            return views

        rows, tmp, total, qt = carve((NT, D + 4), (NT, D), (NT, D), (NT, D))
        kv, ea = carve((RS, C, 2 * D), (RS, C * D))
        stat = sb("stat", [P, 4, NT])
        dis = sb("dis", [P, NT])
        in_deg = sb("in_deg", [P, NT])
        out_deg = sb("out_deg", [P, NT])
        wrow = sb("wrow", [D, 5, D])
        webd = sb("webd", [P, P])
        wcat = sb("wcat", [D + 1, 3 * D])
        idx = sb("idx", [P, RS, C], i32)
        g_edge = sb("g_edge", [P, RS, C, D + 4])
        hot = sb("hot", [P, C, W])
        be_row = sb("be_row", [BF, D])
        attc = sb("attc", [D, 2])
        attrep = sb("attrep", [D, P])
        blk = sb("blk", [D, 6])
        w_e = sb("w_e", [2, 1])
        wedge = sb("wedge", [2, 2])
        we2n = sb("we2n", [D, 2])
        wm = sb("wm", [D, 2, D])
        wfcT = sb("wfcT", [D, D + 1])
        small = sb("small", [P, 32])

        bits_u8 = sb("bits_u8", [P, NP], u8)
        zeros_b = sb("zeros_b", [P, P], fp16)
        bank = [ctx.enter_context(nc.psum_tensor(f"bank{i}", [P, 512], fp32)) for i in range(8)]

        count = sb("count", [P, NT, NP + 16], u8)
        early = ExitStack()
        ctx.enter_context(early)
        holder = [early]

        def sb(name, shape, dt=fp32):
            return holder[0].enter_context(nc.sbuf_tensor(name, shape, dt))

        score = sb("score", [P, C * H])
        expo = sb("expo", [P, C * H])
        count_i = count[:, :, :].rearrange("p h n -> p (h n)").bitcast(i32)
        tab = count[:, :, :].rearrange("p h n -> p (h n)")[:, 0:NT * 2 * D * 4].bitcast(fp32).rearrange("p (t f) -> p t f", t=NT)
        counting = ExitStack()
        ctx.enter_context(counting)
        holder[0] = counting
        tile_lo = sb("tile_lo", [P, G, C])
        tile_hi = sb("tile_hi", [P, G, C])
        tile_rel0 = sb("tile_rel0", [P, G * GG, GT])
        tile_key = sb("tile_key", [P, G, C])
        tile_rel = sb("tile_rel", [P, G * GG, GT])
        tile_hiw = sb("tile_hiw", [P, G, C])
        key_hot = sb("key_hot", [P, C, KC], fp16)
        lo_dist = sb("lo_dist", [P, C, P], fp16)
        lo_hot = sb("lo_hot", [P, C, P], fp16)
        iota_key = sb("iota_key", [P, KC], fp16)
        starting = ExitStack()
        ctx.enter_context(starting)
        holder[0] = starting
        dst_i = sb("dst_i", [P, G, C], i32)
        lowest = sb("lowest", [P, 4 * P])
        lowest_col = sb("lowest_col", [P, 4])
        lowest_diag = sb("lowest_diag", [P, 4, P])
        group_base = sb("group_base", [P, 4 * P])
        super_base = sb("super_base", [P, G])
        span = sb("span", [P, 4])
        iota_i = sb("iota_i", [P, KC], i32)
        webd_row = sb("webd_row", [P, P])

        s_zero, s_graph, s_x, s_w = sem("zeroed"), sem("graph_loaded"), sem("x_loaded"), sem("w_loaded")
        s_const, s_tail = sem("const"), sem("tail_loaded")
        s_rows, s_tiles, s_wt = sem("edge_rows_ready"), sem("edge_rows_turned"), sem("w_turned")
        s_base, s_basec, s_bdiag, s_brep = sem("low_ready"), sem("low_turned"), sem("diag_ready"), sem("base_spread")
        s_sp, s_spt = sem("span_ready"), sem("span_turned")
        src_r = acc[:, 0:TB * P].bitcast(i32).rearrange("p (k e) -> p k e", k=TB)
        dst_r = acc[:, TB * P:2 * TB * P].bitcast(i32).rearrange("p (k e) -> p k e", k=TB)
        lo_r = acc[:, 2 * TB * P:3 * TB * P].bitcast(i32).rearrange("p (k e) -> p k e", k=TB)
        tab_flat = tab[:, :, :].rearrange("p t f -> p (t f)")
        lo_f, hi_f, dst_f = (tab_flat[:, i * TB * P:(i + 1) * TB * P].rearrange("p (k e) -> p k e", k=TB) for i in range(3))

        with nc.Block() as block:
            @block.gpsimd
            def _(pool):
                nc.gpsimd.memset(ident[:, :], 0.0).then_inc(s_const, 1)
                nc.gpsimd.iota(iota_i[:, :], pattern=[[1, KC]], base=0, channel_multiplier=0).then_inc(s_const, 1)
                pool.wait_ge(s_const, 2)
                nc.gpsimd.affine_select(out=ident[:, :], in_=ident[:, :], compare_op=ALU.not_equal, fill=1.0,
                                        base=0, pattern=[[-1, P]], channel_multiplier=1).then_inc(s_const, 1)
                nc.gpsimd.memset(count_i[:, NT * 2 * D:], 0)

            @block.sync
            def _(sp):
                full = (G - 1) * ST
                head = (TB - 1) * P * P
                sp.dma_start(dst_r[:, 0:TB - 1, :], dst[0:head].rearrange("(k r e) -> r k e", r=P, e=P)).then_inc(s_graph, 16)
                sp.dma_start(src_r[:, 0:TB - 1, :], src[0:head].rearrange("(k r e) -> r k e", r=P, e=P)).then_inc(s_graph, 16)
                sp.dma_start(dst_i[:, 0:G - 1, :], dst[0:full].rearrange("(g p c) -> p g c", p=P, c=C)).then_inc(s_graph, 16)
                sp.wait_ge(s_zero, 1)
                whole = TE - (TB - 1) * P
                for into, of in ((dst_r, dst), (src_r, src)):
                    sp.dma_start(into[0:whole, TB - 1, :], of[head:TE * P].rearrange("(r e) -> r e", e=P)).then_inc(s_tail, 16)
                    sp.dma_start(into[whole:whole + 1, TB - 1, 0:E - TE * P], of[TE * P:E].rearrange("(a e) -> a e", a=1)).then_inc(s_tail, 16)
                sp.dma_start(webd_row[0:D, 0:D], We).then_inc(s_tail, 16)
                sp.dma_start(webd_row[D:P, D:P], We).then_inc(s_tail, 16)
                sp.dma_start(xrow[0:NL, NT - 1, :], x[(NT - 1) * P:N, :]).then_inc(s_tail, 16)
                sp.dma_start(dst_i[0:PL, G - 1, :], dst[full:E].rearrange("(p c) -> p c", c=C)).then_inc(s_tail, 16)

            @block.scalar
            def _(act):
                act.dma_start(xrow[:, 0:NT - 1, :], x[0:(NT - 1) * P, :].rearrange("(t p) f -> p t f", p=P)).then_inc(s_x, 16)
                act.dma_start(wrow[:, 0, :], Wk).then_inc(s_w, 16)
                act.dma_start(wrow[:, 1, :], Wv).then_inc(s_w, 16)
                act.dma_start(wrow[:, 2, :], Wq).then_inc(s_w, 16)
                act.dma_start(wrow[:, 3, :], W_fc).then_inc(s_w, 16)
                for i, b in enumerate((bk, bv, bq)):
                    act.dma_start(wcat[D:D + 1, i * D:(i + 1) * D], b.rearrange("(a n) -> a n", a=1)).then_inc(s_w, 16)
                act.dma_start(be_row[:, :], be.rearrange("(a n) -> a n", a=1).to_broadcast([BF, D])).then_inc(s_w, 16)
                act.dma_start(attc[:, :], attn_w.rearrange("(k p) -> p k", p=D), allow_slow_non_contiguous=True).then_inc(s_w, 16)
                act.dma_start(blk[:, :], W_attn[0, 0:6 * D].rearrange("(k p) -> p k", p=D), allow_slow_non_contiguous=True).then_inc(s_w, 16)
                act.dma_start(w_e[:, :], W_attn[0, 6 * D:6 * D + 2].rearrange("(p a) -> p a", a=1), allow_slow_non_contiguous=True).then_inc(s_w, 16)
                act.dma_start(wedge[:, :], W_edge).then_inc(s_w, 16)
                act.dma_start(we2n[:, :], W_e2n).then_inc(s_w, 16)
                act.dma_start(wm[:, 0, :], W_m1).then_inc(s_w, 16)
                act.dma_start(wm[:, 1, :], W_m2).then_inc(s_w, 16)
                act.wait_ge(s_wt, 1)
                nc.scalar.activation(wcat[0:D, :], bank[3][0:D, 0:3 * D], ACT.Copy)
                nc.scalar.activation(wfcT[:, 0:D], bank[3][0:D, 3 * D:4 * D], ACT.Copy)
                nc.scalar.activation(webd[:, :], bank[4][:, 0:P], ACT.Copy)
                act.wait_ge(s_x, 16)

            @block.vector
            def _(dve):
                nc.vector.memset(dst_i[:, G - 1, :], int(NONE))
                nc.vector.memset(dst_r[:, TB - 1, :], int(NONE))
                nc.vector.memset(src_r[:, TB - 1, :], int(NONE))
                nc.vector.memset(webd_row[:, :], 0.0)
                nc.vector.memset(xrow[:, NT - 1, :], 0.0)
                dve.drain().then_inc(s_zero, 1)
                nc.vector.memset(ones[:, :], 1.0)
                nc.vector.memset(zeros_b[:, :], 0.0)
                nc.vector.memset(span[:, :], 0.0)
                nc.vector.memset(base0[:, :, :], 0.0)
                nc.vector.memset(lowest[:, :], NONE)
                dve.wait_ge(s_const, 3)
                nc.vector.tensor_copy(iota[:, :], iota_i[:, 0:P])
                nc.vector.tensor_scalar(iota_neg[:, :], iota_i[:, 0:P], -1.0, None, ALU.mult)
                nc.vector.tensor_copy(iota_key[:, :], iota_i[:, :])
                dve.wait_ge(s_graph, 48)
                dve.wait_ge(s_tail, 16 * 8)
                nc.vector.tensor_scalar(lo_r, src_r, P - 1, None, ALU.bitwise_and)
                nc.vector.tensor_copy(dst_f, dst_r)
                nc.vector.tensor_copy(dst_rel0[:, :, :], dst_i[:, :, :])
                dve.drain()
                nc.vector.tensor_copy(lo_f, lo_r)
                dve.drain()
                nc.vector.tensor_scalar(lo_r, src_r, 7, None, ALU.arith_shift_right)
                dve.drain()
                nc.vector.tensor_copy(hi_f, lo_r)
                dve.drain().then_inc(s_rows, 1)
                dve.wait_ge(s_tiles, 1)
                rest = G * C - 4 * P
                for into, (b0, b1) in ((tile_lo, (0, 1)), (tile_hi, (2, 5)), (tile_rel0, (6, 7))):
                    flat = into[:, :, :].rearrange("p a b -> p (a b)")
                    nc.vector.tensor_copy(flat[:, 0:4 * P], bank[b0][:, :])
                    nc.vector.tensor_copy(flat[:, 4 * P:G * C], bank[b1][:, 0:rest])
                dve.drain()
                nc.vector.tensor_reduce(lowest[:, 0:G * GG], tile_rel0[:, :, :], AX.X, ALU.min)
                dve.drain().then_inc(s_base, 1)
                dve.wait_ge(s_basec, 1)
                nc.vector.tensor_reduce(lowest_col[:, :], bank[0][:, :].rearrange("p (k e) -> p k e", k=4), AX.X, ALU.min)
                dve.drain()
                for k in range(4):
                    nc.vector.tensor_scalar(lowest_diag[:, k, :], ident[:, :], lowest_col[:, k:k + 1], None, ALU.mult)
                dve.drain().then_inc(s_bdiag, 1)
                dve.wait_ge(s_brep, 1)
                nc.vector.tensor_copy(group_base[:, :], bank[1][:, :])
                dve.drain()
                groups = group_base[:, 0:G * GG]
                nc.vector.tensor_reduce(super_base[:, :], groups.rearrange("p (g q) -> p g q", q=GG), AX.X, ALU.min)
                nc.vector.tensor_tensor(tile_rel0[:, :, :], tile_rel0[:, :, :], bc(groups, 2, GT), ALU.subtract)
                nc.vector.tensor_copy(base0[:, :, 1:1 + GG], group_base[0:1, 0:G * GG].rearrange("p (g q) -> p g q", q=GG))
                dve.drain()
                nc.vector.tensor_copy(base0[:, :, 0], super_base[0:1, :])
                nc.vector.tensor_tensor(dst_rel0[:, :, :], dst_rel0[:, :, :], bc(super_base[:, :], 2, C), ALU.subtract)
                nc.vector.scalar_tensor_tensor(tile_rel[:, :, :], tile_rel0[:, :, :], NONE / 10, tile_rel0[:, :, :], ALU.is_lt, ALU.mult)
                dve.drain()
                nc.vector.tensor_reduce(span[:, 2:3], dst_rel0[:, 0:G - 1, :], AX.XY, ALU.max)
                nc.vector.tensor_reduce(span[0:PL, 3:4], dst_rel0[0:PL, G - 1, :], AX.X, ALU.max)
                nc.vector.tensor_reduce(span[:, 1:2], tile_rel[:, :, :], AX.XY, ALU.max)
                dve.drain()
                nc.vector.tensor_reduce(span[:, 0:1], span[:, 2:4], AX.X, ALU.max)
                dve.drain().then_inc(s_sp, 1)
                dve.wait_ge(s_spt, 1)
                nc.vector.tensor_reduce(sweeps_f[:, 0:2], bank[2][0:1, 0:2 * P].rearrange("a (k e) -> a k e", k=2), AX.X, ALU.max)
                dve.drain()
                nc.vector.tensor_scalar(sweeps_f[:, 1:2], sweeps_f[:, 1:2], float(DIV), None, ALU.mult)
                dve.drain()
                nc.vector.tensor_copy(sweeps_i[:, 2:4], sweeps_f[:, 0:2])
                dve.drain()
                nc.vector.tensor_scalar(sweeps_i[:, 4:5], sweeps_i[:, 2:3], W.bit_length() - 1, None, ALU.arith_shift_right)
                nc.vector.tensor_scalar(sweeps_i[:, 5:6], sweeps_i[:, 3:4], 16, None, ALU.arith_shift_right)
                dve.drain()
                nc.vector.tensor_copy(sweeps_f[:, 0:2], sweeps_i[:, 4:6])
                dve.drain()
                nc.vector.tensor_tensor(sweeps_f[:, 2:3], sweeps_f[:, 0:1], sweeps_f[:, 1:2], ALU.max)
                dve.drain()
                nc.vector.tensor_scalar(sweeps_i[:, 0:1], sweeps_f[:, 0:1], 1.0, None, ALU.add)
                nc.vector.tensor_scalar(sweeps_i[:, 1:2], sweeps_f[:, 2:3], 1.0, None, ALU.add)
                nc.vector.tensor_scalar(tile_hiw[:, :, :], tile_hi[:, :, :], float(WC), 1.0, ALU.mult, ALU.add)
                nc.vector.memset(xT[D:D + 1, 0:NP], 1.0)

            @block.tensor
            def _(pe):
                pe.wait_ge(s_const, 3)
                pe.wait_ge(s_rows, 1)
                for rows_of, (b0, b1) in ((lo_f, (0, 1)), (hi_f, (2, 5)), (dst_f, (6, 7))):
                    for k in range(TB):
                        last = nc.tensor.transpose(bank[b0 if k < 4 else b1][:, k % 4 * P:(k % 4 + 1) * P], rows_of[:, k, :], ident[:, :])
                last.then_inc(s_tiles, 1)
                pe.wait_ge(s_w, 16 * 15)
                pe.wait_ge(s_tail, 16 * 8)
                for i in range(4):
                    nc.tensor.transpose(bank[3][0:D, i * D:(i + 1) * D], wrow[:, i, :], ident[0:D, 0:D])
                nc.tensor.transpose(bank[4][:, 0:P], webd_row[:, :], ident[:, :]).then_inc(s_wt, 1)
                pe.wait_ge(s_base, 1)
                for k in range(4):
                    last = nc.tensor.transpose(bank[0][:, k * P:(k + 1) * P], lowest[:, k * P:(k + 1) * P], ident[:, :])
                last.then_inc(s_basec, 1)
                pe.wait_ge(s_bdiag, 1)
                for k in range(4):
                    last = nc.tensor.matmul(bank[1][:, k * P:(k + 1) * P], ones[:, :], lowest_diag[:, k, :], start=True, stop=True)
                last.then_inc(s_brep, 1)
                pe.wait_ge(s_sp, 1)
                nc.tensor.transpose(bank[2][0:1, 0:P], span[:, 0:1], ident[:, :])
                nc.tensor.transpose(bank[2][0:1, P:2 * P], span[:, 1:2], ident[:, :]).then_inc(s_spt, 1)

        starting.close()
        holder[0] = counting

        p_sems = [sem(f"p_{n}") for n in ("turned", "copied", "done", "taken", "row", "row_out")]
        projected = [0, 0, 0]

        def project(tag, cols, K, rhs, evacuate, row_rep=None):
            turned, copied, done, taken, arow, arow_out = p_sems
            groups = [range(t, min(t + MT, NT)) for t in range(0, NT, MT)]
            per = max(1, min(2, 512 // cols))
            mms = [range(t, min(t + per, NT)) for t in range(0, NT, per)]
            chunks = [(c, min(c + 512, NP)) for c in range(0, NP, 512)]
            T, M, A = projected
            projected[:] = [T + len(groups), M + len(mms), A + (len(chunks) if row_rep is not None else 0)]
            with nc.Block() as block:
                @block.tensor
                def _(pe):
                    for k, ts in enumerate(groups):
                        if k >= 2:
                            pe.wait_ge(copied, T + k - 1)
                        for j, t in enumerate(ts):
                            last = nc.tensor.transpose(bank[k % 2][0:D, j * P:(j + 1) * P], xrow[:, t, :], ident[:, :])
                        last.then_inc(turned, 1)
                    pe.wait_ge(copied, T + len(groups))
                    for k, ts in enumerate(mms):
                        if k >= 2:
                            pe.wait_ge(taken, M + k - 1)
                        for j, t in enumerate(ts):
                            last = nc.tensor.matmul(bank[2 + k % 2][:, j * cols:(j + 1) * cols], xT[0:K, t * P:(t + 1) * P],
                                                    rhs, start=True, stop=True)
                        last.then_inc(done, 1)
                    if row_rep is not None:
                        for k, (a, b) in enumerate(chunks):
                            if k >= 2:
                                pe.wait_ge(arow_out, A + k - 1)
                            nc.tensor.matmul(bank[4 + k % 2][:, 0:b - a], row_rep, xT[0:D, a:b], start=True, stop=True).then_inc(arow, 1)

                @block.scalar
                def _(act):
                    for k, ts in enumerate(groups):
                        act.wait_ge(turned, T + k + 1)
                        nc.scalar.activation(xT[0:D, ts[0] * P:(ts[-1] + 1) * P], bank[k % 2][0:D, 0:len(ts) * P], ACT.Copy).then_inc(copied, 1)
                    if row_rep is not None:
                        for k, (a, b) in enumerate(chunks):
                            act.wait_ge(arow, A + k + 1)
                            nc.scalar.activation(ad_row[:, a:b], bank[4 + k % 2][:, 0:b - a], ACT.Copy).then_inc(arow_out, 1)

                @block.vector
                def _(dve):
                    for k, ts in enumerate(mms):
                        dve.wait_ge(done, M + k + 1)
                        ps = bank[2 + k % 2][:, 0:len(ts) * cols].rearrange("p (t n) -> p t n", n=cols)
                        evacuate(ts[0], ts[-1] + 1, ps).then_inc(taken, 1)
                    if row_rep is not None:
                        nc.vector.memset(ad_row[:, NP:NP + W], 0.0)

        def store_table(tag, pairs, way=lambda eng: nullcontext()):
            stored = sem(f"{tag}_stored")
            with nc.Block() as block:
                @block.sync
                def _(sp):
                    with way(sp):
                        for t, view in pairs:
                            sp.dma_start(t, view).then_inc(stored, 16)
                        sp.wait_ge(stored, 16 * len(pairs))

        def take_l0(a, b, ps):
            nc.vector.tensor_scalar(tab[:, a:b, 0:D], ps[:, :, 0:D], DH ** -0.5, None, ALU.mult)
            nc.vector.tensor_copy(tab[:, a:b, D:2 * D], ps[:, :, D:2 * D])
            return nc.vector.tensor_copy(qt[:, a:b, :], ps[:, :, 2 * D:3 * D])

        project("l0", 3 * D, D + 1, wcat[:, :], take_l0)
        with nc.Block() as block:
            @block.vector
            def _(dve):
                nc.vector.memset(tmp[0:W, 0, :], 0.0)
        by_tile = "(t p) f -> p t f"
        store_table("l0", [(kv_tab.rearrange(by_tile, p=P), tab[:, :, :]),
                           (q_tab[0:NP, :].rearrange(by_tile, p=P), qt[:, :, :]),
                           (q_tab[NP:NP + W, :], tmp[0:W, 0, :])])

        def start_sweep(dve, ready, counting=False):
            nc.vector.tensor_scalar(dst_rel[:, :, :], dst_rel[:, :, :], float(-W), None, ALU.add)
            nc.vector.tensor_scalar(base[:, :, 0:1], base[:, :, 0:1], float(W), float(NP), ALU.add, ALU.min)
            if counting:
                nc.vector.tensor_scalar(base[:, :, 1:1 + GG], base[:, :, 1:1 + GG], float(WC), float(NP), ALU.add, ALU.min)
                nc.vector.tensor_scalar(tile_rel[:, :, :], tile_rel[:, :, :], float(-WC), None, ALU.add)
                dve.drain()
                rel = tile_rel[:, :, :].rearrange("p a b -> p (a b)")
                key, far_key = (t[:, :, :].rearrange("p a b -> p (a b)") for t in (tile_key, edge_scratch))
                nc.vector.tensor_tensor(key, rel, tile_hiw[:, :, :].rearrange("p a b -> p (a b)"), ALU.add)
                nc.vector.tensor_scalar(far_key, rel, 0.0, None, ALU.is_ge)
                dve.drain()
                nc.vector.tensor_tensor(key, key, far_key, ALU.mult)
                dve.drain()
                nc.vector.scalar_tensor_tensor(far_key, rel, float(WC), key, ALU.is_lt, ALU.mult)
                dve.drain()
                nc.vector.tensor_scalar(key, far_key, -1.0, None, ALU.add)
            dve.drain()
            nc.vector.tensor_copy(base_i[:, :, :], base[:, :, :])
            dve.drain().then_inc(ready, 1)

        def reset_windows(dve, counting=False):
            nc.vector.tensor_scalar(dst_rel[:, :, :], dst_rel0[:, :, :], float(W), None, ALU.add)
            nc.vector.tensor_scalar(base[:, :, :], base0[:, :, :], float(-W), None, ALU.add)
            if counting:
                nc.vector.tensor_scalar(tile_rel[:, :, :], tile_rel0[:, :, :], float(WC), None, ALU.add)
                dve.drain()
                nc.vector.tensor_scalar(base[:, :, 1:1 + GG], base0[:, :, 1:1 + GG], float(-WC), None, ALU.add)
                nc.vector.memset(base[:, :, 1 + GG:8], 0.0)
            else:
                dve.drain()
                nc.vector.memset(base[:, :, 1:8], 0.0)
            nc.vector.memset(acc[:, :], 0.0)
            dve.drain()

        def forget_rows(pool, rows_in, slot_free, cleared, done):
            pool.wait_ge(slot_free, done)
            pass_on(pool)
            for s, one in enumerate(rows_in):
                nc.gpsimd.inc_swdge_sem([one], [len(range(s, G, len(rows_in))) * C * 16], mode="sub")
            pool.sem_inc(cleared, 1)

        def sweeps(eng, which=0):
            return eng.value_load(sweeps_i[0:1, which:which + 1], min_val=1, max_val=NP // WC + 1)

        def spans(eng, g):
            return nc.values_load_multi_w_load_instructions(
                base_i[0:1, bass.ds(g, 1), 0:1].rearrange("a g k -> a (g k)"), engines=[eng.engine], min_val=0, max_val=NP,
                skip_runtime_bounds_check_because="start_sweep keeps them within 0 and NP")[1][0]

        passed = sem("passed")

        def pass_on(eng):
            eng.sem_inc(passed, 1)

        ea_main = edge_attr_64[0:(G - 1) * ST, :].rearrange("(g p c) f -> g p (c f)", p=P, c=C)
        ea_last = edge_attr_64[(G - 1) * ST:E, :].rearrange("(p c) f -> p (c f)", c=C)

        src_main = src[0:(G - 1) * ST].rearrange("(g p c) -> g p c", p=P, c=C)
        src_last = src[(G - 1) * ST:E].rearrange("(p c) -> p c", c=C)

        def load_idx(sp, g, s, last, into):
            if last:
                sp.dma_start(idx[0:PL, s, :], src_last).then_inc(into, 16)
            else:
                sp.dma_start(idx[:, s, :], src_main[bass.ds(g, 1), :, :].rearrange("g p c -> (g p) c")).then_inc(into, 16)

        gating = ExitStack()
        ctx.enter_context(gating)
        holder[0] = gating
        hotT = sb("hotT", [P, C // 2, P])
        qwin = sb("qwin", [P, RS, 2, D])
        be_parts = sb("be_parts", [BF, C, D], bf16)
        be_rest = sb("be_rest", [BF, 2, D])
        be_part = sb("be_part", [BF, BF, D], bf16)
        ones_b = sb("ones_b", [BF, P], bf16)
        eaT = sb("eaT", [P, C * D])
        prod = sb("prod", [P, C * D])
        msg = sb("msg", [P, C, D + 1])
        hots = sb("hots", [P, 2, C, W])

        def pipelined(eng, front, step):
            front(0, 0, 1)
            with eng.Fori(0, G // RS) as it:
                for s in range(RS):
                    step(it * RS + s, s, it + 1, (it * RS + s + 1, (s + 1) % RS, it + 1 + (s + 1) // RS))
            for g in range(G - G % RS, G):
                step(g, g % RS, g // RS + 1, (g + 1, (g + 1) % RS, (g + 1) // RS + 1) if g + 1 < G else None)

        def each(eng, step):
            with eng.Fori(0, G // RS) as it:
                for s in range(RS):
                    step(it * RS + s, s, it + 1)
            for g in range(G - G % RS, G):
                step(g, g % RS, g // RS + 1)

        def uses(s):
            return len(range(s, G, RS))

        begun = sem("a_begun")
        slot_free, idx_in = sem("a_slot_free"), [sem(f"a_idx{s}") for s in range(RS)]
        ea_in, kv_in = [sem(f"a_ea{s}") for s in range(RS)], [sem(f"a_kv{s}") for s in range(RS)]
        hot_ok, ea_t, ea_ts, hot_t, hot_ts = sem("a_hot"), sem("a_eaT"), sem("a_eaTs"), sem("a_hotT"), sem("a_hotTs")
        ee_ok, qd_ok, sc_ok, ex_ok, msg_ok, sum_ok = (sem("a_ee"), sem("a_qd"), sem("a_score"), sem("a_exp"), sem("a_msg"), sem("a_sum"))
        cleared, q_in = sem("a_cleared"), sem("a_queries")
        key_ok, lo_ok, count_ok, bank_free = sem("a_key"), sem("a_lo"), sem("a_count"), sem("a_count_added")
        with nc.Block() as block:
            @block.sync
            def _(sp):
                nj = sweeps(sp, 1)
                with sp.Fori(0, nj) as j:
                    sp.wait_ge(slot_free, j * G + RS)
                    pass_on(sp)

                    def load(g, s, m):
                        last = isinstance(g, int) and g == G - 1
                        sp.wait_ge(slot_free, j * G + g + 1)
                        pass_on(sp)
                        load_idx(sp, g, s, last, idx_in[s])
                        if last:
                            sp.dma_start(ea[0:PL, s, :], ea_last).then_inc(ea_in[s], 16)
                        else:
                            at = bass.ds(g, 1)
                            sp.dma_start(ea[:, s, :], ea_main[at, :, :].rearrange("g p n -> (g p) n")).then_inc(ea_in[s], 16)

                    each(sp, load)

            @block.gpsimd
            def _(pool):
                nj = sweeps(pool, 1)
                with pool.Fori(0, nj) as j:
                    def gather(g, s, m):
                        pool.wait_ge(idx_in[s], (j * uses(s) + m) * 16)
                        pass_on(pool)
                        for c in range(C):
                            nc.gpsimd.indirect_dma_start(
                                kv[:, s, c, :], None, kv_tab, bass.IndirectOffsetOnAxis(ap=idx[:, s, c:c + 1], axis=0)
                            ).then_inc(kv_in[s], 16)

                    each(pool, gather)
                    forget_rows(pool, kv_in, slot_free, cleared, (j + 1) * G + RS)

            @block.vector
            def _(dve):
                nj = sweeps(dve, 1)
                dve.sem_inc(slot_free, RS)
                dve.sem_inc(cleared, 1)
                nc.vector.memset(count_i[:, 0:NT * 2 * D], 0)
                nc.vector.memset(msg[:, :, D:D + 1], 1.0)
                nc.vector.memset(qwin[:, :, :, :], 0.0)
                nc.vector.memset(ones_b[:, :], 1.0)
                rest = be_row[:, :]
                for k in range(BF):
                    nc.vector.tensor_copy(be_part[:, k, :], rest)
                    dve.drain()
                    if k + 1 < BF:
                        nc.vector.tensor_tensor(be_rest[:, k, :], rest, be_part[:, k, :], ALU.subtract)
                        dve.drain()
                        rest = be_rest[:, k, :]
                nc.vector.tensor_scalar(be_rest[:, 0, :], be_part[:, 0, :], ident[0:BF, 0:1], None, ALU.mult)
                dve.drain()
                for k in range(1, BF):
                    nc.vector.scalar_tensor_tensor(be_rest[:, k % 2, :], be_part[:, k, :], ident[0:BF, k:k + 1], be_rest[:, (k - 1) % 2, :], ALU.mult, ALU.add)
                    dve.drain()
                nc.vector.tensor_copy(be_parts[:, :, :], bc(be_rest[:, (BF - 1) % 2, :], 1, C))
                reset_windows(dve, True)
                dve.sem_inc(bank_free, 2)
                with dve.Fori(0, nj) as j:
                    dve.wait_ge(cleared, j + 1)
                    pass_on(dve)
                    start_sweep(dve, begun, True)

                    def node_hots(g, s, m):
                        nc.vector.tensor_tensor(hots[:, s % 2, :, :], bc(dst_rel[:, bass.ds(g, 1), :].rearrange("p g c -> p (g c)"), 2, W),
                                                bc(iota[:, 0:W], 1, C), ALU.is_equal).then_inc(hot_ok, 1)

                    def key_hots(g, s, m):
                        keys = tile_key[:, bass.ds(g, 1), :].rearrange("p g c -> p (g c)")
                        for c in range(C):
                            last = nc.vector.tensor_scalar(key_hot[:, c, :], iota_key[:, :], keys[:, c:c + 1], None, ALU.is_equal)
                        last.then_inc(key_ok, 1)

                    def front(g, s, m):
                        node_hots(g, s, m)
                        key_hots(g, s, m)

                    def step(g, s, m, after):
                        n = j * G + g + 1

                        def add_counts(q):
                            at = count[:, :, bass.ds(group_at[q], WC)]
                            dve.wait_ge(count_ok, j * (G * GG) + g * GG + q + 1)
                            nc.vector.tensor_tensor(at, at, bank[6 + q % 2][:, 0:KC].rearrange("p (h w) -> p h w", w=WC),
                                                    ALU.add).then_inc(bank_free, 1)

                        kvs = kv[:, s, :, :]
                        dve.wait_ge(kv_in[s], m * (16 * C))
                        dve.wait_ge(ee_ok, n)
                        nc.vector.tensor_tensor(prod[:, :].rearrange("p (c f) -> p c f", c=C),
                                                bank[3][:, :].rearrange("p (c f) -> p c f", c=C), kvs[:, :, 0:D], ALU.mult)
                        b, *group_at = nc.values_load_multi_w_load_instructions(
                            base_i[0:1, bass.ds(g, 1), 0:1 + GG].rearrange("a g k -> a (g k)"), engines=[mybir.EngineType.DVE],
                            min_val=0, max_val=NP,
                            skip_runtime_bounds_check_because="start_sweep keeps them within 0 and NP")[1]
                        dve.drain()
                        dve.wait_ge(qd_ok, n)
                        nc.vector.tensor_tensor(prod[:, :], prod[:, :], bank[4][:, :], ALU.mult)
                        dve.drain()
                        nc.vector.tensor_reduce(score[:, :], prod[:, :].rearrange("p (a d) -> p a d", d=DH), AX.X, ALU.add)
                        dve.drain()
                        nc.vector.tensor_scalar(score[:, :], score[:, :], -5.0, 5.0, ALU.max, ALU.min).then_inc(sc_ok, 1)
                        add_counts(0)
                        if after:
                            node_hots(*after)
                        dve.drain()
                        add_counts(1)
                        dve.wait_ge(ex_ok, n)
                        nc.vector.tensor_tensor(msg[:, :, 0:D].rearrange("p c (h d) -> p c h d", h=H),
                                                kvs[:, :, D:2 * D].rearrange("p c (h d) -> p c h d", h=H),
                                                bc(expo[:, :].rearrange("p (c h) -> p c h", h=H), 3, DH), ALU.mult).then_inc(msg_ok, 1)
                        for q in range(2, GG):
                            dve.drain()
                            add_counts(q)
                        if after:
                            key_hots(*after)
                        dve.wait_ge(sum_ok, n)
                        nc.vector.tensor_tensor(acc[0:D + 1, bass.ds(b, W)], acc[0:D + 1, bass.ds(b, W)], bank[5][0:D + 1, 0:W], ALU.add).then_inc(slot_free, 1)
                        dve.drain()

                    pipelined(dve, front, step)

            @block.scalar
            def _(act):
                nj = sweeps(act, 1)
                with act.Fori(0, nj) as j:
                    act.wait_ge(begun, j + 1)
                    pass_on(act)

                    def front(g, s, m):
                        n = j * G + g + 1
                        act.wait_ge(slot_free, n)
                        pass_on(act)
                        b = spans(act, g)
                        for i in range(2):
                            act.dma_start(qwin[i * W:(i + 1) * W, s, i, :], q_tab[bass.ds(b, W), :]).then_inc(q_in, 16)
                        act.wait_ge(ea_t, n)
                        nc.scalar.activation(eaT[:, :], bank[0][:, :], ACT.Copy).then_inc(ea_ts, 1)
                        act.wait_ge(hot_t, n)
                        nc.scalar.activation(hotT[:, :, :].rearrange("p c e -> p (c e)"), bank[1][:, :], ACT.Copy).then_inc(hot_ts, 1)
                        los = tile_lo[:, bass.ds(g, 1), :].rearrange("p g c -> p (g c)")
                        for c in range(C):
                            nc.scalar.activation(lo_dist[:, c, :], iota_neg[:, :], ACT.Abs, bias=los[:, c:c + 1])
                        act.drain()
                        if not (isinstance(g, int) and g == 0):
                            act.wait_ge(count_ok, j * (G * GG) + g * GG)
                            pass_on(act)
                        nc.scalar.activation(lo_hot[:, :, :], lo_dist[:, :, :], ACT.Relu, bias=1.0, scale=-1.0).then_inc(lo_ok, 1)

                    def step(g, s, m, after):
                        act.wait_ge(sc_ok, j * G + g + 1)
                        nc.scalar.activation(expo[:, :], score[:, :], ACT.Exp).then_inc(ex_ok, 1)
                        if after:
                            front(*after)

                    pipelined(act, front, step)

            @block.tensor
            def _(pe):
                nj = sweeps(pe, 1)
                with pe.Fori(0, nj) as j:
                    def turn_edges(g, s, m):
                        pe.wait_ge(ea_in[s], (j * uses(s) + m) * 16)
                        pass_on(pe)
                        for q in range(4):
                            last = nc.tensor.transpose(bank[0][:, q * P:(q + 1) * P], ea[:, s, q * P:(q + 1) * P], ident[:, :])
                        last.then_inc(ea_t, 1)

                    def turn_hots(g, s, m):
                        pe.wait_ge(hot_ok, j * G + g + 1)
                        pass_on(pe)
                        for c in range(0, C, 2):
                            last = nc.tensor.transpose(bank[1][:, c // 2 * P:(c // 2 + 1) * P],
                                                       hots[:, s % 2, c:c + 2, :].rearrange("p c n -> p (c n)"), ident[:, :])
                        last.then_inc(hot_t, 1)

                    def edge_products(g, s, m):
                        n = j * G + g + 1
                        pe.wait_ge(ea_ts, n)
                        for q in range(4):
                            nc.tensor.matmul(bank[3][:, q * P:(q + 1) * P], eaT[:, q * P:(q + 1) * P], webd[:, :],
                                             start=q == 0, stop=False, skip_group_check=True)
                        last = nc.tensor.matmul(bank[3][:, :], ones_b[:, :], be_parts[:, :, :].rearrange("a c f -> a (c f)"),
                                                start=False, stop=True, skip_group_check=True)
                        last.then_inc(ee_ok, 1)
                        pe.wait_ge(hot_ts, n)
                        pe.wait_ge(q_in, n * 32)
                        for c in range(0, C, 2):
                            last = nc.tensor.matmul(bank[4][:, c * D:(c + 2) * D], hotT[:, c // 2, :],
                                                    qwin[:, s, :, :].rearrange("p a f -> p (a f)"), start=True, stop=True)
                        last.then_inc(qd_ok, 1)

                    def front(g, s, m):
                        turn_edges(g, s, m)
                        turn_hots(g, s, m)
                        edge_products(g, s, m)

                    def step(g, s, m, after):
                        n = j * G + g + 1

                        def count_group(q):
                            pe.wait_ge(bank_free, j * (G * GG) + g * GG + q + 1)
                            pass_on(pe)
                            for i in range(GT):
                                c = GT * q + i
                                last = nc.tensor.matmul(bank[6 + q % 2][:, 0:KC], lo_hot[:, c, :], key_hot[:, c, :], start=i == 0, stop=i == GT - 1)
                            last.then_inc(count_ok, 1)

                        pe.wait_ge(key_ok, n)
                        pe.wait_ge(lo_ok, n)
                        for q in range(2):
                            count_group(q)
                        if after:
                            turn_edges(*after)
                        for q in range(2, GG):
                            count_group(q)
                        if after:
                            turn_hots(*after)
                        pe.wait_ge(msg_ok, n)
                        for c in range(C):
                            last = nc.tensor.matmul(bank[5][0:D + 1, 0:W], msg[:, c, :], hots[:, s % 2, c, :], start=c == 0, stop=c == C - 1)
                        last.then_inc(sum_ok, 1)
                        if after:
                            edge_products(*after)

                    pipelined(pe, front, step)
        gating.close()

        rows_turned = sem("rows_turned")
        read = []

        def read_back(M):
            turned, before = rows_turned, 4 * len(read)
            read.append(M)
            groups = [range(t, min(t + RT, NT)) for t in range(0, NT, RT)]
            with nc.Block() as block:
                @block.tensor
                def _(pe):
                    for k, ts in enumerate(groups):
                        for i, t in enumerate(ts):
                            last = nc.tensor.transpose(bank[k][:, i * M:(i + 1) * M], acc[0:M, t * P:(t + 1) * P], ident[0:M, 0:M])
                        last.then_inc(turned, 1)

                @block.vector
                def _(dve):
                    for k, ts in enumerate(groups):
                        dve.wait_ge(turned, before + k + 1)
                        nc.vector.tensor_copy(rows[:, ts[0]:ts[-1] + 1, 0:M], bank[k][:, 0:len(ts) * M].rearrange("p (t m) -> p t m", m=M))

        var_ok, std_ok = sem("variance_ready"), sem("deviation_ready")
        norms = []

        def layernorm(tag, before, after, replicate=None):
            norms.append(tag)
            nth = len(norms)
            aux_in, aux_ok = (sem(f"{tag}_aux_in"), sem(f"{tag}_aux")) if replicate is not None else (None, None)
            with nc.Block() as block:
                @block.vector
                def _(dve):
                    before(dve, aux_in, aux_ok)
                    dve.drain()
                    nc.vector.tensor_reduce(stat[:, 0, :], xrow[:, :, :], AX.X, ALU.add)
                    dve.drain()
                    nc.vector.tensor_scalar(stat[:, 1, :], stat[:, 0, :], 1.0 / D, None, ALU.mult)
                    dve.drain()
                    nc.vector.tensor_tensor(tmp[:, :, :], xrow[:, :, :], bc(stat[:, 1, :], 2, D), ALU.subtract)
                    dve.drain()
                    nc.vector.tensor_tensor(xrow[:, :, :], tmp[:, :, :], tmp[:, :, :], ALU.mult)
                    dve.drain()
                    nc.vector.tensor_reduce(stat[:, 2, :], xrow[:, :, :], AX.X, ALU.add)
                    dve.drain()
                    nc.vector.tensor_scalar(stat[:, 3, :], stat[:, 2, :], 1.0 / D, EPS, ALU.mult, ALU.add)
                    dve.drain().then_inc(var_ok, 1)
                    dve.wait_ge(std_ok, nth)
                    nc.vector.reciprocal(stat[:, 1, :], stat[:, 0, :])
                    dve.drain()
                    nc.vector.tensor_tensor(xrow[:, :, :], tmp[:, :, :], bc(stat[:, 1, :], 2, D), ALU.mult)
                    dve.drain()
                    after(dve)

                @block.scalar
                def _(act):
                    if replicate is not None:
                        replicate[1](act, aux_in, aux_ok)
                    act.wait_ge(var_ok, nth)
                    nc.scalar.activation(stat[:, 0, :], stat[:, 3, :], ACT.Sqrt).then_inc(std_ok, 1)

                @block.tensor
                def _(pe):
                    if replicate is not None:
                        replicate[0](pe, aux_in, aux_ok)

        ored, worst, worst_t = sem("counts_ored"), sem("worst_ready"), sem("worst_turned")
        half = NT // 2 + 4
        count8 = count[:, :, :].bitcast(fp8)
        bits = bits_u8[:, :].bitcast(i32)
        with nc.Block() as block:
            @block.vector
            def _(dve):
                nc.vector.memset(bits_u8[:, :], 0)
                for h in range(NT):
                    dve.drain()
                    nc.vector.tensor_tensor(bits, bits, count[:, h, 0:NP].bitcast(i32), ALU.bitwise_or).then_inc(ored, 1)
                dve.drain()
                nc.vector.tensor_reduce(small[:, 0:1], bits_u8[:, :], AX.X, ALU.max)
                dve.drain().then_inc(worst, 1)
                for h in range(half, NT):
                    nc.vector.tensor_scalar(count8[:, h, 0:NP], count[:, h, 0:NP], 1.0, None, ALU.mult, ALU.add,
                                            accum_out=out_deg[:, h:h + 1], saturate=False)
                dve.wait_ge(worst_t, 1)
                nc.vector.tensor_reduce(sweeps_f[:, 0:1], bank[0][0:1, 0:P], AX.X, ALU.max)
                dve.drain()
                nc.vector.tensor_scalar(flag_i[:, 0:1], sweeps_f[:, 0:1], 16.0, None, ALU.is_ge)

            @block.tensor
            def _(pe):
                pe.wait_ge(worst, 1)
                nc.tensor.transpose(bank[0][0:1, 0:P], small[:, 0:1], ident[:, :]).then_inc(worst_t, 1)

            @block.scalar
            def _(act):
                for h in range(half):
                    act.wait_ge(ored, h + 1)
                    nc.scalar.activation(count8[:, h, 0:NP], count[:, h, 0:NP], ACT.Copy, accum_out=out_deg[:, h:h + 1], saturate=False)

        def many(eng):
            return eng.value_load(flag_i[0:1, 0:1], min_val=0, max_val=1)

        gl_ok, gl_used, gl_done = sem("g_hots"), sem("g_hots_used"), sem("g_done")
        hi_hot = key_hot[:, :, 0:NT]
        with nc.Block() as block:
            @block.vector
            def _(dve):
                with dve.If(many(dve) > 0):
                    with dve.Fori(0, G) as g:
                        nc.vector.tensor_tensor(lo_hot[:, :, :], bc(tile_lo[:, bass.ds(g, 1), :].rearrange("p g c -> p (g c)"), 2, P),
                                                bc(iota[:, :], 1, C), ALU.is_equal)
                        nc.vector.tensor_tensor(hi_hot, bc(tile_hi[:, bass.ds(g, 1), :].rearrange("p g c -> p (g c)"), 2, NT),
                                                bc(iota[:, 0:NT], 1, C), ALU.is_equal)
                        dve.drain().then_inc(gl_ok, 1)
                        dve.wait_ge(gl_used, g + 1)
                        pass_on(dve)
                    dve.wait_ge(gl_done, 1)
                    nc.vector.tensor_copy(out_deg[:, :], bank[6][:, 0:NT])

            @block.tensor
            def _(pe):
                with pe.If(many(pe) > 0):
                    nc.tensor.matmul(bank[6][:, 0:NT], zeros_b[:, :], zeros_b[:, 0:NT], start=True, stop=False, skip_group_check=True)
                    with pe.Fori(0, G) as g:
                        pe.wait_ge(gl_ok, g + 1)
                        pass_on(pe)
                        for c in range(C):
                            last = nc.tensor.matmul(bank[6][:, 0:NT], lo_hot[:, c, :], hi_hot[:, c, :], start=False, stop=False, skip_group_check=True)
                        last.then_inc(gl_used, 1)
                    nc.tensor.matmul(bank[6][:, 0:NT], zeros_b[:, :], zeros_b[:, 0:NT], start=False, stop=True, skip_group_check=True).then_inc(gl_done, 1)

        counting.close()
        hopping = ExitStack()
        ctx.enter_context(hopping)
        holder[0] = hopping
        parts = sb("parts", [P, NT, 3, D], bf16)
        parts_new = sb("parts_new", [P, NT, 3, D], bf16)

        read_back(D + 1)

        def l0_before(dve, aux_in, aux_ok):
            nc.vector.tensor_tensor(xrow[:, :, :], xrow[:, :, :], rows[:, :, 0:D], ALU.add)
            nc.vector.tensor_copy(in_deg[:, :], rows[:, :, D])
            dve.drain()
            nc.vector.tensor_scalar(dis[:, :], in_deg[:, :], 1.0, None, ALU.max)
            dve.drain().then_inc(aux_in, 1)
            dve.wait_ge(aux_ok, 1)
            nc.vector.reciprocal(dis[:, :], small[:, 0:NT])
            nc.vector.tensor_scalar(stat[:, 0, :], in_deg[:, :], 1.0, None, ALU.min)
            dve.drain()
            nc.vector.tensor_tensor(dis[:, :], dis[:, :], stat[:, 0, :], ALU.mult)

        def l0_after(dve):
            nc.vector.tensor_tensor(qt[:, :, :], xrow[:, :, :], bc(dis[:, :], 2, D), ALU.mult)
            split(dve, parts, qt[:, :, :], tmp[:, :, :], rows[:, :, 0:D])
            nc.vector.tensor_copy(total[:, :, :], xrow[:, :, :])

        def root_degree(act, aux_in, aux_ok):
            act.wait_ge(aux_in, 1)
            nc.scalar.activation(small[:, 0:NT], dis[:, :], ACT.Sqrt).then_inc(aux_ok, 1)

        def split(dve, into, of, rest, rest2):
            dve.drain()
            nc.vector.tensor_copy(into[:, :, 0, :], of)
            dve.drain()
            nc.vector.tensor_tensor(rest, of, into[:, :, 0, :], ALU.subtract)
            dve.drain()
            nc.vector.tensor_copy(into[:, :, 1, :], rest)
            dve.drain()
            nc.vector.tensor_tensor(rest2, rest, into[:, :, 1, :], ALU.subtract)
            dve.drain()
            nc.vector.tensor_copy(into[:, :, 2, :], rest2)
            dve.drain()

        layernorm("l0", l0_before, l0_after, (lambda pe, a, b: None, root_degree))

        HG = [range(t, min(t + 2, NT)) for t in range(0, NT, 2)]
        x_ok, agg_ok, agg_used = sem("hop_rows"), sem("hop_sum"), sem("hop_sum_used")
        with nc.Block() as block:
            @block.tensor
            def _(pe):
                with pe.If(many(pe) < 1):
                    with pe.Fori(0, 3) as k:
                        pe.wait_ge(x_ok, k + 1)
                        pass_on(pe)
                        for q, ts in enumerate(HG):
                            if q >= 4:
                                pe.wait_ge(agg_used, k * len(HG) + q - 3)
                                pass_on(pe)
                            for i, t in enumerate(ts):
                                for h in range(NT):
                                    last = nc.tensor.matmul(bank[q % 4][:, i * 3 * D:(i + 1) * 3 * D], count8[:, h, t * P:(t + 1) * P],
                                                            parts[:, h, :, :].rearrange("p k f -> p (k f)"), start=h == 0, stop=h == NT - 1)
                            last.then_inc(agg_ok, 1)

            @block.vector
            def _(dve):
                with dve.If(many(dve) < 1):
                    dve.sem_inc(x_ok, 1)
                    with dve.Fori(0, 3) as k:
                        for q, ts in enumerate(HG):
                            w = slice(ts[0], ts[-1] + 1)
                            dve.wait_ge(agg_ok, k * len(HG) + q + 1)
                            nc.vector.tensor_reduce(tmp[:, w, :], bank[q % 4][:, 0:len(ts) * 3 * D].rearrange("p (t k f) -> p t f k", k=3, f=D),
                                                    AX.X, ALU.add).then_inc(agg_used, 1)
                            dve.drain()
                            nc.vector.tensor_tensor(rows[:, w, 0:D], tmp[:, w, :], bc(dis[:, w], 2, D), ALU.mult)
                            dve.drain()
                            nc.vector.tensor_tensor(total[:, w, :], total[:, w, :], rows[:, w, 0:D], ALU.add)
                            nc.vector.tensor_tensor(qt[:, w, :], rows[:, w, 0:D], bc(dis[:, w], 2, D), ALU.mult)
                            split(dve, parts_new[:, w, :, :], qt[:, w, :], tmp[:, w, :], rows[:, w, 0:D])
                        nc.vector.tensor_copy(parts[:, :, :, :], parts_new[:, :, :, :])
                        dve.drain().then_inc(x_ok, 1)

        def sweep_pool(pool, table, width, into, idx_in, rows_in, slot_free, cleared, k=0):
            nj = sweeps(pool)
            with pool.Fori(k * nj, (k + 1) * nj) as j:
                with pool.Fori(0, IT) as it:
                    for s in range(NS):
                        pool.wait_ge(idx_in[s], (j * IT + it + 1) * 16)
                        pass_on(pool)
                        for c in range(C):
                            nc.gpsimd.indirect_dma_start(
                                into[:, s, c, 0:width], None, table, bass.IndirectOffsetOnAxis(ap=idx[:, s, c:c + 1], axis=0)
                            ).then_inc(rows_in[s], 16)
                forget_rows(pool, rows_in, slot_free, cleared, (j + 1) * G + NS)

        def sweep_loads(sp, begun, slot_free, idx_in, k=0):
            nj = sweeps(sp)
            with sp.Fori(k * nj, (k + 1) * nj) as j:
                sp.wait_ge(begun, j + 1)
                pass_on(sp)
                with sp.Fori(0, IT - 1) as it:
                    for s in range(NS):
                        sp.wait_ge(slot_free, j * G + it * NS + s + 1)
                        load_idx(sp, it * NS + s, s, False, idx_in[s])
                for s in range(NS):
                    g = G - NS + s
                    sp.wait_ge(slot_free, j * G + g + 1)
                    load_idx(sp, g, s, g == G - 1, idx_in[s])

        begun, slot_free, hot_ok, sum_ok = sem("h_begun"), sem("h_free"), sem("h_hot"), sem("h_sum")
        idx_in, rows_in = [sem(f"h_idx{s}") for s in range(NS)], [sem(f"h_rows{s}") for s in range(NS)]
        turned, stored, cleared = sem("h_turned"), sem("h_stored"), sem("h_cleared")

        def hop(k):
            with nc.Block() as block:
                @block.sync
                def _(sp):
                    with sp.If(many(sp) > 0):
                        sp.dma_start(hop_tab[k].rearrange(by_tile, p=P), qt[:, :, :]).then_inc(stored, 16)
                        sp.wait_ge(stored, 16 * (k + 1))
                        sweep_loads(sp, begun, slot_free, idx_in, k)

                @block.gpsimd
                def _(pool):
                    with pool.If(many(pool) > 0):
                        pool.wait_ge(stored, 16 * (k + 1))
                        sweep_pool(pool, hop_tab[k], D, g_edge, idx_in, rows_in, slot_free, cleared, k)

                @block.vector
                def _(dve):
                    with dve.If(many(dve) > 0):
                        nj = sweeps(dve)
                        reset_windows(dve)
                        if k == 0:
                            dve.sem_inc(slot_free, NS)
                            dve.sem_inc(cleared, 1)
                        with dve.Fori(k * nj, (k + 1) * nj) as j:
                            dve.wait_ge(cleared, j + 1)
                            pass_on(dve)
                            start_sweep(dve, begun)
                            with dve.Fori(0, IT) as it:
                                for s in range(NS):
                                    g = it * NS + s
                                    n = j * G + g + 1
                                    nc.vector.tensor_tensor(hot[:, :, :], bc(dst_rel[:, bass.ds(g, 1), :].rearrange("p g c -> p (g c)"), 2, W),
                                                            bc(iota[:, 0:W], 1, C), ALU.is_equal).then_inc(hot_ok, 1)
                                    b = spans(dve, g)
                                    dve.wait_ge(sum_ok, n)
                                    nc.vector.tensor_tensor(acc[0:D, bass.ds(b, W)], acc[0:D, bass.ds(b, W)], bank[5][0:D, 0:W], ALU.add).then_inc(slot_free, 1)
                                    dve.drain()
                        for q in range(-(-NT // RT)):
                            ts = range(q * RT, min((q + 1) * RT, NT))
                            dve.wait_ge(turned, k * 4 + q + 1)
                            nc.vector.tensor_tensor(tmp[:, ts[0]:ts[-1] + 1, :], bank[q][:, 0:len(ts) * D].rearrange("p (t m) -> p t m", m=D),
                                                    bc(dis[:, ts[0]:ts[-1] + 1], 2, D), ALU.mult)
                        dve.drain()
                        nc.vector.tensor_tensor(total[:, :, :], total[:, :, :], tmp[:, :, :], ALU.add)
                        nc.vector.tensor_tensor(qt[:, :, :], tmp[:, :, :], bc(dis[:, :], 2, D), ALU.mult)

                @block.tensor
                def _(pe):
                    with pe.If(many(pe) > 0):
                        nj = sweeps(pe)
                        with pe.Fori(k * nj, (k + 1) * nj) as j:
                            with pe.Fori(0, IT) as it:
                                for s in range(NS):
                                    pe.wait_ge(hot_ok, j * G + it * NS + s + 1)
                                    pe.wait_ge(rows_in[s], (it + 1) * (16 * C))
                                    for c in range(C):
                                        last = nc.tensor.matmul(bank[5][0:D, 0:W], g_edge[:, s, c, 0:D], hot[:, c, :], start=c == 0, stop=c == C - 1)
                                    last.then_inc(sum_ok, 1)
                        pe.wait_ge(slot_free, (k + 1) * nj * G + NS)
                        pass_on(pe)
                        for q in range(-(-NT // RT)):
                            for i, t in enumerate(range(q * RT, min((q + 1) * RT, NT))):
                                last = nc.tensor.transpose(bank[q][:, i * D:(i + 1) * D], acc[0:D, t * P:(t + 1) * P], ident[0:D, 0:D])
                            last.then_inc(turned, 1)

        for k in range(3):
            hop(k)

        def l1_before(dve, aux_in, aux_ok):
            nc.vector.tensor_scalar(total[:, :, :], total[:, :, :], 0.25, None, ALU.mult)
            dve.drain()
            nc.vector.tensor_tensor(xrow[:, :, :], xrow[:, :, :], total[:, :, :], ALU.add)

        def l1_after(dve):
            nc.vector.tensor_copy(tab[:, :, 0:D], xrow[:, :, :])
            nc.vector.memset(tab[:, :, D + 1:D + 2], 1.0)
            nc.vector.tensor_copy(attrep[:, :], attc[:, 1:2].to_broadcast([D, P]))

        hopping.close()
        early.close()
        holder[0] = ctx
        tab = sb("tab", [P, NT, 2 * D])
        ad_row = sb("ad_row", [P, NP + W])
        ad_col = sb("ad_col", [P, NT])
        u_edge = sb("u_edge", [P, 2, C])
        top, ea2, edge_c, edge_t, added, leaky, logit, arg, prob, far = carve(
            (NP + W,), (G, C, 2), (G, C), (G, C), (2, C, W), (C, W), (2, C, W), (C, W), (C, W), (C, W),
            shared=count[:, :, :].rearrange("p h n -> p (h n)").bitcast(fp32))
        pmax = sb("pmax", [P, 2, W])
        nmax = sb("nmax", [W, 1])
        ndiag = sb("ndiag", [W, W])
        newtop = sb("newtop", [P, W])
        drop = sb("drop", [P, W])
        decay = sb("decay", [P, W])
        w_e_rep = sb("w_e_rep", [2, P])
        m_row = sb("m_row", [1, 8, D])
        wmv = sb("wmv", [1, 4, D])
        wedge_rep = sb("wedge_rep", [2, 2, P])
        edge_w = sb("edge_w", [P, 2])
        e2n_rep = sb("e2n_rep", [P, 2, D])
        konst = sb("konst", [1, 1])
        mean_z = sb("mean_z", [P, D])
        e2nT = sb("e2nT", [2, D])


        layernorm("l1", l1_before, l1_after)

        def attention(tag, table, M, edge_features, way=lambda eng: nullcontext(), prepare=(lambda eng: None,) * 3):
            begun, slot_free, cleared = sem(f"{tag}_begun"), sem(f"{tag}_free"), sem(f"{tag}_cleared")
            idx_in, rows_in = [sem(f"{tag}_idx{s}") for s in range(RS)], [sem(f"{tag}_rows{s}") for s in range(RS)]
            u_ok, added_ok, pm_ok, pm_t, nd_ok, top_rep, drop_ok, decay_ok, arg_ok, prob_ok, sum_ok = (
                sem(f"{tag}_{n}") for n in ("u", "added", "pmax", "pmaxT", "diag", "toprep", "drop", "decay", "arg", "prob", "sum"))
            with nc.Block() as block:
                @block.sync
                def _(sp):
                    with way(sp):
                        nj = sweeps(sp)
                        with sp.Fori(0, nj) as j:
                            sp.wait_ge(slot_free, j * G + RS)
                            pass_on(sp)

                            def load(g, s, m):
                                sp.wait_ge(slot_free, j * G + g + 1)
                                pass_on(sp)
                                load_idx(sp, g, s, isinstance(g, int) and g == G - 1, idx_in[s])

                            each(sp, load)

                @block.gpsimd
                def _(pool):
                    with way(pool):
                        nj = sweeps(pool)
                        with pool.Fori(0, nj) as j:
                            def gather(g, s, m):
                                pool.wait_ge(idx_in[s], (j * uses(s) + m) * 16)
                                pass_on(pool)
                                for c in range(C):
                                    nc.gpsimd.indirect_dma_start(
                                        g_edge[:, s, c, 0:D + 2], None, table, bass.IndirectOffsetOnAxis(ap=idx[:, s, c:c + 1], axis=0)
                                    ).then_inc(rows_in[s], 16)

                            each(pool, gather)
                            forget_rows(pool, rows_in, slot_free, cleared, (j + 1) * G + RS)

                @block.vector
                def _(dve):
                    with way(dve):
                        nj = sweeps(dve)
                        dve.sem_inc(slot_free, RS)
                        dve.sem_inc(cleared, 1)
                        prepare[0](dve)
                        reset_windows(dve)
                        nc.vector.memset(top[:, :], LOW)
                        if not edge_features:
                            nc.vector.memset(edge_c[:, :, :], 0.0)
                        with dve.Fori(0, nj) as j:
                            dve.wait_ge(cleared, j + 1)
                            pass_on(dve)
                            start_sweep(dve, begun)
                            at = {}

                            def source_terms(g, s, m):
                                ge, p = g_edge[:, s, :, :], s % 2
                                if edge_features:
                                    nc.vector.tensor_copy(ge[:, :, D + 2:D + 4], ea2[:, bass.ds(g, 1), :, :].rearrange("p g c k -> p (g c) k"))
                                dve.wait_ge(rows_in[s], m * (16 * C))
                                nc.vector.tensor_tensor(u_edge[:, p, :], ge[:, :, D], edge_c[:, bass.ds(g, 1), :].rearrange("p g c -> p (g c)"), ALU.add).then_inc(u_ok, 1)

                            def outside(g):
                                nc.vector.tensor_tensor(far[:, :, :], bc(dst_rel[:, bass.ds(g, 1), :].rearrange("p g c -> p (g c)"), 2, W),
                                                        bc(iota[:, 0:W], 1, C), ALU.not_equal)

                            def logits(g, s, m):
                                n = j * G + g + 1
                                p = s % 2
                                dve.wait_ge(added_ok, n)
                                nc.vector.scalar_tensor_tensor(leaky[:, :, :], added[:, p, :, :], 0.01, added[:, p, :, :], ALU.mult, ALU.max)
                                dve.drain()
                                nc.vector.scalar_tensor_tensor(logit[:, p, :, :], far[:, :, :], FAR, leaky[:, :, :], ALU.mult, ALU.add)
                                dve.drain()
                                nc.vector.tensor_reduce(pmax[:, p, :], logit[:, p, :, :].rearrange("p c n -> p n c"), AX.X, ALU.max).then_inc(pm_ok, 1)

                            def maxima(g, s, m):
                                n = j * G + g + 1
                                p = s % 2
                                dve.wait_ge(pm_t, n)
                                nc.vector.tensor_reduce(nmax[:, :], bank[p][0:W, 0:P], AX.X, ALU.max)
                                dve.drain()
                                nc.vector.tensor_scalar(ndiag[:, :], ident[0:W, 0:W], nmax[:, 0:1], None, ALU.mult).then_inc(nd_ok, 1)

                            def exponents(g, s, m, b):
                                n = j * G + g + 1
                                p = s % 2
                                dve.wait_ge(top_rep, n)
                                nc.vector.tensor_tensor(newtop[:, :], top[:, bass.ds(b, W)], bank[2][:, 0:W], ALU.max)
                                dve.drain()
                                nc.vector.tensor_tensor(arg[:, :, :], logit[:, p, :, :], bc(newtop[:, :], 1, C), ALU.subtract).then_inc(arg_ok, 1)
                                nc.vector.tensor_tensor(drop[:, :], top[:, bass.ds(b, W)], newtop[:, :], ALU.subtract).then_inc(drop_ok, 1)
                                dve.drain()
                                nc.vector.tensor_copy(top[:, bass.ds(b, W)], newtop[:, :])

                            def add_sums(g, s, m, b):
                                n = j * G + g + 1
                                dve.wait_ge(decay_ok, n)
                                nc.vector.tensor_tensor(acc[0:M, bass.ds(b, W)], acc[0:M, bass.ds(b, W)], decay[0:M, :], ALU.mult)
                                dve.drain()
                                dve.wait_ge(sum_ok, n)
                                nc.vector.tensor_tensor(acc[0:M, bass.ds(b, W)], acc[0:M, bass.ds(b, W)], bank[3][0:M, 0:W], ALU.add).then_inc(slot_free, 1)
                                dve.drain()

                            def front(g, s, m):
                                source_terms(g, s, m)
                                outside(g)
                                logits(g, s, m)

                            def step(g, s, m, after):
                                b = spans(dve, g)
                                if after:
                                    source_terms(*after)
                                maxima(g, s, m)
                                if after:
                                    outside(after[0])
                                exponents(g, s, m, b)
                                if after:
                                    logits(*after)
                                add_sums(g, s, m, b)

                            pipelined(dve, front, step)

                @block.scalar
                def _(act):
                    with way(act):
                        prepare[1](act)
                        nj = sweeps(act)
                        with act.Fori(0, nj) as j:
                            act.wait_ge(begun, j + 1)
                            pass_on(act)

                            def add(g, s, m):
                                n = j * G + g + 1
                                p = s % 2
                                b = spans(act, g)
                                act.wait_ge(u_ok, n)
                                for c in range(C):
                                    last = nc.scalar.activation(added[:, p, c, :], ad_row[:, bass.ds(b, W)], ACT.Identity, bias=u_edge[:, p, c:c + 1])
                                last.then_inc(added_ok, 1)

                            def step(g, s, m, after):
                                if after:
                                    add(*after)
                                n = j * G + g + 1
                                act.wait_ge(arg_ok, n)
                                nc.scalar.activation(prob[:, :, :], arg[:, :, :], ACT.Exp).then_inc(prob_ok, 1)
                                act.wait_ge(drop_ok, n)
                                nc.scalar.activation(decay[:, :], drop[:, :], ACT.Exp).then_inc(decay_ok, 1)

                            pipelined(act, add, step)

                @block.tensor
                def _(pe):
                    with way(pe):
                        prepare[2](pe)
                        nj = sweeps(pe)
                        with pe.Fori(0, nj) as j:
                            def turn(g, s, m):
                                pe.wait_ge(pm_ok, j * G + g + 1)
                                pass_on(pe)
                                nc.tensor.transpose(bank[s % 2][0:W, 0:P], pmax[:, s % 2, :], ident[:, :]).then_inc(pm_t, 1)

                            def step(g, s, m, after):
                                n = j * G + g + 1
                                pe.wait_ge(nd_ok, n)
                                nc.tensor.matmul(bank[2][:, 0:W], ones[0:W, :], ndiag[:, :], start=True, stop=True).then_inc(top_rep, 1)
                                pe.wait_ge(prob_ok, n)
                                for c in range(C):
                                    last = nc.tensor.matmul(bank[3][0:M, 0:W], g_edge[:, s, c, 0:M], prob[:, c, :], start=c == 0, stop=c == C - 1)
                                last.then_inc(sum_ok, 1)
                                if after:
                                    turn(*after)

                            pipelined(pe, turn, step)

        def take_l2(a, b, ps):
            nc.vector.tensor_copy(tab[:, a:b, D:D + 1], ps[:, :, 0:1])
            return nc.vector.tensor_copy(ad_col[:, a:b], ps[:, :, 1])

        project("l2", 2, D, attc[:, 0:2], take_l2, attrep[:, :])
        dense = sb("dense", [P, 8, NT])
        limits = sb("limits", [P, 4])
        ex1, ex2 = carve((NK, KW), (NK, KW))
        diag, = carve((2, MT, P))
        src_max, u_low, u_level, near, node_top, near_row, slow_row, u_slow = (dense[:, i, :] for i in range(8))
        near_rep, slow_rep = ad_row, acc
        u = tab[:, :, D]
        lim_in, lim_t, lim_ok, lim_rep, max_ok, max_t, dg_ok, dg_rep, dg_out = (
            sem(f"d_{n}") for n in ("limits", "limitsT", "limits_row", "limits_rep", "max", "maxT", "diag", "diag_rep", "diag_out"))
        quads = [range(t, min(t + MT, NT)) for t in range(0, NT, MT)]
        with nc.Block() as block:
            @block.vector
            def _(dve):
                with dve.If(many(dve) < 1):
                    nc.vector.memset(acc[:, 0:NP], 0.0)
                    nc.vector.tensor_scalar(u_low, u, -1.0, None, ALU.mult)
                    nc.vector.tensor_scalar(u_slow, u, 0.01, None, ALU.mult)
                    nc.vector.tensor_reduce(limits[:, 0:1], u, AX.X, ALU.max)
                    dve.drain()
                    nc.vector.tensor_reduce(limits[:, 1:2], u_low, AX.X, ALU.max)
                    dve.drain().then_inc(lim_in, 1)
                    dve.wait_ge(lim_t, 1)
                    nc.vector.tensor_reduce(small[0:1, 0:2], bank[0][0:1, 0:2 * P].rearrange("p (k n) -> p k n", k=2), AX.X, ALU.max)
                    dve.drain()
                    nc.vector.tensor_tensor(small[0:1, 2:3], small[0:1, 0:1], small[0:1, 1:2], ALU.add)
                    dve.drain()
                    nc.vector.tensor_scalar(small[0:1, 3:4], small[0:1, 2:3], 1e-20, 2.0, ALU.max, ALU.mult)
                    dve.drain()
                    nc.vector.reciprocal(small[0:1, 2:3], small[0:1, 3:4])
                    dve.drain().then_inc(lim_ok, 1)
                    dve.wait_ge(lim_rep, 1)
                    nc.vector.tensor_copy(limits[:, 0:3], bank[1][:, 1:4])
                    dve.drain()
                    nc.vector.tensor_scalar(u_level, u, limits[:, 0:1], limits[:, 1:2], ALU.add, ALU.mult)
                    dve.drain()
                    nc.vector.tensor_scalar(u_level, u_level, 0.25, None, ALU.add)
                    for h in range(NT):
                        dve.drain()
                        nc.vector.scalar_tensor_tensor(acc[:, 0:NP], count8[:, h, 0:NP], u_level[:, h:h + 1], acc[:, 0:NP], ALU.min, ALU.max)
                    dve.drain().then_inc(max_ok, 1)
                    for k, ts in enumerate(quads):
                        dve.wait_ge(max_t, k + 1)
                        nc.vector.tensor_reduce(src_max[:, ts[0]:ts[-1] + 1], bank[k][:, 0:len(ts) * P].rearrange("p (t n) -> p t n", n=P), AX.X, ALU.max)
                    dve.drain()
                    nc.vector.tensor_scalar(src_max, src_max, -0.25, limits[:, 2:3], ALU.add, ALU.mult)
                    dve.drain()
                    nc.vector.tensor_scalar(src_max, src_max, limits[:, 0:1], None, ALU.subtract)
                    dve.drain()
                    nc.vector.tensor_tensor(near, src_max, ad_col[:, :], ALU.add)
                    dve.drain()
                    nc.vector.scalar_tensor_tensor(node_top, near, 0.01, near, ALU.mult, ALU.max)
                    dve.drain()
                    nc.vector.tensor_tensor(near_row, ad_col[:, :], node_top, ALU.subtract)
                    nc.vector.scalar_tensor_tensor(slow_row, ad_col[:, :], 0.01, node_top, ALU.mult, ALU.subtract)
                    dve.drain()
                    for i, (col, ts) in enumerate((col, ts) for col in (near_row, slow_row) for ts in quads):
                        if i >= 2:
                            dve.wait_ge(dg_rep, i - 1)
                        nc.vector.tensor_tensor(diag[:, i % 2, 0:len(ts), :], bc(ident[:, :], 1, len(ts)), bc(col[:, ts[0]:ts[-1] + 1], 2, P),
                                                ALU.mult).then_inc(dg_ok, 1)

            @block.tensor
            def _(pe):
                with pe.If(many(pe) < 1):
                    pe.wait_ge(lim_in, 1)
                    for i in range(2):
                        last = nc.tensor.transpose(bank[0][0:1, i * P:(i + 1) * P], limits[:, i:i + 1], ident[:, :])
                    last.then_inc(lim_t, 1)
                    pe.wait_ge(lim_ok, 1)
                    nc.tensor.matmul(bank[1][:, 1:4], ones[0:1, :], small[0:1, 1:4], start=True, stop=True).then_inc(lim_rep, 1)
                    pe.wait_ge(max_ok, 1)
                    for k, ts in enumerate(quads):
                        for i, t in enumerate(ts):
                            last = nc.tensor.transpose(bank[k][:, i * P:(i + 1) * P], acc[:, t * P:(t + 1) * P], ident[:, :])
                        last.then_inc(max_t, 1)
                    for i, ts in enumerate(quads + quads):
                        pe.wait_ge(dg_ok, i + 1)
                        if i >= 2:
                            pe.wait_ge(dg_out, i - 1)
                        nc.tensor.matmul(bank[i % 2][:, 0:len(ts) * P], ones[:, :],
                                         diag[:, i % 2, 0:len(ts), :].rearrange("p t n -> p (t n)"), start=True, stop=True).then_inc(dg_rep, 1)

            @block.scalar
            def _(act):
                with act.If(many(act) < 1):
                    for i, (row, ts) in enumerate((row, ts) for row in (near_rep, slow_rep) for ts in quads):
                        act.wait_ge(dg_rep, i + 1)
                        nc.scalar.activation(row[:, ts[0] * P:(ts[-1] + 1) * P], bank[i % 2][:, 0:len(ts) * P], ACT.Copy).then_inc(dg_out, 1)

        chunks = [(h, k) for h in range(NT) for k in range(NK)]
        NB = -(-NP // 512)
        exp_ok, weight_ok, chunk_free, dense_ok = (sem(f"d_{n}") for n in ("exp", "weight", "chunk_free", "sums"))
        with nc.Block() as block:
            @block.scalar
            def _(act):
                with act.If(many(act) < 1):
                    for h in range(NT):
                        for k in range(NK):
                            cols = slice(k * KW, (k + 1) * KW)
                            act.wait_ge(chunk_free, h * NK + k + 1)
                            nc.scalar.activation(ex1[:, k, :], near_rep[:, cols], ACT.Exp, bias=tab[:, h, D:D + 1])
                            nc.scalar.activation(ex2[:, k, :], slow_rep[:, cols], ACT.Exp, bias=u_slow[:, h:h + 1]).then_inc(exp_ok, 1)
                    act.wait_ge(dense_ok, 1)
                    for q in range(1, NB, 2):
                        a, b = q * 512, min((q + 1) * 512, NP)
                        nc.scalar.activation(acc[0:D + 2, a:b], bank[q][0:D + 2, 0:b - a], ACT.Copy)

            @block.vector
            def _(dve):
                with dve.If(many(dve) < 1):
                    dve.sem_inc(chunk_free, NK)
                    for two in (chunks[i:i + 2] for i in range(0, len(chunks), 2)):
                        for h, k in two:
                            dve.wait_ge(exp_ok, h * NK + k + 1)
                            nc.vector.tensor_tensor(ex1[:, k, :], ex1[:, k, :], ex2[:, k, :], ALU.max)
                        dve.drain()
                        for h, k in two:
                            nc.vector.scalar_tensor_tensor(ex1[:, k, :], ex1[:, k, :], 2.0, count8[:, h, k * KW:(k + 1) * KW],
                                                           ALU.min, ALU.mult).then_inc(weight_ok, 1)
                    dve.wait_ge(dense_ok, 1)
                    for q in range(0, NB, 2):
                        a, b = q * 512, min((q + 1) * 512, NP)
                        nc.vector.tensor_copy(acc[0:D + 2, a:b], bank[q][0:D + 2, 0:b - a])

            @block.tensor
            def _(pe):
                with pe.If(many(pe) < 1):
                    for h, k in chunks:
                        pe.wait_ge(weight_ok, h * NK + k + 1)
                        a = k * KW
                        while a < (k + 1) * KW:
                            b = min((k + 1) * KW, (a // 512 + 1) * 512)
                            last = nc.tensor.matmul(bank[a // 512][0:D + 2, a % 512:a % 512 + b - a], tab[:, h, 0:D + 2],
                                                    ex1[:, k, a - k * KW:b - k * KW], start=h == 0 and a % 512 == 0,
                                                    stop=h == NT - 1 and b in (NP, (a // 512 + 1) * 512), skip_group_check=True)
                            a = b
                        last.then_inc(chunk_free, 1)
                    pe.drain().then_inc(dense_ok, 1)

        general = lambda eng: eng.If(many(eng) > 0)
        store_table("l2", [(att_tab[0].rearrange(by_tile, p=P), tab[:, :, 0:D + 2])], general)
        attention("l2", att_tab[0], D + 2, False, general)
        read_back(D + 2)

        def normalise(dve, width):
            nc.vector.tensor_scalar(stat[:, 0, :], rows[:, :, D + 1], 1e-30, None, ALU.max)
            dve.drain()
            nc.vector.reciprocal(stat[:, 1, :], stat[:, 0, :])
            dve.drain()
            nc.vector.tensor_tensor(tmp[:, :, :], rows[:, :, 0:D], bc(stat[:, 1, :], 2, D), ALU.mult)
            dve.drain()

        def l2_before(dve, aux_in, aux_ok):
            normalise(dve, D)
            nc.vector.tensor_scalar(total[:, :, :], tmp[:, :, :], 0.0, None, ALU.min)
            dve.drain().then_inc(aux_in, 1)
            dve.wait_ge(aux_ok, 1)
            nc.vector.tensor_scalar(qt[:, :, :], total[:, :, :], -1.0, None, ALU.add)
            dve.drain()
            nc.vector.scalar_tensor_tensor(total[:, :, :], tmp[:, :, :], 0.0, qt[:, :, :], ALU.max, ALU.add)
            dve.drain()
            nc.vector.tensor_tensor(xrow[:, :, :], xrow[:, :, :], total[:, :, :], ALU.add)

        def l2_exp(act, aux_in, aux_ok):
            act.wait_ge(aux_in, 1)
            nc.scalar.activation(total[:, :, :], total[:, :, :], ACT.Exp).then_inc(aux_ok, 1)

        
        def l2_after(dve):
            nc.vector.memset(tab[:, :, D + 1:D + 2], 1.0)
            nc.vector.memset(ea2[:, G - 1, :, :], 0.0)

        layernorm("l2", l2_before, l2_after, (lambda pe, a, b: None, l2_exp))

        ea2_in = sem("edge_attr_2_loaded")
        f_a, f_b, f_c, f_d = sem("fold_in"), sem("fold_out"), sem("fold_reps"), sem("fold_e2n")
        with nc.Block() as block:
            @block.sync
            def _(sp):
                full = (G - 1) * ST
                sp.dma_start(ea2[:, 0:G - 1, :, :], edge_attr_2[0:full, :].rearrange("(g p c) k -> p g c k", p=P, c=C)).then_inc(ea2_in, 16)
                sp.dma_start(ea2[0:PL, G - 1, :, :], edge_attr_2[full:E, :].rearrange("(p c) k -> p c k", c=C)).then_inc(ea2_in, 16)
                sp.wait_ge(ea2_in, 32)

            @block.vector
            def _(dve):
                nc.vector.tensor_copy(attrep[:, :], blk[:, 3:4].to_broadcast([D, P]))
                nc.vector.tensor_copy(w_e_rep[:, :], w_e[:, 0:1].to_broadcast([2, P]))
                nc.vector.tensor_copy(wedge_rep[:, 0, :], wedge[:, 0:1].to_broadcast([2, P]))
                nc.vector.tensor_copy(wedge_rep[:, 1, :], wedge[:, 1:2].to_broadcast([2, P]))
                dve.drain().then_inc(f_a, 1)
                dve.wait_ge(f_b, 1)
                nc.vector.tensor_copy(wfcT[:, D:D + 1], bank[0][0:D, 0:1])
                nc.vector.tensor_copy(attrep[:, :], bank[1][0:D, 0:P])
                nc.vector.tensor_copy(wmv[:, :, :], bank[2][0:1, 0:4 * D].rearrange("p (k f) -> p k f", k=4))
                nc.vector.tensor_copy(e2nT[:, :], bank[3][0:2, 0:D])
                nc.vector.tensor_copy(edge_w[:, :], bank[4][:, 0:2])
                dve.drain().then_inc(f_c, 1)
                dve.wait_ge(f_d, 1)
                nc.vector.tensor_copy(e2n_rep[:, :, :], bank[5][:, 0:2 * D].rearrange("p (k f) -> p k f", k=2))

            @block.tensor
            def _(pe):
                pe.wait_ge(f_a, 1)
                nc.tensor.matmul(bank[0][0:D, 0:1], wrow[:, 3, :], blk[:, 0:1], start=True, stop=True)
                nc.tensor.matmul(bank[1][0:D, 0:P], wrow[:, 3, :], attrep[:, :], start=True, stop=True)
                for i, (b, w) in enumerate(((1, 0), (2, 1), (4, 0), (5, 1))):
                    nc.tensor.matmul(bank[2][0:1, i * D:(i + 1) * D], blk[:, b:b + 1], wm[:, w, :], start=True, stop=True)
                nc.tensor.transpose(bank[3][0:2, 0:D], we2n[:, :], ident[0:D, 0:D])
                nc.tensor.matmul(bank[4][:, 0:2], w_e_rep[:, :], wedge[:, :], start=True, stop=True).then_inc(f_b, 1)
                pe.wait_ge(f_c, 1)
                nc.tensor.matmul(bank[5][:, 0:D], wedge_rep[:, 0, :], e2nT[:, :], start=True, stop=True)
                nc.tensor.matmul(bank[5][:, D:2 * D], wedge_rep[:, 1, :], e2nT[:, :], start=True, stop=True).then_inc(f_d, 1)

        project("l3", D + 1, D, wfcT[:, :], lambda a, b, ps: nc.vector.tensor_copy(tab[:, a:b, 0:D + 1], ps), attrep[:, :])
        store_table("l3", [(att_tab[1].rearrange(by_tile, p=P), tab[:, :, 0:D + 2])])

        mu_ok, zc_ok, mom_ok, root_in, root_ok, const_in, const_ok, zdone = (
            sem(f"m_{n}") for n in ("mean", "centred", "moment", "root_in", "root", "const_in", "const", "zdone"))
        def moments_pe(pe):
            for i, deg in enumerate((out_deg, in_deg)):
                for t in range(NT):
                    last = nc.tensor.matmul(bank[i][:, 0:D], deg[:, t:t + 1].to_broadcast([P, P]), tab[:, t, 0:D], start=t == 0, stop=t == NT - 1)
            last.then_inc(mu_ok, 1)
            for i, deg in enumerate((out_deg, in_deg)):
                pe.wait_ge(zc_ok, i + 1)
                for t in range(NT):
                    nc.tensor.matmul(bank[2 + 2 * i][0:1, 0:D], deg[:, t:t + 1], total[:, t, :], start=t == 0, stop=t == NT - 1)
                    last = nc.tensor.matmul(bank[3 + 2 * i][0:1, 0:D], deg[:, t:t + 1], qt[:, t, :], start=t == 0, stop=t == NT - 1)
                last.then_inc(mom_ok, 1)
            pe.wait_ge(const_in, 1)
            nc.tensor.matmul(bank[6][:, 0:1], ones[0:1, :], konst[:, :], start=True, stop=True).then_inc(const_ok, 1)

        def moments_dve(dve):
            dve.wait_ge(mu_ok, 1)
            for i in range(2):
                nc.vector.tensor_scalar(mean_z[:, :], bank[i][:, 0:D], 1.0 / E, None, ALU.mult)
                dve.drain()
                nc.vector.tensor_tensor(tmp[:, :, :], tab[:, :, 0:D], bc(mean_z[:, :], 1, NT), ALU.subtract)
                dve.drain()
                if i:
                    dve.wait_ge(mom_ok, 1)
                nc.vector.tensor_tensor(total[:, :, :], tmp[:, :, :], tmp[:, :, :], ALU.mult)
                dve.drain()
                nc.vector.tensor_tensor(qt[:, :, :], total[:, :, :], tmp[:, :, :], ALU.mult).then_inc(zc_ok, 1)
            dve.wait_ge(mom_ok, 2)
            for i in range(2):
                nc.vector.tensor_scalar(m_row[:, 2 * i, :], bank[2 + 2 * i][0:1, 0:D], 1.0 / E, None, ALU.mult)
                nc.vector.tensor_scalar(m_row[:, 2 * i + 1, :], bank[3 + 2 * i][0:1, 0:D], 1.0 / E, None, ALU.mult)
            dve.drain()
            cubes = m_row[:, 0:4, :].rearrange("a (i k) f -> a i k f", k=2)[:, :, 1, :]
            signs = m_row[:, 4:8, :].rearrange("a (i k) f -> a i k f", k=2)[:, :, 1, :]
            sizes = m_row[:, 4:8, :].rearrange("a (i k) f -> a i k f", k=2)[:, :, 0, :]
            nc.vector.scalar_tensor_tensor(sizes, cubes, -1.0, cubes, ALU.mult, ALU.max)
            nc.vector.tensor_scalar(signs, cubes, 0.0, None, ALU.is_gt)
            dve.drain()
            nc.vector.tensor_scalar(cubes, cubes, 0.0, None, ALU.is_lt)
            dve.drain()
            nc.vector.tensor_tensor(signs, signs, cubes, ALU.subtract)
            nc.vector.tensor_scalar(sizes, sizes, 1e-19, None, ALU.max)
            dve.drain().then_inc(root_in, 1)
            dve.wait_ge(root_ok, 1)
            nc.vector.tensor_tensor(cubes, sizes, signs, ALU.mult)
            dve.drain()
            nc.vector.tensor_tensor(m_row[:, 4:8, :], m_row[:, 0:4, :], wmv[:, :, :], ALU.mult)
            dve.drain()
            nc.vector.tensor_reduce(konst[:, :], m_row[:, 4:8, :].rearrange("a k f -> a (k f)"), AX.X, ALU.add)
            dve.drain().then_inc(const_in, 1)
            dve.wait_ge(const_ok, 1)
            nc.vector.tensor_scalar(edge_t[:, :, :], ea2[:, :, :, 0], edge_w[:, 0:1], bank[6][:, 0:1], ALU.mult, ALU.add)
            dve.drain()
            nc.vector.scalar_tensor_tensor(edge_c[:, :, :], ea2[:, :, :, 1], edge_w[:, 1:2], edge_t[:, :, :], ALU.mult, ALU.add)

        def moments_act(act):
            act.wait_ge(root_in, 1)
            squares = m_row[:, 0:4, :].rearrange("a (i k) f -> a i k f", k=2)[:, :, 0, :]
            sizes = m_row[:, 4:8, :].rearrange("a (i k) f -> a i k f", k=2)[:, :, 0, :]
            nc.scalar.activation(squares, squares, ACT.Sqrt)
            nc.scalar.activation(sizes, sizes, ACT.Ln)
            act.drain()
            nc.scalar.activation(sizes, sizes, ACT.Exp, scale=1.0 / 3.0)
            act.drain().then_inc(root_ok, 1)

        attention("l3", att_tab[1], D + 4, True, prepare=(moments_dve, moments_act, moments_pe))
        read_back(D + 4)

        def l3_before(dve, aux_in, aux_ok):
            for k in range(2):
                nc.vector.tensor_tensor(total[:, :, :], bc(rows[:, :, D + 2 + k], 2, D), bc(e2n_rep[:, k, :], 1, NT), ALU.mult)
                dve.drain()
                nc.vector.tensor_tensor(rows[:, :, 0:D], rows[:, :, 0:D], total[:, :, :], ALU.add)
                dve.drain()
            normalise(dve, D)
            nc.vector.tensor_tensor(xrow[:, :, :], xrow[:, :, :], tmp[:, :, :], ALU.add)

        layernorm("l3", l3_before, lambda dve: None)
        stored = sem("out_stored")
        with nc.Block() as block:
            @block.sync
            def _(sp):
                sp.dma_start(out[0:(NT - 1) * P, :].rearrange(by_tile, p=P), xrow[:, 0:NT - 1, :]).then_inc(stored, 16)
                sp.dma_start(out[(NT - 1) * P:N, :], xrow[0:NL, NT - 1, :]).then_inc(stored, 16)
                sp.wait_ge(stored, 32)


_INS = ["x", "src", "dst", "edge_attr_2", "edge_attr_64", "L0_gnn_Wq", "L0_gnn_bq", "L0_gnn_Wk", "L0_gnn_bk",
        "L0_gnn_We", "L0_gnn_be", "L0_gnn_Wv", "L0_gnn_bv", "L2_gnn_attn_w", "L3_gnn_W_fc", "L3_gnn_W_attn",
        "L3_gnn_W_edge", "L3_gnn_W_e2n", "L3_gnn_W_m1", "L3_gnn_W_m2"]


def kernel(**inputs):
    import concourse.bacc as bacc
    from concourse.bass_utils import run_bass_kernel_spmd

    nc = bacc.Bacc("TRN2", target_bir_lowering=False, num_devices=1)
    arrays, args = {}, []
    for name in _INS:
        a = np.ascontiguousarray(inputs[name])
        arrays[f"in_{name}"] = a
        args.append(nc.dram_tensor(f"in_{name}", a.shape, mybir.dt.from_np(a.dtype), kind="ExternalInput").ap())
    out = nc.dram_tensor("out_0", (N, D), fp32, kind="ExternalOutput").ap()
    build(nc, *args, out)
    return run_bass_kernel_spmd(nc, [arrays], core_ids=[0]).results[0]["out_0"]
```
